# Optimizing a Trainium2 kernel written in Bass

```python
import numpy as np
import jax
import jax.numpy as jnp

def _softmax(x, axis=-1):
    return jax.nn.softmax(x, axis=axis)

def _gelu(x):
    return jax.nn.gelu(x, approximate=True)

def _silu(x):
    return jax.nn.silu(x)

def _sigmoid(x):
    return jax.nn.sigmoid(x)

def _layernorm(x, axis=-1, eps=1e-05):
    m = jnp.mean(x, axis=axis, keepdims=True)
    v = jnp.var(x, axis=axis, keepdims=True)
    return (x - m) / jnp.sqrt(v + eps)

def _scatter_add(tgt, idx, src, axis=0):
    return tgt.at[idx].add(src)

def _segment_sum(src, seg, n):
    return jax.ops.segment_sum(src, seg, n)
kernel_name = 'mk_decoder_postln_d2_seqx_r8_ab77f1'

def setup_inputs(seed: int=0):
    np.random.seed(seed)
    _w = jnp.asarray

    def _rec_inputs():
        import jax
        import jax.numpy as jnp
        _rk = jax.random.key(seed)
        x = 7.22e-05 + 1 * jax.random.normal(jax.random.fold_in(_rk, 1), (16, 128, 256), jnp.float32)
        _lenS = 128 - jax.random.randint(jax.random.fold_in(_rk, 7), (16,), 0, max(1, 128 // 4) + 1, jnp.int32)
        _lenS2 = 128 - jax.random.randint(jax.random.fold_in(_rk, 8), (16,), 0, max(1, 128 // 4) + 1, jnp.int32)
        _ctx_512P = jax.random.normal(jax.random.fold_in(_rk, 11), (16, 16, 64), jnp.float32)
        _ctx_512c = jax.random.dirichlet(jax.random.fold_in(_rk, 511), 0.3 * jnp.ones((16,), jnp.float32), (16, 128))
        _ctx_512t = jnp.einsum('bsk,bkd->bsd', _ctx_512c, _ctx_512P)
        _ctx_512t = _ctx_512t * jax.lax.rsqrt(jnp.mean(jnp.square(_ctx_512t)) + 1e-12) * 0.953939
        ctx_512 = -0.000514642 + 1.00011 * (_ctx_512t + 0.3 * jax.random.normal(jax.random.fold_in(_rk, 611), (16, 128, 64), jnp.float32))
        return (x, ctx_512)
    x, ctx_512 = _rec_inputs()

    def _L0_attn_setup():
        import jax, jax.numpy as jnp
        import numpy as np
        NH, HS, K = (32, 256, 16)
        HD = HS // NH
        B, L = (4, 256)
        EPS = 1e-06

        def _ln(x, gamma, beta):
            mu = x.mean(-1, keepdims=True)
            var = x.var(-1, keepdims=True)
            return gamma * ((x - mu) / jnp.sqrt(var + EPS)) + beta

        def _ln_fused_l2_bwd(x, target, gamma, beta):
            D = x.shape[-1]
            mu = x.mean(-1, keepdims=True)
            std = jnp.sqrt(x.var(-1, keepdims=True) + EPS)
            xh = (x - mu) / std
            gxh = (gamma * xh + beta - target) * gamma
            return (D * gxh - gxh.sum(-1, keepdims=True) - xh * (gxh * xh).sum(-1, keepdims=True)) / (D * std)

        def _forward(hidden_states, q_w, k_w, v_w, o_w, W1, b1, ttt_norm_weight, ttt_norm_bias, ttt_lr_weight, ttt_lr_bias, learnable_token_idx, post_norm_weight, post_norm_bias):
            Bb, Ll, _ = hidden_states.shape
            NM = Ll // K

            def proj_heads(w):
                return (hidden_states @ w.T).reshape(Bb, Ll, NH, HD).transpose(0, 2, 1, 3)
            XQ = proj_heads(q_w).reshape(Bb, NH, NM, K, HD)
            XK = proj_heads(k_w).reshape(Bb, NH, NM, K, HD)
            XV = proj_heads(v_w).reshape(Bb, NH, NM, K, HD)
            X = hidden_states.reshape(Bb, NM, K, HS)
            ttt_lr = jnp.einsum('bnkc,hdc->bhnkd', X, ttt_lr_weight) + ttt_lr_bias.reshape(1, NH, 1, 1, 1)
            ttt_lr_eta = jax.nn.sigmoid(ttt_lr).transpose(0, 1, 2, 4, 3) / HD
            token_idx = jnp.clip(1.0 / jnp.arange(1, K + 1, dtype=jnp.float32) + learnable_token_idx, 0.0, None)
            eta = token_idx.reshape(1, 1, 1, K, 1) * ttt_lr_eta
            ln_w = ttt_norm_weight.reshape(NH, 1, HD)
            ln_b = ttt_norm_bias.reshape(NH, 1, HD)

            def step(carry, x):
                W1_s, b1_s = carry
                xq, xk, xv, eta_mb = x
                Z1 = xk @ W1_s + b1_s
                grad = _ln_fused_l2_bwd(Z1, xv - xk, ln_w, ln_b)
                Attn1 = jnp.tril(xq @ xk.swapaxes(-1, -2))
                b1_bar = b1_s - jnp.tril(eta_mb) @ grad
                Z1_bar = xq @ W1_s - eta_mb * Attn1 @ grad + b1_bar
                last_eta = eta_mb[:, :, -1, :, None]
                W1_new = W1_s - (last_eta * xk).swapaxes(-1, -2) @ grad
                b1_new = b1_s - jnp.sum(last_eta * grad, axis=-2, keepdims=True)
                out = xq + _ln(Z1_bar, ln_w, ln_b)
                return ((W1_new, b1_new), out)
            init = (jnp.tile(W1[None], (Bb, 1, 1, 1)), jnp.tile(b1[None], (Bb, 1, 1, 1)))
            xs = (XQ.transpose(2, 0, 1, 3, 4), XK.transpose(2, 0, 1, 3, 4), XV.transpose(2, 0, 1, 3, 4), eta.transpose(2, 0, 1, 3, 4))
            _, ys = jax.lax.scan(step, init, xs)
            out = ys.transpose(1, 0, 3, 2, 4).reshape(Bb, Ll, HS)
            out = _ln(out, post_norm_weight, post_norm_bias)
            return out @ o_w.T
        key = jax.random.key(seed)
        ks = jax.random.split(key, 8)
        s = 0.02
        return {'hidden_states': jax.random.normal(ks[0], (B, L, HS), jnp.float32), 'position_ids': jnp.tile(jnp.arange(L, dtype=jnp.int32)[None], (B, 1)), 'q_w': jax.random.normal(ks[1], (HS, HS), jnp.float32) * s, 'k_w': jax.random.normal(ks[2], (HS, HS), jnp.float32) * s, 'v_w': jax.random.normal(ks[3], (HS, HS), jnp.float32) * s, 'o_w': jax.random.normal(ks[4], (HS, HS), jnp.float32) * s, 'W1': jax.random.normal(ks[5], (NH, HD, HD), jnp.float32) * s, 'b1': jnp.zeros((NH, 1, HD), jnp.float32), 'ttt_norm_weight': jnp.ones((NH, HD), jnp.float32), 'ttt_norm_bias': jnp.zeros((NH, HD), jnp.float32), 'ttt_lr_weight': jax.random.normal(ks[6], (NH, 1, HS), jnp.float32) * s, 'ttt_lr_bias': jnp.zeros((NH, 1), jnp.float32), 'learnable_token_idx': jnp.zeros((K,), jnp.float32), 'post_norm_weight': jnp.ones((HS,), jnp.float32), 'post_norm_bias': jnp.zeros((HS,), jnp.float32)}
    _L0_attn_all = _L0_attn_setup()
    _L0_attn_in = {k: v for k, v in _L0_attn_all.items() if k in ('position_ids', 'q_w', 'k_w', 'v_w', 'o_w', 'W1', 'b1', 'ttt_norm_weight', 'ttt_norm_bias', 'ttt_lr_weight', 'ttt_lr_bias', 'learnable_token_idx', 'post_norm_weight', 'post_norm_bias')}
    del _L0_attn_all

    def _L0_xattn_setup():
        import jax, jax.numpy as jnp
        import numpy as np
        import math
        NUM_Q_HEADS = 32
        NUM_KV_HEADS = 8
        key = jax.random.key(seed)
        k1, k2, k3 = jax.random.split(key, 3)
        B, S, E = (2, 256, 256)
        kv_E = NUM_KV_HEADS * (E // NUM_Q_HEADS)
        q = jax.random.normal(k1, (B, S, E), dtype=jnp.float32)
        k = jax.random.normal(k2, (B, S, kv_E), dtype=jnp.float32)
        v = jax.random.normal(k3, (B, S, kv_E), dtype=jnp.float32)
        return {'q': q, 'k': k, 'v': v}
    _L0_xattn_all = _L0_xattn_setup()
    _L0_xattn_in = {k: v for k, v in _L0_xattn_all.items() if k in ()}
    del _L0_xattn_all

    def _L0_ffn_setup():
        import jax, jax.numpy as jnp
        import numpy as np
        HIDDEN = 256
        INTER = 1024
        B, S = (4, 128)

        def _qmatmul(x, w_int8, scale):
            y = jnp.einsum('bsh,ho->bso', x, w_int8.astype(x.dtype))
            return y * scale
        key = jax.random.key(seed)
        ks = jax.random.split(key, 7)
        x = jax.random.normal(ks[0], (B, S, HIDDEN), dtype=jnp.float32)
        w_gate = jax.random.randint(ks[1], (HIDDEN, INTER), -128, 128, dtype=jnp.int32).astype(jnp.int8)
        w_up = jax.random.randint(ks[2], (HIDDEN, INTER), -128, 128, dtype=jnp.int32).astype(jnp.int8)
        w_down = jax.random.randint(ks[3], (INTER, HIDDEN), -128, 128, dtype=jnp.int32).astype(jnp.int8)
        s_gate = jax.random.uniform(ks[4], (INTER,), dtype=jnp.float32) * 0.02 + 0.001
        s_up = jax.random.uniform(ks[5], (INTER,), dtype=jnp.float32) * 0.02 + 0.001
        s_down = jax.random.uniform(ks[6], (HIDDEN,), dtype=jnp.float32) * 0.02 + 0.001
        return {'x': x, 'w_gate': w_gate, 'w_up': w_up, 'w_down': w_down, 's_gate': s_gate, 's_up': s_up, 's_down': s_down}
    _L0_ffn_all = _L0_ffn_setup()
    _L0_ffn_in = {k: v for k, v in _L0_ffn_all.items() if k in ('w_gate', 'w_up', 'w_down', 's_gate', 's_up', 's_down')}
    del _L0_ffn_all

    def _L1_attn_setup():
        import jax, jax.numpy as jnp
        import numpy as np
        H = 16
        key = jax.random.key(seed)
        ks = jax.random.split(key, 9)
        L, N, E, I = (256, 2, 256, 256)
        s = 0.02
        return {'query': jax.random.normal(ks[0], (L, N, E), jnp.float32), 'q_proj': jax.random.normal(ks[1], (I, E), jnp.float32) * s, 'q_bias': jax.random.normal(ks[2], (I,), jnp.float32) * s, 'k_proj': jax.random.normal(ks[3], (I, E), jnp.float32) * s, 'k_bias': jax.random.normal(ks[4], (I,), jnp.float32) * s, 'v_proj': jax.random.normal(ks[5], (I, E), jnp.float32) * s, 'v_bias': jax.random.normal(ks[6], (I,), jnp.float32) * s, 'out_proj': jax.random.normal(ks[7], (E, I), jnp.float32) * s, 'out_bias': jax.random.normal(ks[8], (E,), jnp.float32) * s}
    _L1_attn_all = _L1_attn_setup()
    _L1_attn_in = {k: v for k, v in _L1_attn_all.items() if k in ('q_proj', 'q_bias', 'k_proj', 'k_bias', 'v_proj', 'v_bias', 'out_proj', 'out_bias')}
    del _L1_attn_all

    def _L1_xattn_setup():
        import jax, jax.numpy as jnp
        import numpy as np
        B, S, L = (2, 128, 128)
        DIM_Q, H, K, D_C, D_CQ, R = (256, 16, 128, 64, 192, 64)

        def _rope_tables(seq_len, dim, dtype):
            inv_freq = 1.0 / 10000.0 ** (jnp.arange(0, dim, 2, dtype=dtype) / dim)
            t = jnp.arange(seq_len, dtype=dtype)
            freqs = t[:, None] * inv_freq[None, :]
            sin = jnp.repeat(jnp.sin(freqs), 2, axis=-1)
            cos = jnp.repeat(jnp.cos(freqs), 2, axis=-1)
            return (sin, cos)

        def _rotate_half(x):
            h = x.shape[-1] // 2
            return jnp.concatenate([-x[..., h:], x[..., :h]], axis=-1)
        key = jax.random.key(seed)
        ks = jax.random.split(key, 8)
        s_in = 1.0 / np.sqrt(DIM_Q)
        s_k = 1.0 / np.sqrt(K)
        s_cq = 1.0 / np.sqrt(D_CQ)
        s_c = 1.0 / np.sqrt(D_C)
        return {'hidden_q': jax.random.normal(ks[0], (B, S, DIM_Q), jnp.float32), 'kv_c': jax.random.normal(ks[1], (B, L, D_C), jnp.float32), 'Wq': jax.random.normal(ks[2], (H * K, DIM_Q), jnp.float32) * s_in, 'w_kc_q': jax.random.normal(ks[3], (H, K, D_CQ), jnp.float32) * s_k, 'w_kc_kv': jax.random.normal(ks[4], (H, K, D_C), jnp.float32) * s_k, 'W_qr': jax.random.normal(ks[5], (H, D_CQ, R), jnp.float32) * s_cq / np.sqrt(R), 'W_kr': jax.random.normal(ks[6], (H, D_C, R), jnp.float32) * s_c, 'Wo': jax.random.normal(ks[7], (DIM_Q, H * K), jnp.float32) * s_k}
    _L1_xattn_all = _L1_xattn_setup()
    _L1_xattn_in = {k: v for k, v in _L1_xattn_all.items() if k in ('Wq', 'w_kc_q', 'w_kc_kv', 'W_qr', 'W_kr', 'Wo')}
    del _L1_xattn_all

    def _L1_ffn_setup():
        import jax, jax.numpy as jnp
        import numpy as np
        E, K, H, F = (64, 6, 256, 96)
        G, KG = (8, 4)
        SHARED_F = 96
        SCALE = 2.5
        T = 2 * 128
        CAP = 2 * (T * K // E)

        def _grouped_topk(logits, bias):
            scores = jax.nn.sigmoid(logits.astype(jnp.float32))
            scores_b = scores + bias[None, :]
            gs = scores_b.reshape(-1, G, E // G)
            group_scores = jnp.sum(jax.lax.top_k(gs, 2)[0], axis=-1)
            gidx = jax.lax.top_k(group_scores, KG)[1]
            rows = jnp.arange(group_scores.shape[0])[:, None]
            group_mask = jnp.zeros_like(group_scores).at[rows, gidx].set(1.0)
            score_mask = jnp.repeat(group_mask, E // G, axis=-1) > 0
            tmp = jnp.where(score_mask, scores_b, -jnp.inf)
            topk_ids = jax.lax.top_k(tmp, K)[1]
            topk_w = jnp.take_along_axis(scores, topk_ids, axis=-1)
            topk_w = topk_w / jnp.sum(topk_w, axis=-1, keepdims=True)
            return (topk_w * SCALE, topk_ids)

        def _routed_moe(x, topk_w, topk_ids, w_gate, w_up, w_down):
            Tn = x.shape[0]
            flat_e = topk_ids.reshape(-1)
            order = jnp.argsort(flat_e)
            se = flat_e[order]
            pos = jnp.arange(Tn * K) - jnp.searchsorted(se, se, side='left')
            tok = order // K
            valid = pos < CAP
            slot = jnp.where(valid, pos, CAP)
            buf = jnp.zeros((E, CAP + 1, H), x.dtype).at[se, slot].set(x[tok])[:, :CAP]
            h = jax.nn.silu(jnp.einsum('ech,ehf->ecf', buf, w_gate)) * jnp.einsum('ech,ehf->ecf', buf, w_up)
            out = jnp.einsum('ecf,efh->ech', h, w_down)
            gathered = out[se, jnp.minimum(pos, CAP - 1)] * valid.astype(x.dtype)[:, None]
            w = topk_w.reshape(-1)[order].astype(x.dtype)[:, None]
            return jax.ops.segment_sum(gathered * w, tok, num_segments=Tn)
        key = jax.random.key(seed)
        ks = jax.random.split(key, 9)
        s = 0.02
        return dict(hidden_states=jax.random.normal(ks[0], (2, 128, H), jnp.float32), gate_w=jax.random.normal(ks[1], (H, E), jnp.float32) * s, bias=jax.random.normal(ks[2], (E,), jnp.float32) * s, w_gate=jax.random.normal(ks[3], (E, H, F), jnp.float32) * s, w_up=jax.random.normal(ks[4], (E, H, F), jnp.float32) * s, w_down=jax.random.normal(ks[5], (E, F, H), jnp.float32) * s, ws_gate=jax.random.normal(ks[6], (H, SHARED_F), jnp.float32) * s, ws_up=jax.random.normal(ks[7], (H, SHARED_F), jnp.float32) * s, ws_down=jax.random.normal(ks[8], (SHARED_F, H), jnp.float32) * s)
    _L1_ffn_all = _L1_ffn_setup()
    _L1_ffn_in = {k: v for k, v in _L1_ffn_all.items() if k in ('gate_w', 'bias', 'w_gate', 'w_up', 'w_down', 'ws_gate', 'ws_up', 'ws_down')}
    del _L1_ffn_all
    return {'x': x, 'ctx_512': ctx_512, 'L0_attn_position_ids': _L0_attn_in['position_ids'], 'L0_attn_q_w': _L0_attn_in['q_w'], 'L0_attn_k_w': _L0_attn_in['k_w'], 'L0_attn_v_w': _L0_attn_in['v_w'], 'L0_attn_o_w': _L0_attn_in['o_w'], 'L0_attn_W1': _L0_attn_in['W1'], 'L0_attn_b1': _L0_attn_in['b1'], 'L0_attn_ttt_norm_weight': _L0_attn_in['ttt_norm_weight'], 'L0_attn_ttt_norm_bias': _L0_attn_in['ttt_norm_bias'], 'L0_attn_ttt_lr_weight': _L0_attn_in['ttt_lr_weight'], 'L0_attn_ttt_lr_bias': _L0_attn_in['ttt_lr_bias'], 'L0_attn_learnable_token_idx': _L0_attn_in['learnable_token_idx'], 'L0_attn_post_norm_weight': _L0_attn_in['post_norm_weight'], 'L0_attn_post_norm_bias': _L0_attn_in['post_norm_bias'], 'L0_ffn_w_gate': _L0_ffn_in['w_gate'], 'L0_ffn_w_up': _L0_ffn_in['w_up'], 'L0_ffn_w_down': _L0_ffn_in['w_down'], 'L0_ffn_s_gate': _L0_ffn_in['s_gate'], 'L0_ffn_s_up': _L0_ffn_in['s_up'], 'L0_ffn_s_down': _L0_ffn_in['s_down'], 'L1_attn_q_proj': _L1_attn_in['q_proj'], 'L1_attn_q_bias': _L1_attn_in['q_bias'], 'L1_attn_k_proj': _L1_attn_in['k_proj'], 'L1_attn_k_bias': _L1_attn_in['k_bias'], 'L1_attn_v_proj': _L1_attn_in['v_proj'], 'L1_attn_v_bias': _L1_attn_in['v_bias'], 'L1_attn_out_proj': _L1_attn_in['out_proj'], 'L1_attn_out_bias': _L1_attn_in['out_bias'], 'L1_xattn_Wq': _L1_xattn_in['Wq'], 'L1_xattn_w_kc_q': _L1_xattn_in['w_kc_q'], 'L1_xattn_w_kc_kv': _L1_xattn_in['w_kc_kv'], 'L1_xattn_W_qr': _L1_xattn_in['W_qr'], 'L1_xattn_W_kr': _L1_xattn_in['W_kr'], 'L1_xattn_Wo': _L1_xattn_in['Wo'], 'L1_ffn_gate_w': _L1_ffn_in['gate_w'], 'L1_ffn_bias': _L1_ffn_in['bias'], 'L1_ffn_w_gate': _L1_ffn_in['w_gate'], 'L1_ffn_w_up': _L1_ffn_in['w_up'], 'L1_ffn_w_down': _L1_ffn_in['w_down'], 'L1_ffn_ws_gate': _L1_ffn_in['ws_gate'], 'L1_ffn_ws_up': _L1_ffn_in['ws_up'], 'L1_ffn_ws_down': _L1_ffn_in['ws_down']}

def reference(x, ctx_512, L0_attn_position_ids, L0_attn_q_w, L0_attn_k_w, L0_attn_v_w, L0_attn_o_w, L0_attn_W1, L0_attn_b1, L0_attn_ttt_norm_weight, L0_attn_ttt_norm_bias, L0_attn_ttt_lr_weight, L0_attn_ttt_lr_bias, L0_attn_learnable_token_idx, L0_attn_post_norm_weight, L0_attn_post_norm_bias, L0_ffn_w_gate, L0_ffn_w_up, L0_ffn_w_down, L0_ffn_s_gate, L0_ffn_s_up, L0_ffn_s_down, L1_attn_q_proj, L1_attn_q_bias, L1_attn_k_proj, L1_attn_k_bias, L1_attn_v_proj, L1_attn_v_bias, L1_attn_out_proj, L1_attn_out_bias, L1_xattn_Wq, L1_xattn_w_kc_q, L1_xattn_w_kc_kv, L1_xattn_W_qr, L1_xattn_W_kr, L1_xattn_Wo, L1_ffn_gate_w, L1_ffn_bias, L1_ffn_w_gate, L1_ffn_w_up, L1_ffn_w_down, L1_ffn_ws_gate, L1_ffn_ws_up, L1_ffn_ws_down):
    import jax
    import jax.numpy as jnp

    def _L0_attn_ref(hidden_states, position_ids, q_w, k_w, v_w, o_w, W1, b1, ttt_norm_weight, ttt_norm_bias, ttt_lr_weight, ttt_lr_bias, learnable_token_idx, post_norm_weight, post_norm_bias):
        import jax, jax.numpy as jnp
        import numpy as np
        NH, HS, K = (32, 256, 16)
        HD = HS // NH
        B, L = (4, 256)
        EPS = 1e-06

        def _ln(x, gamma, beta):
            mu = x.mean(-1, keepdims=True)
            var = x.var(-1, keepdims=True)
            return gamma * ((x - mu) / jnp.sqrt(var + EPS)) + beta

        def _ln_fused_l2_bwd(x, target, gamma, beta):
            D = x.shape[-1]
            mu = x.mean(-1, keepdims=True)
            std = jnp.sqrt(x.var(-1, keepdims=True) + EPS)
            xh = (x - mu) / std
            gxh = (gamma * xh + beta - target) * gamma
            return (D * gxh - gxh.sum(-1, keepdims=True) - xh * (gxh * xh).sum(-1, keepdims=True)) / (D * std)

        def _forward(hidden_states, q_w, k_w, v_w, o_w, W1, b1, ttt_norm_weight, ttt_norm_bias, ttt_lr_weight, ttt_lr_bias, learnable_token_idx, post_norm_weight, post_norm_bias):
            Bb, Ll, _ = hidden_states.shape
            NM = Ll // K

            def proj_heads(w):
                return (hidden_states @ w.T).reshape(Bb, Ll, NH, HD).transpose(0, 2, 1, 3)
            XQ = proj_heads(q_w).reshape(Bb, NH, NM, K, HD)
            XK = proj_heads(k_w).reshape(Bb, NH, NM, K, HD)
            XV = proj_heads(v_w).reshape(Bb, NH, NM, K, HD)
            X = hidden_states.reshape(Bb, NM, K, HS)
            ttt_lr = jnp.einsum('bnkc,hdc->bhnkd', X, ttt_lr_weight) + ttt_lr_bias.reshape(1, NH, 1, 1, 1)
            ttt_lr_eta = jax.nn.sigmoid(ttt_lr).transpose(0, 1, 2, 4, 3) / HD
            token_idx = jnp.clip(1.0 / jnp.arange(1, K + 1, dtype=jnp.float32) + learnable_token_idx, 0.0, None)
            eta = token_idx.reshape(1, 1, 1, K, 1) * ttt_lr_eta
            ln_w = ttt_norm_weight.reshape(NH, 1, HD)
            ln_b = ttt_norm_bias.reshape(NH, 1, HD)

            def step(carry, x):
                W1_s, b1_s = carry
                xq, xk, xv, eta_mb = x
                Z1 = xk @ W1_s + b1_s
                grad = _ln_fused_l2_bwd(Z1, xv - xk, ln_w, ln_b)
                Attn1 = jnp.tril(xq @ xk.swapaxes(-1, -2))
                b1_bar = b1_s - jnp.tril(eta_mb) @ grad
                Z1_bar = xq @ W1_s - eta_mb * Attn1 @ grad + b1_bar
                last_eta = eta_mb[:, :, -1, :, None]
                W1_new = W1_s - (last_eta * xk).swapaxes(-1, -2) @ grad
                b1_new = b1_s - jnp.sum(last_eta * grad, axis=-2, keepdims=True)
                out = xq + _ln(Z1_bar, ln_w, ln_b)
                return ((W1_new, b1_new), out)
            init = (jnp.tile(W1[None], (Bb, 1, 1, 1)), jnp.tile(b1[None], (Bb, 1, 1, 1)))
            xs = (XQ.transpose(2, 0, 1, 3, 4), XK.transpose(2, 0, 1, 3, 4), XV.transpose(2, 0, 1, 3, 4), eta.transpose(2, 0, 1, 3, 4))
            _, ys = jax.lax.scan(step, init, xs)
            out = ys.transpose(1, 0, 3, 2, 4).reshape(Bb, Ll, HS)
            out = _ln(out, post_norm_weight, post_norm_bias)
            return out @ o_w.T
        del position_ids
        return _forward(hidden_states, q_w, k_w, v_w, o_w, W1, b1, ttt_norm_weight, ttt_norm_bias, ttt_lr_weight, ttt_lr_bias, learnable_token_idx, post_norm_weight, post_norm_bias)

    def _L0_xattn_ref(q, k, v):
        import jax, jax.numpy as jnp
        import numpy as np
        import math
        NUM_Q_HEADS = 32
        NUM_KV_HEADS = 8
        B, S, E = q.shape
        H, KV = (NUM_Q_HEADS, NUM_KV_HEADS)
        D = E // H
        G = H // KV
        scale = math.sqrt(D)
        qh = q.reshape(B, S, KV, G, D).transpose(0, 2, 3, 1, 4)
        kh = k.reshape(B, S, KV, D).transpose(0, 2, 1, 3)
        vh = v.reshape(B, S, KV, D).transpose(0, 2, 1, 3)
        scores = jnp.einsum('bkgsd,bktd->bkgst', qh, kh) / scale
        weights = jax.nn.softmax(scores, axis=-1)
        out = jnp.einsum('bkgst,bktd->bkgsd', weights, vh)
        return out.transpose(0, 3, 1, 2, 4).reshape(B, S, E)

    def _L0_ffn_ref(x, w_gate, w_up, w_down, s_gate, s_up, s_down):
        import jax, jax.numpy as jnp
        import numpy as np
        HIDDEN = 256
        INTER = 1024
        B, S = (4, 128)

        def _qmatmul(x, w_int8, scale):
            y = jnp.einsum('bsh,ho->bso', x, w_int8.astype(x.dtype))
            return y * scale
        gate = jax.nn.silu(_qmatmul(x, w_gate, s_gate))
        up = _qmatmul(x, w_up, s_up)
        fuse = gate * up
        return _qmatmul(fuse, w_down, s_down)

    def _L1_attn_ref(query, q_proj, q_bias, k_proj, k_bias, v_proj, v_bias, out_proj, out_bias):
        import jax, jax.numpy as jnp
        import numpy as np
        H = 16
        L, N, E = query.shape
        h = H
        d = q_proj.shape[0] // h
        scale = d ** (-0.5)

        def split_heads(x):
            return x.reshape(L, N, h, d).transpose(1, 2, 0, 3)
        q = split_heads(query @ q_proj.T + q_bias) * scale
        k = split_heads(query @ k_proj.T + k_bias)
        v = split_heads(query @ v_proj.T + v_bias)
        scores = jnp.einsum('nhld,nhkd->nhlk', q, k)
        causal = jnp.tril(jnp.ones((L, L), dtype=bool))
        scores = jnp.where(causal, scores, jnp.float32(-10000.0))
        attn = jax.nn.softmax(scores, axis=-1)
        ctx = jnp.einsum('nhlk,nhkd->nhld', attn, v)
        ctx = ctx.transpose(2, 0, 1, 3).reshape(L, N, h * d)
        return ctx @ out_proj.T + out_bias

    def _L1_xattn_ref(hidden_q, kv_c, Wq, w_kc_q, w_kc_kv, W_qr, W_kr, Wo):
        import jax, jax.numpy as jnp
        import numpy as np
        B, S, L = (2, 128, 128)
        DIM_Q, H, K, D_C, D_CQ, R = (256, 16, 128, 64, 192, 64)

        def _rope_tables(seq_len, dim, dtype):
            inv_freq = 1.0 / 10000.0 ** (jnp.arange(0, dim, 2, dtype=dtype) / dim)
            t = jnp.arange(seq_len, dtype=dtype)
            freqs = t[:, None] * inv_freq[None, :]
            sin = jnp.repeat(jnp.sin(freqs), 2, axis=-1)
            cos = jnp.repeat(jnp.cos(freqs), 2, axis=-1)
            return (sin, cos)

        def _rotate_half(x):
            h = x.shape[-1] // 2
            return jnp.concatenate([-x[..., h:], x[..., :h]], axis=-1)
        b, s, _ = hidden_q.shape
        l = kv_c.shape[1]
        q_hk = (hidden_q @ Wq.T).reshape(b, s, H, K)
        q_big = jnp.einsum('bshk,hkq->bshq', q_hk, w_kc_q)
        sin, cos = _rope_tables(l, D_C, kv_c.dtype)
        kv_rope = kv_c * cos[None] + _rotate_half(kv_c) * sin[None]
        q_r = jnp.einsum('bshq,hqr->bhsr', q_big, W_qr)
        k_r = jnp.einsum('bld,hdr->bhlr', kv_rope, W_kr)
        scores = jnp.einsum('bhsr,bhlr->bhsl', q_r, k_r)
        attn = jax.nn.softmax(scores, axis=-1)
        ctx_c = jnp.einsum('bhsl,bld->bhsd', attn, kv_rope)
        ctx_lat = jnp.einsum('bhsd,hkd->bshk', ctx_c, w_kc_kv)
        out = ctx_lat.reshape(b, s, H * K) @ Wo.T
        return out

    def _L1_ffn_ref(hidden_states, gate_w, bias, w_gate, w_up, w_down, ws_gate, ws_up, ws_down):
        import jax, jax.numpy as jnp
        import numpy as np
        E, K, H, F = (64, 6, 256, 96)
        G, KG = (8, 4)
        SHARED_F = 96
        SCALE = 2.5
        T = 2 * 128
        CAP = 2 * (T * K // E)

        def _grouped_topk(logits, bias):
            scores = jax.nn.sigmoid(logits.astype(jnp.float32))
            scores_b = scores + bias[None, :]
            gs = scores_b.reshape(-1, G, E // G)
            group_scores = jnp.sum(jax.lax.top_k(gs, 2)[0], axis=-1)
            gidx = jax.lax.top_k(group_scores, KG)[1]
            rows = jnp.arange(group_scores.shape[0])[:, None]
            group_mask = jnp.zeros_like(group_scores).at[rows, gidx].set(1.0)
            score_mask = jnp.repeat(group_mask, E // G, axis=-1) > 0
            tmp = jnp.where(score_mask, scores_b, -jnp.inf)
            topk_ids = jax.lax.top_k(tmp, K)[1]
            topk_w = jnp.take_along_axis(scores, topk_ids, axis=-1)
            topk_w = topk_w / jnp.sum(topk_w, axis=-1, keepdims=True)
            return (topk_w * SCALE, topk_ids)

        def _routed_moe(x, topk_w, topk_ids, w_gate, w_up, w_down):
            Tn = x.shape[0]
            flat_e = topk_ids.reshape(-1)
            order = jnp.argsort(flat_e)
            se = flat_e[order]
            pos = jnp.arange(Tn * K) - jnp.searchsorted(se, se, side='left')
            tok = order // K
            valid = pos < CAP
            slot = jnp.where(valid, pos, CAP)
            buf = jnp.zeros((E, CAP + 1, H), x.dtype).at[se, slot].set(x[tok])[:, :CAP]
            h = jax.nn.silu(jnp.einsum('ech,ehf->ecf', buf, w_gate)) * jnp.einsum('ech,ehf->ecf', buf, w_up)
            out = jnp.einsum('ecf,efh->ech', h, w_down)
            gathered = out[se, jnp.minimum(pos, CAP - 1)] * valid.astype(x.dtype)[:, None]
            w = topk_w.reshape(-1)[order].astype(x.dtype)[:, None]
            return jax.ops.segment_sum(gathered * w, tok, num_segments=Tn)
        orig_shape = hidden_states.shape
        x = hidden_states.reshape(-1, H)
        router_logits = x @ gate_w
        topk_w, topk_ids = _grouped_topk(router_logits, bias)
        y = _routed_moe(x, topk_w, topk_ids, w_gate, w_up, w_down)
        shared = jax.nn.silu(x @ ws_gate) * (x @ ws_up) @ ws_down
        return (y + shared).reshape(orig_shape)
    x = _layernorm(x + _L0_attn_ref(x, L0_attn_position_ids, L0_attn_q_w, L0_attn_k_w, L0_attn_v_w, L0_attn_o_w, L0_attn_W1, L0_attn_b1, L0_attn_ttt_norm_weight, L0_attn_ttt_norm_bias, L0_attn_ttt_lr_weight, L0_attn_ttt_lr_bias, L0_attn_learnable_token_idx, L0_attn_post_norm_weight, L0_attn_post_norm_bias), axis=-1)
    x = _layernorm(x + _L0_xattn_ref(x, ctx_512, ctx_512), axis=-1)
    x = _layernorm(x + _L0_ffn_ref(x, L0_ffn_w_gate, L0_ffn_w_up, L0_ffn_w_down, L0_ffn_s_gate, L0_ffn_s_up, L0_ffn_s_down), axis=-1)
    x = _layernorm(x + _L1_attn_ref(x, L1_attn_q_proj, L1_attn_q_bias, L1_attn_k_proj, L1_attn_k_bias, L1_attn_v_proj, L1_attn_v_bias, L1_attn_out_proj, L1_attn_out_bias), axis=-1)
    x = _layernorm(x + _L1_xattn_ref(x, ctx_512, L1_xattn_Wq, L1_xattn_w_kc_q, L1_xattn_w_kc_kv, L1_xattn_W_qr, L1_xattn_W_kr, L1_xattn_Wo), axis=-1)
    x = _layernorm(x + _L1_ffn_ref(x, L1_ffn_gate_w, L1_ffn_bias, L1_ffn_w_gate, L1_ffn_w_up, L1_ffn_w_down, L1_ffn_ws_gate, L1_ffn_ws_up, L1_ffn_ws_down), axis=-1)
    return x

_drawn_inputs = setup_inputs


def setup_inputs(seed=0):
    import zlib

    import numpy as np

    out = dict(_drawn_inputs(seed))
    spreads = {'L0_attn_b1': (0.0, 0.1),
     'L0_attn_ttt_norm_weight': (1.0, 0.2),
     'L0_attn_ttt_norm_bias': (0.0, 0.1),
     'L0_attn_ttt_lr_bias': (0.0, 0.8),
     'L0_attn_learnable_token_idx': (0.0, 0.1),
     'L0_attn_post_norm_weight': (1.0, 0.2),
     'L0_attn_post_norm_bias': (0.0, 0.1)}
    factors = {'L1_attn_q_proj': 8.0,
     'L1_attn_q_bias': 8.0,
     'L1_attn_k_proj': 8.0,
     'L1_attn_k_bias': 8.0,
     'L1_attn_v_bias': 8.0,
     'L1_attn_out_bias': 3.805,
     'L1_ffn_gate_w': 8.0,
     'L1_ffn_bias': 8.0,
     'L1_ffn_w_gate': 8.0,
     'L1_ffn_w_up': 8.0,
     'L1_ffn_w_down': 8.0,
     'L1_ffn_ws_gate': 5.411,
     'L1_ffn_ws_up': 5.495,
     'L1_ffn_ws_down': 5.399}
    for name, (base, spread) in spreads.items():
        noise = np.random.default_rng([zlib.crc32(name.encode()), seed]).standard_normal(out[name].shape)
        drawn = base * np.exp(spread * noise) if base else spread * noise
        out[name] = jnp.asarray(drawn.astype(out[name].dtype))
    for name, factor in factors.items():
        out[name] = (out[name] * factor).astype(out[name].dtype)
    return out
```

```python
from contextlib import ExitStack

import concourse.bass as bass
import numpy as np
from concourse import mybir

ALU = mybir.AluOpType
ACT = mybir.ActivationFunctionType
F32 = mybir.dt.float32
BF16 = mybir.dt.bfloat16
U32 = mybir.dt.uint32
I8 = mybir.dt.int8
I32 = mybir.dt.int32
AX_X = mybir.AxisListType.X

P = 128
B = 16
T = 128
D = 256
DH = D // P
LN_EPS = 1e-5


def need(eng, sem, value):
    if isinstance(value, int) and value <= 0:
        return
    eng.wait_ge(sem, value)


class Order:

    def __init__(self, eng, sem):
        self.eng, self.sem = eng, sem
        self.base, self.trip, self.per, self.k = 0, 0, 0, 0

    def enter(self, trip, per):
        self.base += self.k
        self.trip, self.per, self.k = trip, per, 0

    def leave(self, trips):
        assert self.k == self.per, (self.k, self.per)
        self.base += trips * self.per
        self.trip, self.per, self.k = 0, 0, 0

    def __call__(self, ins):
        ins.then_inc(self.sem, 1)
        self.k += 1
        self.eng.wait_ge(self.sem, self.base + self.trip * self.per + self.k)


def new_semaphore(nc, keep, name):
    keep["semaphores"].append(nc.alloc_semaphore(name))
    return keep["semaphores"][-1]


def give_back_semaphores(nc, keep):
    nc.clear_and_free_semaphores(keep["semaphores"])
    keep["semaphores"] = []
    nc.all_engine_barrier()


def first(b):
    return isinstance(b, int) and b == 0


def since(b, n):
    return not isinstance(b, int) or b >= n


def lagged(step, b, par, u, lag, units):
    k = u - lag
    if k >= 0:
        if not (isinstance(b, int) and b == B):
            step(b, par, k)
    elif not first(b):
        step(b - 1, 1 - par, k + units)


def each_sequence(eng, step, order=None, per=0, peeled=2):
    for b in range(peeled):
        step(b, b % 2, b // 2)
    trips = (B - peeled) // 2
    with eng.Fori(0, trips) as i:
        if order:
            order.enter(i, per)
        for par in range(2):
            step(2 * i + peeled + par, par, i + peeled // 2)
        if order:
            order.leave(trips)


class Norm:

    CHAIN = 4

    def __init__(self, nc, ctx, tag, keep, turned_psum):
        self.nc, self.x_tok, self.xT, self.ident, self.neg_half = nc, keep["x_tok"], keep["xT"], keep["ident"], keep["neg_half"]
        sb = lambda name, shape: ctx.enter_context(nc.sbuf_tensor(f"{tag}_{name}", shape, F32))
        sem = lambda name: new_semaphore(nc, keep, f"{tag}_{name}")
        self.total, self.stats, self.mean_var = sb("total", [P, D]), sb("stats", [P, 6]), sb("mean_var", [P, 2])
        self.spare = sb("spare", [P, 1])
        self.var_eps, self.rstd, self.normed = sb("var_eps", [P, 1]), sb("rstd", [P, 1]), sb("normed", [P, D])
        self.turned = turned_psum
        self.var_ready, self.rstd_ready = sem("var_ready"), sem("rstd_ready")
        self.norm_ready, self.kept = sem("norm_ready"), sem("kept")
        self.turn_ready, self.turn_copied = sem("turn_ready"), sem("turn_copied")

    def vector(self, eng, order, b, y):
        self.vector_begin(eng, order, b, y)
        self.vector_end(eng, b)

    def vector_begin(self, eng, order, b, y):
        nc = self.nc
        order(nc.vector.tensor_tensor(self.total[:], y, self.x_tok[:, b, :], ALU.add))
        order(nc.vector.bn_stats(self.stats[:], self.total[:]))
        nc.vector.memset(self.spare[:], 0.0)
        order(nc.vector.bn_aggr(self.mean_var[:], self.stats[:]))
        nc.vector.tensor_scalar(self.var_eps[:], self.mean_var[:, 1:2], LN_EPS, None, ALU.add).then_inc(self.var_ready, 1)

    def vector_end(self, eng, b):
        nc = self.nc
        need(eng, self.rstd_ready, b + 1)
        need(eng, self.kept, b)
        need(eng, self.turn_ready, b)
        nc.vector.tensor_scalar(self.normed[:], self.total[:], self.mean_var[:, 0:1], self.rstd[:],
                                ALU.subtract, ALU.mult).then_inc(self.norm_ready, 1)
        need(eng, self.norm_ready, b + 1)

    def gpsimd(self, eng, b):
        nc = self.nc
        need(eng, self.var_ready, b + 1)
        nc.gpsimd.tensor_tensor(self.rstd[:], self.var_eps[:], self.neg_half[:], ALU.pow).then_inc(self.rstd_ready, 1)
        need(eng, self.norm_ready, b + 1)
        nc.gpsimd.tensor_copy(self.x_tok[:, b, :], self.normed[:]).then_inc(self.kept, 1)

    def tensor(self, eng, b):
        need(eng, self.norm_ready, b + 1)
        need(eng, self.turn_copied, b)
        for c in range(DH):
            ins = self.nc.tensor.transpose(self.turned[:, c * T:(c + 1) * T], self.normed[:, c * P:(c + 1) * P], self.ident[:])
        ins.then_inc(self.turn_ready, 1)

    def scalar(self, eng, b):
        need(eng, self.turn_ready, b + 1)
        self.nc.scalar.copy(self.xT[:, :, bass.ts(b, T)], self.turned[:].rearrange("p (c t) -> p c t", c=DH)).then_inc(self.turn_copied, 1)

    def done(self, eng):
        eng.wait_ge(self.kept, B)
        eng.wait_ge(self.turn_copied, B)


def cross_attention_gqa(nc, keep, io):
    NQ, NKV, HD = 32, 8, 8
    G = NQ // NKV
    UH = G
    U = NQ // UH
    NB = 4
    TURN_LAG, WEIGH_LAG = 3, 4
    SKEW = 4
    with ExitStack() as ctx:
        sb = lambda name, shape: ctx.enter_context(nc.sbuf_tensor(f"gqa_{name}", shape, F32))
        ps = lambda name, shape: ctx.enter_context(nc.psum_tensor(f"gqa_{name}", shape, F32))
        sem = lambda name: new_semaphore(nc, keep, f"gqa_{name}")
        q_feat = sb("q_feat", [P, 2, DH, NKV // DH, T])
        keys = sb("keys", [P, 2, DH, G, T])
        keys_in = sb("keys_in", [P, 2, DH, T])
        ctx_in = sb("ctx_in", [T, B, NKV * HD])
        values = sb("values", [T, 2, NKV, HD + 1])
        probs = sb("probs", [T, NB, UH, T])
        probsT = sb("probsT", [T, NB, UH, T])
        row_max = sb("row_max", [T, NB, UH])
        rsum = sb("rsum", [T, NQ])
        attended = sb("attended", [T, NQ, HD])
        scores = ps("scores", [T, NB, UH, T])
        turned = ps("turned", [T, 2, UH, T])
        weighted = ps("weighted", [T, NQ * (HD + 1)])
        normT = ps("normT", [P, DH * T])
        keys_ready, keys_loaded, ctx_loaded, ones_set = sem("keys_ready"), [sem("keys_loaded0"), sem("keys_loaded1")], sem("ctx_loaded"), sem("ones_set")
        q_ready, v_ready = sem("q_ready"), sem("v_ready")
        scores_ready, shifted, max_ready = sem("scores_ready"), sem("shifted"), sem("max_ready")
        exp_ready, turn_ready, turn_copied, weigh_ready, out_read, chain = (
            sem("exp_ready"), sem("turn_ready"), sem("turn_copied"), sem("weigh_ready"), sem("out_read"), sem("chain"))
        norm = Norm(nc, ctx, "gqa_n", keep, normT)
        weighted3 = weighted[:].rearrange("p (h e) -> p h e", h=NQ)
        HKV = NKV // DH
        ROWS = G * HD

        block = ctx.enter_context(nc.Block())

        @block.sync
        def _(sp):
            sp.dma_start(ctx_in[:], io["ctx"].rearrange("b t d -> t b d")).then_inc(ctx_loaded, 16)
            def step(b, par, pair):
                need(sp, keys_ready, b - 1)
                sp.dma_start(keys_in[:, par], io["ctx_rep"][b].rearrange("c p t -> p c t")).then_inc(keys_loaded[par], 16)
            each_sequence(sp, step)

        @block.gpsimd
        def _(pool):
            nc.gpsimd.memset(values[:, :, :, HD:HD + 1], 1.0).then_inc(ones_set, 1)
            pool.wait_ge(ctx_loaded, 16)

            def step(b, par, pair):
                need(pool, scores_ready, U * (b - 1))
                nc.gpsimd.tensor_tensor(q_feat[:, par], keep["xT"][:, :, bass.ts(b, T)].unsqueeze(2).to_broadcast([P, DH, HKV, T]),
                                        keep["group_mask"][:].unsqueeze(1).unsqueeze(3).to_broadcast([P, DH, HKV, T]), ALU.mult).then_inc(q_ready, 1)
                need(pool, weigh_ready, U * (b - 1))
                nc.gpsimd.tensor_copy(values[:, par, :, 0:HD], ctx_in[:, b, :].rearrange("p (k d) -> p k d", k=NKV)).then_inc(v_ready, 1)
                if not first(b):
                    norm.gpsimd(pool, b - 1)
            each_sequence(pool, step)
            norm.gpsimd(pool, B - 1)

        @block.tensor
        def _(pe):
            def score(b, par, u):
                if u == 0:
                    need(pe, keys_ready, b + 1)
                    need(pe, q_ready, b + 1)
                need(pe, shifted, U * b + u + 1 - NB)
                half, r = u // HKV, u % HKV
                nc.tensor.matmul(scores[:, u % NB], q_feat[:, par, half, r, :], keys[:, par, half, :, :],
                                 start=True, stop=True).then_inc(scores_ready, 1)

            def turn(b, par, u):
                need(pe, exp_ready, U * b + u + 1)
                need(pe, turn_copied, U * b + u - 1)
                for h in range(UH):
                    ins = nc.tensor.transpose(turned[:, u % 2, h, :], probs[:, u % NB, h, :], keep["ident"][:])
                ins.then_inc(turn_ready, 1)

            def weigh(b, par, u):
                if u == 0:
                    need(pe, v_ready, b + 1)
                    need(pe, out_read, b)
                need(pe, turn_copied, U * b + u + 1)
                for h in range(UH):
                    ins = nc.tensor.matmul(weighted3[:, u * UH + h, :], probsT[:, u % NB, h, :], values[:, par, u, :],
                                           start=True, stop=True)
                ins.then_inc(weigh_ready, 1)

            pe.wait_ge(ones_set, 1)

            def step(b, par, pair):
                for u in range(U):
                    score(b, par, u)
                    lagged(turn, b, par, u, TURN_LAG, U)
                    lagged(weigh, b, par, u, WEIGH_LAG, U)
                    if u == U - 1 and not first(b):
                        norm.tensor(pe, b - 1)
            each_sequence(pe, step)
            for u in range(WEIGH_LAG):
                if u < TURN_LAG:
                    lagged(turn, B, 0, u, TURN_LAG, U)
                lagged(weigh, B, 0, u, WEIGH_LAG, U)
            norm.tensor(pe, B - 1)

        @block.scalar
        def _(act):
            def spread_keys(b, par, pair):
                act.wait_ge(keys_loaded[par], 16 * (pair + 1))
                need(act, scores_ready, U * (b - 1))
                for j in range(G):
                    ins = nc.scalar.mul(keys[:, par, :, j, :], keys_in[:, par], keep["head_mask"][:, j:j + 1])
                ins.then_inc(keys_ready, 1)

            def copy_turned(b, par, u):
                need(act, turn_ready, U * b + u + 1)
                need(act, weigh_ready, U * b + u + 1 - NB)
                nc.scalar.copy(probsT[:, u % NB], turned[:, u % 2]).then_inc(turn_copied, 1)

            def exponential(b, par, u):
                need(act, shifted, U * b + u + 1)
                nc.scalar.activation(probs[:, u % NB], probs[:, u % NB], ACT.Exp, scale=HD ** -0.5).then_inc(exp_ready, 1)

            def step(b, par, pair):
                spread_keys(b, par, pair)
                for u in range(U):
                    lagged(copy_turned, b, par, u, TURN_LAG + SKEW, U)
                    lagged(exponential, b, par, u, SKEW, U)
                    if u == SKEW and since(b, 2):
                        norm.scalar(act, b - 2)
            each_sequence(act, step)
            for u in range(TURN_LAG + SKEW):
                lagged(copy_turned, B, 0, u, TURN_LAG + SKEW, U)
                if u < SKEW:
                    lagged(exponential, B, 0, u, SKEW, U)
                if u == SKEW:
                    norm.scalar(act, B - 2)
            norm.scalar(act, B - 1)
            norm.done(act)

        @block.vector
        def _(dve):
            order = Order(dve, chain)

            def divide(b):
                need(dve, weigh_ready, U * (b + 1))
                order(nc.vector.reciprocal(rsum[:], weighted3[:, :, HD]))
                nc.vector.tensor_tensor(attended[:], weighted3[:, :, 0:HD], rsum[:].unsqueeze(2).to_broadcast([T, NQ, HD]),
                                        ALU.mult).then_inc(out_read, 1)

            def add(b):
                need(dve, out_read, b + 1)
                norm.vector_begin(dve, order, b, attended[:].rearrange("p h e -> p (h e)"))

            def step(b, par, pair):
                for u in range(U):
                    need(dve, scores_ready, U * b + u + 1)
                    order(nc.vector.tensor_reduce(row_max[:, u % NB], scores[:, u % NB], AX_X, ALU.max))
                    need(dve, turn_ready, U * b + u + 1 - NB)
                    nc.vector.tensor_tensor(probs[:, u % NB], scores[:, u % NB],
                                            row_max[:, u % NB].unsqueeze(2).to_broadcast([T, UH, T]), ALU.subtract).then_inc(shifted, 1)
                    if u == WEIGH_LAG - 1 and not first(b):
                        divide(b - 1)
                    if u == WEIGH_LAG and not first(b):
                        add(b - 1)
                    if u == WEIGH_LAG + 1 and not first(b):
                        norm.vector_end(dve, b - 1)
            each_sequence(dve, step, order, per=2 * (U + 4))
            divide(B - 1)
            add(B - 1)
            norm.vector_end(dve, B - 1)


def gated_ffn_int8(nc, keep, io):
    F = io["ffn_w_gate"].shape[1] * 4
    FT = F // P
    GB = 4
    GT = GB * T
    NG = B // GB
    PARTS = 3
    with ExitStack() as ctx:
        sb = lambda name, shape, dt=F32: ctx.enter_context(nc.sbuf_tensor(f"ff_{name}", shape, dt))
        ps = lambda name, shape: ctx.enter_context(nc.psum_tensor(f"ff_{name}", shape, F32))
        sem = lambda name: new_semaphore(nc, keep, f"ff_{name}")
        w_in = sb("w_in", [P, DH, 2, F // 4], I32)
        wd_in = sb("wd_in", [P, FT, D // 4], I32)
        w_up = sb("w_gate_up", [P, DH, 2, F], BF16)
        w_down = sb("w_down", [P, FT, D], BF16)
        s_in = sb("s_in", [P, 2, FT])
        s_down = sb("s_down", [P, D])
        x_parts = sb("x_parts", [P, PARTS, DH, GT], BF16)
        x_rest = sb("x_rest", [P, DH, GT])
        gate = sb("gate", [P, 2, GT])
        fused = sb("fused", [P, 2, GT])
        h_rest = sb("h_rest", [P, 2, GT])
        h_parts = sb("h_parts", [P, 2, PARTS, FT, GT], BF16)
        y = sb("y", [P, D])
        gate_ps, up_ps = ps("gate_ps", [P, 2, GT]), ps("up_ps", [P, 2, GT])
        down_ps = ps("down_ps", [P, 2, 512])
        normT = ps("normT", [P, DH * T])
        loaded, cast_done, x_split, x_first, x_second = sem("loaded"), sem("cast_done"), sem("x_split"), sem("x_first"), sem("x_second")
        gate_ready, up_ready, silu_ready, fused_ready, h_first, h_second, h_split = (
            sem("gate_ready"), sem("up_ready"), sem("silu_ready"), sem("fused_ready"), sem("h_first"), sem("h_second"), sem("h_split"))
        h_rest_ready, x_rest_ready = sem("h_rest_ready"), sem("x_rest_ready")
        down_ready, y_ready, chain = sem("down_ready"), sem("y_ready"), sem("chain")
        norm = Norm(nc, ctx, "ff_n", keep, normT)

        block = ctx.enter_context(nc.Block())

        @block.sync
        def _(sp):
            for k, name in enumerate(("ffn_w_gate", "ffn_w_up")):
                sp.dma_start(w_in[:, :, k, :], io[name].rearrange("(c p) f -> p c f", p=P)).then_inc(loaded, 16)
            sp.dma_start(wd_in[:], io["ffn_w_down"].rearrange("(f p) d -> p f d", p=P)).then_inc(loaded, 16)
            for k, name in enumerate(("ffn_s_gate", "ffn_s_up")):
                sp.dma_start(s_in[:, k, :], io[name]).then_inc(loaded, 16)
            sp.dma_start(s_down[:], io["ffn_s_down"].unsqueeze(0).to_broadcast([P, D])).then_inc(loaded, 16)

        LOADED = 6 * 16

        @block.gpsimd
        def _(pool):
            def step(b):
                norm.gpsimd(pool, b)
            with pool.Fori(0, B) as b:
                step(b)

        @block.scalar
        def _(act):
            act.wait_ge(loaded, LOADED)
            nc.scalar.copy(w_up[:, 0], w_in[:, 0].bitcast(I8)).then_inc(cast_done, 1)

            def group(g):
                need(act, up_ready, FT * g)
                nc.scalar.copy(x_parts[:, 0], keep["xT"][:, :, bass.ts(g, GT)]).then_inc(x_first, 1)
                act.wait_ge(x_rest_ready, g + 1)
                nc.scalar.copy(x_parts[:, 1], x_rest[:]).then_inc(x_second, 1)
                for f in range(FT):
                    n = FT * g + f
                    need(act, gate_ready, n + 1)
                    need(act, fused_ready, n - 1)
                    nc.scalar.activation(gate[:, f % 2], gate_ps[:, f % 2], ACT.Silu, scale=s_in[:, 0, f:f + 1]).then_inc(silu_ready, 1)
                    need(act, fused_ready, n + 1)
                    need(act, down_ready, GB * (g - 1))
                    nc.scalar.copy(h_parts[:, g % 2, 0, f, :], fused[:, f % 2]).then_inc(h_first, 1)
                    act.wait_ge(h_rest_ready, n + 1)
                    nc.scalar.copy(h_parts[:, g % 2, 1, f, :], h_rest[:, f % 2]).then_inc(h_second, 1)
                    if g and f % 2 == 1 and f > 1:
                        norm.scalar(act, GB * (g - 1) + f // 2 - 1)
            for g in range(NG):
                group(g)
                if g:
                    norm.scalar(act, GB * g - 1)
            for j in range(GB):
                norm.scalar(act, GB * (NG - 1) + j)
            norm.done(act)

        @block.vector
        def _(dve):
            order = Order(dve, chain)
            dve.wait_ge(loaded, LOADED)
            nc.vector.tensor_copy(w_up[:, 1], w_in[:, 1].bitcast(I8)).then_inc(cast_done, 1)
            nc.vector.tensor_copy(w_down[:], wd_in[:].bitcast(I8)).then_inc(cast_done, 1)

            def finish(b):
                dve.wait_ge(down_ready, b + 1)
                nc.vector.tensor_tensor(y[:], down_ps[:, b % 2, 0:D], s_down[:], ALU.mult).then_inc(y_ready, 1)
                dve.wait_ge(y_ready, b + 1)
                norm.vector(dve, order, b, y[:])

            def group(g):
                dve.wait_ge(x_first, g + 1)
                nc.vector.tensor_tensor(x_rest[:], keep["xT"][:, :, bass.ts(g, GT)], x_parts[:, 0], ALU.subtract).then_inc(x_rest_ready, 1)
                dve.wait_ge(x_second, g + 1)
                nc.vector.tensor_tensor(x_parts[:, 2], x_rest[:], x_parts[:, 1], ALU.subtract).then_inc(x_split, 1)
                for f in range(FT):
                    n = FT * g + f
                    need(dve, silu_ready, n + 1)
                    need(dve, up_ready, n + 1)
                    need(dve, h_first, n - 1)
                    nc.vector.scalar_tensor_tensor(fused[:, f % 2], up_ps[:, f % 2], s_in[:, 1, f:f + 1], gate[:, f % 2],
                                                   ALU.mult, ALU.mult).then_inc(fused_ready, 1)
                    dve.wait_ge(h_first, n + 1)
                    nc.vector.tensor_tensor(h_rest[:, f % 2], fused[:, f % 2], h_parts[:, g % 2, 0, f, :], ALU.subtract).then_inc(h_rest_ready, 1)
                    dve.wait_ge(h_second, n + 1)
                    nc.vector.tensor_tensor(h_parts[:, g % 2, 2, f, :], h_rest[:, f % 2], h_parts[:, g % 2, 1, f, :], ALU.subtract).then_inc(h_split, 1)
                    if g and f % 2 == 1:
                        finish(GB * (g - 1) + f // 2)
            for g in range(NG):
                group(g)
            for j in range(GB):
                finish(GB * (NG - 1) + j)

        @block.tensor
        def _(pe):
            def up(g, f):
                n = FT * g + f
                for k, tile in enumerate((gate_ps, up_ps)):
                    need(pe, silu_ready if k == 0 else fused_ready, n - 1)
                    for c in range(DH):
                        for part in range(PARTS):
                            ins = nc.tensor.matmul(tile[:, f % 2], w_up[:, c, k, f * P:(f + 1) * P], x_parts[:, part, c, :],
                                                   start=(c == 0 and part == 0), stop=(c == DH - 1 and part == PARTS - 1))
                    ins.then_inc(up_ready if k else gate_ready, 1)

            def down(b):
                g, j = b // GB, b % GB
                pe.wait_ge(h_split, FT * (g + 1))
                need(pe, y_ready, b - 1)
                for f in range(FT):
                    for part in range(PARTS):
                        ins = nc.tensor.matmul(down_ps[:, b % 2, 0:D], h_parts[:, g % 2, part, f, j * T:(j + 1) * T], w_down[:, f, :],
                                               start=(f == 0 and part == 0), stop=(f == FT - 1 and part == PARTS - 1))
                ins.then_inc(down_ready, 1)

            pe.wait_ge(cast_done, 3)
            for g in range(NG):
                pe.wait_ge(x_first, g + 1)
                pe.wait_ge(x_split, g + 1)
                for f in range(FT):
                    up(g, f)
                    if g and f % 2 == 0:
                        down(GB * (g - 1) + f // 2)
                    if g and f % 2 == 1 and f > 1:
                        norm.tensor(pe, GB * (g - 1) + f // 2 - 1)
                if g:
                    norm.tensor(pe, GB * g - 1)
            for j in range(GB):
                down(GB * (NG - 1) + j)
            for j in range(GB):
                norm.tensor(pe, GB * (NG - 1) + j)


def batch_axis_attention(nc, keep, io):
    H = 16
    HD = D // H
    L = B
    MASKED = -10000.0
    with ExitStack() as ctx:
        sb = lambda name, shape: ctx.enter_context(nc.sbuf_tensor(f"bat_{name}", shape, F32))
        ps = lambda name, shape: ctx.enter_context(nc.psum_tensor(f"bat_{name}", shape, F32))
        sem = lambda name: new_semaphore(nc, keep, f"bat_{name}")
        w_qkv = sb("w_qkv", [P, DH, 3 * D])
        b_qkv = sb("b_qkv", [1, 3 * D])
        w_out = sb("w_out", [P, DH, D])
        b_out = sb("b_out", [1, D])
        ones = sb("ones", [1, T])
        x_feat = sb("x_feat", [P, 2, DH, T])
        q, k, v = sb("q", [T, L, D]), sb("k", [T, L, D]), sb("v", [T, L, D])
        later = sb("later", [T, L, D])
        prod = sb("prod", [T, L, D])
        s = sb("s", [T, L, H, L])
        row_max, row_sum = sb("row_max", [T, L * H]), sb("row_sum", [T, L * H])
        attended = sb("attended", [T, 2, D])
        masked_part = sb("masked_part", [T, D])
        causal_part = sb("causal_part", [T, D])
        attT = sb("attT", [P, 2, D])
        qkv_ps = ps("qkv_ps", [T, 2, 1024])
        attT_ps, out_ps, normT = ps("attT_ps", [P, D]), ps("out_ps", [T, D]), ps("normT", [P, D])
        loaded, ones_set, x_ready, qkv_ready, qkv_copied = sem("loaded"), sem("ones_set"), sem("x_ready"), sem("qkv_ready"), sem("qkv_copied")
        shifted, exp_ready, att_ready, attT_ready, attT_copied, out_ready = (
            sem("shifted"), sem("exp_ready"), sem("att_ready"), sem("attT_ready"), sem("attT_copied"), sem("out_ready"))
        chain = sem("chain")
        norm = Norm(nc, ctx, "ba_n", keep, normT)

        block = ctx.enter_context(nc.Block())

        @block.sync
        def _(sp):
            sp.dma_start(w_qkv[:], io["ba_w_qkv"].rearrange("(c p) o -> p c o", p=P)).then_inc(loaded, 16)
            sp.dma_start(b_qkv[:], io["ba_b_qkv"].unsqueeze(0)).then_inc(loaded, 16)
            sp.dma_start(w_out[:], io["ba_w_out"].rearrange("(c p) o -> p c o", p=P)).then_inc(loaded, 16)
            sp.dma_start(b_out[:], io["ba_b_out"].unsqueeze(0)).then_inc(loaded, 16)

        @block.gpsimd
        def _(pool):
            nc.gpsimd.memset(ones[:], 1.0).then_inc(ones_set, 1)

            def step(l, par, pair):
                need(pool, qkv_ready, l - 1)
                nc.gpsimd.tensor_copy(x_feat[:, par], keep["xT"][:, :, bass.ts(l, T)]).then_inc(x_ready, 1)
            each_sequence(pool, step)
            with pool.Fori(0, L) as l:
                norm.gpsimd(pool, l)

        @block.tensor
        def _(pe):
            pe.wait_ge(loaded, 4 * 16)
            pe.wait_ge(ones_set, 1)

            def project(l, par, pair):
                need(pe, x_ready, l + 1)
                need(pe, qkv_copied, l - 1)
                for lo, n in ((0, 512), (512, 256)):
                    for c in range(DH):
                        nc.tensor.matmul(qkv_ps[:, par, lo:lo + n], x_feat[:, par, c, :], w_qkv[:, c, lo:lo + n],
                                         start=(c == 0), stop=False)
                    ins = nc.tensor.matmul(qkv_ps[:, par, lo:lo + n], ones[:], b_qkv[:, lo:lo + n], start=False, stop=True)
                ins.then_inc(qkv_ready, 1)
            each_sequence(pe, project)

            def out(l, par, pair):
                need(pe, att_ready, l + 1)
                need(pe, attT_copied, l)
                for c in range(DH):
                    ins = nc.tensor.transpose(attT_ps[:, c * T:(c + 1) * T], attended[:, par, c * P:(c + 1) * P], keep["ident"][:])
                ins.then_inc(attT_ready, 1)
                need(pe, attT_copied, l + 1)
                need(pe, norm.var_ready, l)
                for c in range(DH):
                    nc.tensor.matmul(out_ps[:], attT[:, par, c * T:(c + 1) * T], w_out[:, c, :], start=(c == 0), stop=False)
                nc.tensor.matmul(out_ps[:], ones[:], b_out[:], start=False, stop=True).then_inc(out_ready, 1)
                if not first(l):
                    norm.tensor(pe, l - 1)
            each_sequence(pe, out)
            norm.tensor(pe, L - 1)

        @block.scalar
        def _(act):
            def copy_qkv(l, par, pair):
                need(act, qkv_ready, l + 1)
                nc.scalar.mul(q[:, l, :], qkv_ps[:, par, 0:D], HD ** -0.5)
                nc.scalar.copy(k[:, l, :], qkv_ps[:, par, D:2 * D])
                nc.scalar.copy(v[:, l, :], qkv_ps[:, par, 2 * D:3 * D]).then_inc(qkv_copied, 1)
            each_sequence(act, copy_qkv)
            act.wait_ge(shifted, 1)
            nc.scalar.activation(s[:], s[:], ACT.Exp).then_inc(exp_ready, 1)

            def copy_attended(l, par, pair):
                need(act, attT_ready, l + 1)
                need(act, out_ready, l - 1)
                nc.scalar.copy(attT[:, par, :], attT_ps[:]).then_inc(attT_copied, 1)
                if not first(l):
                    norm.scalar(act, l - 1)
            each_sequence(act, copy_attended)
            norm.scalar(act, L - 1)
            norm.done(act)

        @block.vector
        def _(dve):
            order = Order(dve, chain)
            order(nc.vector.memset(s[:], MASKED))
            for l in range(L):
                dve.wait_ge(qkv_copied, l + 1)
                order(nc.vector.tensor_tensor(prod[:, 0:l + 1, :], k[:, 0:l + 1, :],
                                              q[:, l, :].unsqueeze(1).to_broadcast([T, l + 1, D]), ALU.mult))
                order(nc.vector.tensor_reduce(s[:, l, :, 0:l + 1].rearrange("p h k -> p k h"),
                                              prod[:, 0:l + 1, :].rearrange("p k (h d) -> p k h d", h=H), AX_X, ALU.add))
            rows = s[:].rearrange("p l h k -> p (l h) k")
            order(nc.vector.tensor_reduce(row_max[:], rows, AX_X, ALU.max))
            nc.vector.tensor_tensor(rows, rows, row_max[:].unsqueeze(2).to_broadcast([T, L * H, L]), ALU.subtract).then_inc(shifted, 1)
            order(nc.vector.memset(later[:, L - 1, :], 0.0))
            for l in range(L - 2, -1, -1):
                order(nc.vector.tensor_tensor(later[:, l, :], later[:, l + 1, :], v[:, l + 1, :], ALU.add))
            dve.wait_ge(exp_ready, 1)
            order(nc.vector.tensor_reduce(row_sum[:], rows, AX_X, ALU.add))
            order(nc.vector.reciprocal(row_sum[:], row_sum[:]))
            order(nc.vector.tensor_tensor(rows, rows, row_sum[:].unsqueeze(2).to_broadcast([T, L * H, L]), ALU.mult))
            for l in range(L):
                v_h = v[:, 0:l + 1, :].rearrange("p k (h d) -> p k h d", h=H)
                p_h = s[:, l, :, 0:l + 1].rearrange("p h k -> p k h").unsqueeze(3).to_broadcast([T, l + 1, H, HD])
                order(nc.vector.tensor_tensor(prod[:, 0:l + 1, :].rearrange("p k (h d) -> p k h d", h=H), v_h, p_h, ALU.mult))
                order(nc.vector.tensor_tensor(masked_part[:].rearrange("p (h d) -> p h d", h=H),
                                              later[:, l, :].rearrange("p (h d) -> p h d", h=H),
                                              s[:, l, :, L - 1].unsqueeze(2).to_broadcast([T, H, HD]), ALU.mult))
                order(nc.vector.tensor_reduce(causal_part[:], prod[:, 0:l + 1, :].rearrange("p k f -> p f k"), AX_X, ALU.add))
                need(dve, attT_ready, l - 1)
                nc.vector.tensor_tensor(attended[:, l % 2], causal_part[:], masked_part[:], ALU.add).then_inc(att_ready, 1)
                dve.wait_ge(att_ready, l + 1)
                if l:
                    dve.wait_ge(out_ready, l)
                    norm.vector(dve, order, l - 1, out_ps[:])
            dve.wait_ge(out_ready, L)
            norm.vector(dve, order, L - 1, out_ps[:])


def latent_cross_attention(nc, keep, io):
    H, K, DC, DQ, R = 16, 128, 64, 192, 64
    QH = DQ // 2
    UH = 4
    U = H // UH
    PAIRS = H // 2
    HALF = DC // 2
    with ExitStack() as ctx:
        sb = lambda name, shape: ctx.enter_context(nc.sbuf_tensor(f"mla_{name}", shape, F32))
        sem = lambda name: new_semaphore(nc, keep, f"mla_{name}")
        to_keys = sb("to_keys", [P, DH, H, DC])
        to_out = sb("to_out", [P, PAIRS, D])
        keys = sb("keys", [P, B, 2, T])
        values = sb("values", [T, B, DC + 1])

        with ExitStack() as inner:
            sbi = lambda name, shape: inner.enter_context(nc.sbuf_tensor(f"mla_{name}", shape, F32))
            wq, kc_qT, qrT, krT = sbi("wq", [K, H, D]), sbi("kc_qT", [QH, 2, H, K]), sbi("qrT", [R, H, DQ]), sbi("krT", [R, H, DC])
            kc_kv, woT = sbi("kc_kv", [K, H, DC]), sbi("woT", [K, H, D])
            t1, t2 = sbi("t1", [QH, 2, H, DC]), sbi("t2", [K, H, DC])
            kv, cosines, sines = sbi("kv", [T, B, DC]), sbi("cosines", [T, DC]), sbi("sines", [T, DC])
            turned_kv, both = sbi("turned_kv", [T, B, DC]), sbi("both", [T, B, 2, DC])
            acc = inner.enter_context(nc.psum_tensor("mla_acc", [P, 2, 2048], F32))
            loaded, t1_ready, t1_copied, t2_ready, t2_copied = sem("loaded"), sem("t1_ready"), sem("t1_copied"), sem("t2_ready"), sem("t2_copied")
            keys_done, out_done, keys_copied, out_copied = sem("to_keys_ready"), sem("to_out_ready"), sem("to_keys_copied"), sem("to_out_copied")
            both_ready, keysT_ready, keysT_copied, prep_chain = sem("both_ready"), sem("keysT_ready"), sem("keysT_copied"), sem("prep_chain")
            block = inner.enter_context(nc.Block())

            @block.sync
            def _(sp):
                for dst, src in ((qrT, io["mla_qrT"]), (krT, io["mla_krT"]), (kc_qT, io["mla_kc_qT"]),
                                 (wq, io["mla_wq"].rearrange("(h k) i -> k h i", k=K)),
                                 (kv, io["ctx"].rearrange("b t d -> t b d")), (cosines, io["cosines"]), (sines, io["sines"]),
                                 (kc_kv, io["mla_kc_kv"].rearrange("h k d -> k h d")), (woT, io["mla_woT"].rearrange("(h k) n -> k h n", k=K))):
                    sp.dma_start(dst[:], src).then_inc(loaded, 16)

            LOADED = 9 * 16

            @block.tensor
            def _(pe):
                pe.wait_ge(loaded, LOADED)
                first_half, second_half = acc[:, 0], acc[:, 1]
                t1_ps = first_half.rearrange("p (c h d) -> p c h d", c=2, h=H)
                for h in range(H):
                    for c in range(2):
                        ins = nc.tensor.matmul(t1_ps[0:QH, c, h, :], qrT[:, h, c * QH:(c + 1) * QH], krT[:, h, :], start=True, stop=True)
                ins.then_inc(t1_ready, 1)
                pe.wait_ge(t1_copied, 1)
                t2_ps = second_half[:, 0:H * DC].rearrange("p (h d) -> p h d", h=H)
                for h in range(H):
                    for c in range(2):
                        ins = nc.tensor.matmul(t2_ps[:, h, :], kc_qT[:, c, h, :], t1[:, c, h, :], start=(c == 0), stop=(c == 1))
                ins.then_inc(t2_ready, 1)
                pe.wait_ge(t2_copied, 1)
                keys_ps = first_half.rearrange("p (c h d) -> p c h d", c=DH, h=H)
                for h in range(H):
                    for c in range(DH):
                        ins = nc.tensor.matmul(keys_ps[:, c, h, :], wq[:, h, c * P:(c + 1) * P], t2[:, h, :], start=True, stop=True)
                ins.then_inc(keys_done, 1)
                out_ps = second_half.rearrange("p (q n) -> p q n", q=PAIRS)
                for h in range(H):
                    r = (h % 2) * DC
                    ins = nc.tensor.matmul(out_ps[r:r + DC, h // 2, :], kc_kv[:, h, :], woT[:, h, :], start=True, stop=True)
                ins.then_inc(out_done, 1)
                pe.wait_ge(keys_copied, 1)
                pe.wait_ge(both_ready, 1)
                for b in range(B):
                    ins = nc.tensor.transpose(first_half[:, b * T:(b + 1) * T], both[:, b].rearrange("p k d -> p (k d)"), keep["ident"][:])
                ins.then_inc(keysT_ready, 1)

            @block.scalar
            def _(act):
                act.wait_ge(t1_ready, 1)
                nc.scalar.copy(t1[:].rearrange("p c h d -> p (c h d)"), acc[0:QH, 0]).then_inc(t1_copied, 1)
                act.wait_ge(t2_ready, 1)
                nc.scalar.copy(t2[:].rearrange("p h d -> p (h d)"), acc[:, 1, 0:H * DC]).then_inc(t2_copied, 1)
                act.wait_ge(keys_done, 1)
                nc.scalar.copy(to_keys[:].rearrange("p c h d -> p (c h d)"), acc[:, 0]).then_inc(keys_copied, 1)
                act.wait_ge(out_done, 1)
                nc.scalar.copy(to_out[:].rearrange("p q n -> p (q n)"), acc[:, 1]).then_inc(out_copied, 1)
                act.wait_ge(keysT_ready, 1)
                turned = acc[:, 0].rearrange("p (b t) -> p b t", b=B)
                for k in range(2):
                    rows = slice(k * DC, (k + 1) * DC)
                    nc.scalar.copy(keys[rows, :, k, :], turned[rows]).then_inc(keysT_copied, 1)

            @block.vector
            def _(dve):
                order = Order(dve, prep_chain)
                nc.vector.memset(keys[0:DC, :, 1, :], 0.0)
                nc.vector.memset(keys[DC:P, :, 0, :], 0.0)
                nc.vector.memset(values[:, :, DC:DC + 1], 1.0)
                dve.wait_ge(loaded, LOADED)
                per_b = lambda table, lo, hi: table[:, lo:hi].unsqueeze(1).to_broadcast([T, B, hi - lo])
                order(nc.vector.tensor_tensor(values[:, :, 0:DC], kv[:], per_b(cosines, 0, DC), ALU.mult))
                order(nc.vector.tensor_tensor(turned_kv[:, :, 0:HALF], kv[:, :, HALF:DC], per_b(sines, 0, HALF), ALU.mult))
                order(nc.vector.tensor_tensor(turned_kv[:, :, HALF:DC], kv[:, :, 0:HALF], per_b(sines, HALF, DC), ALU.mult))
                order(nc.vector.tensor_tensor(values[:, :, 0:DC], values[:, :, 0:DC], turned_kv[:], ALU.add))
                nc.vector.tensor_copy(both[:], values[:, :, 0:DC].unsqueeze(2).to_broadcast([T, B, 2, DC])).then_inc(both_ready, 1)

        ps = lambda name, shape: ctx.enter_context(nc.psum_tensor(f"mla_{name}", shape, F32))
        q_feat = sb("q_feat", [P, 2, PAIRS, T])
        NB = 4
        probs, probsT, row_max = sb("probs", [T, NB, UH, T]), sb("probsT", [T, NB, UH, T]), sb("row_max", [T, NB, UH])
        rsum = sb("rsum", [T, NB, UH])
        attended = sb("attended", [T, 2, H, DC])
        attT = sb("attT", [P, 2, PAIRS, T])
        scores, turned = ps("scores", [T, 2, UH, T]), ps("turned", [T, 2, UH, T])
        weighted = ps("weighted", [T, UH, DC + 1])
        shared = ps("shared", [P, PAIRS // 2, T])
        out_ps, normT = ps("out_ps", [T, D]), ps("normT", [P, D])
        q_done, q_copied, scores_ready, shifted, exp_ready = sem("q_done"), sem("q_copied"), sem("scores_ready"), sem("shifted"), sem("exp_ready")
        turn_ready, turn_copied, weigh_ready, scaled = sem("turn_ready"), sem("turn_copied"), sem("weigh_ready"), sem("scaled")
        attT_ready, attT_copied, out_ready, chain = sem("attT_ready"), sem("attT_copied"), sem("out_ready"), sem("chain")
        norm = Norm(nc, ctx, "mla_n", keep, normT)
        TURN_LAG, WEIGH_LAG = 1, 2
        block = ctx.enter_context(nc.Block())

        @block.gpsimd
        def _(pool):
            with pool.Fori(0, B) as b:
                norm.gpsimd(pool, b)

        @block.tensor
        def _(pe):
            def project(b, r):
                if r == 0:
                    need(pe, attT_copied, 2 * (b - 1))
                else:
                    need(pe, q_copied, 2 * b + 1)
                for k in range(PAIRS // 2):
                    pair = r * PAIRS // 2 + k
                    for c in range(DH):
                        ins = nc.tensor.matmul(shared[:, k, :], to_keys[:, c, 2 * pair:2 * pair + 2, :], keep["xT"][:, c, bass.ts(b, T)],
                                               start=(c == 0), stop=(c == DH - 1))
                ins.then_inc(q_done, 1)

            def score(b, par, u):
                if u % 2 == 0:
                    need(pe, q_copied, 2 * b + u // 2 + 1)
                need(pe, shifted, U * b + u - 1)
                for k in range(UH // 2):
                    ins = nc.tensor.matmul(scores[:, u % 2, 2 * k:2 * k + 2, :], q_feat[:, par, u * UH // 2 + k, :], keys[:, b, :, :],
                                           start=True, stop=True)
                ins.then_inc(scores_ready, 1)

            def turn(b, par, u):
                need(pe, exp_ready, U * b + u + 1)
                need(pe, turn_copied, U * b + u - 1)
                for h in range(UH):
                    ins = nc.tensor.transpose(turned[:, u % 2, h, :], probs[:, u % NB, h, :], keep["ident"][:])
                ins.then_inc(turn_ready, 1)

            def weigh(b, par, u):
                need(pe, turn_copied, U * b + u + 1)
                need(pe, scaled, U * b + u)
                for h in range(UH):
                    ins = nc.tensor.matmul(weighted[:, h, :], probsT[:, u % NB, h, :], values[:, b, :], start=True, stop=True)
                ins.then_inc(weigh_ready, 1)

            def turn_out(b, par, r):
                if r == 0:
                    need(pe, q_copied, 2 * b + 4)
                    need(pe, scaled, U * (b + 1))
                else:
                    need(pe, attT_copied, 2 * b + 1)
                for k in range(PAIRS // 2):
                    pair = r * PAIRS // 2 + k
                    ins = nc.tensor.transpose(shared[:, k, :], attended[:, par, 2 * pair:2 * pair + 2, :].rearrange("p h d -> p (h d)"),
                                              keep["ident"][:])
                ins.then_inc(attT_ready, 1)

            def project_out(b, par):
                need(pe, attT_copied, 2 * b + 2)
                need(pe, norm.var_ready, b)
                for k in range(PAIRS):
                    ins = nc.tensor.matmul(out_ps[:], attT[:, par, k, :], to_out[:, k, :], start=(k == 0), stop=(k == PAIRS - 1))
                ins.then_inc(out_ready, 1)

            def step(b, par, pair):
                rest = not first(b)
                project(b, 0)
                if rest:
                    turn(b - 1, 1 - par, U - 1)
                    weigh(b - 1, 1 - par, U - 2)
                project(b, 1)
                score(b, par, 0)
                if rest:
                    weigh(b - 1, 1 - par, U - 1)
                score(b, par, 1)
                turn(b, par, 0)
                if rest:
                    turn_out(b - 1, 1 - par, 0)
                score(b, par, 2)
                if rest:
                    turn_out(b - 1, 1 - par, 1)
                turn(b, par, 1)
                weigh(b, par, 0)
                score(b, par, 3)
                if rest:
                    project_out(b - 1, 1 - par)
                turn(b, par, 2)
                weigh(b, par, 1)
                if rest:
                    norm.tensor(pe, b - 1)
            each_sequence(pe, step)
            last = B - 1
            turn(last, 1, U - 1)
            weigh(last, 1, U - 2)
            weigh(last, 1, U - 1)
            pe.wait_ge(scaled, U * B)
            for r in range(2):
                if r:
                    pe.wait_ge(attT_copied, 2 * last + 1)
                for k in range(PAIRS // 2):
                    q = r * PAIRS // 2 + k
                    ins = nc.tensor.transpose(shared[:, k, :], attended[:, 1, 2 * q:2 * q + 2, :].rearrange("p h d -> p (h d)"), keep["ident"][:])
                ins.then_inc(attT_ready, 1)
            project_out(last, 1)
            norm.tensor(pe, last)

        @block.scalar
        def _(act):
            def copy_q(b, par, r):
                need(act, q_done, 2 * b + r + 1)
                need(act, scores_ready, U * (b - 1))
                nc.scalar.copy(q_feat[:, par, r * PAIRS // 2:(r + 1) * PAIRS // 2, :], shared[:]).then_inc(q_copied, 1)

            def exp(b, u):
                need(act, shifted, U * b + u + 1)
                nc.scalar.activation(probs[:, u % NB], probs[:, u % NB], ACT.Exp).then_inc(exp_ready, 1)

            def copy_turned(b, u):
                need(act, turn_ready, U * b + u + 1)
                need(act, weigh_ready, U * b + u + 1 - NB)
                nc.scalar.copy(probsT[:, u % NB], turned[:, u % 2]).then_inc(turn_copied, 1)

            def copy_out(b, par, r):
                need(act, attT_ready, 2 * b + r + 1)
                nc.scalar.copy(attT[:, par, r * PAIRS // 2:(r + 1) * PAIRS // 2, :], shared[:]).then_inc(attT_copied, 1)

            def step(b, par, pair):
                rest = not first(b)
                copy_q(b, par, 0)
                if rest:
                    copy_turned(b - 1, U - 1)
                copy_q(b, par, 1)
                exp(b, 0)
                exp(b, 1)
                copy_turned(b, 0)
                if rest:
                    copy_out(b - 1, 1 - par, 0)
                    copy_out(b - 1, 1 - par, 1)
                copy_turned(b, 1)
                exp(b, 2)
                exp(b, 3)
                copy_turned(b, 2)
                if rest:
                    norm.scalar(act, b - 1)
            each_sequence(act, step)
            copy_turned(B - 1, U - 1)
            copy_out(B - 1, 1, 0)
            copy_out(B - 1, 1, 1)
            norm.scalar(act, B - 1)
            norm.done(act)

        @block.vector
        def _(dve):
            order = Order(dve, chain)

            def shift(b, u):
                need(dve, scores_ready, U * b + u + 1)
                order(nc.vector.tensor_reduce(row_max[:, u % NB], scores[:, u % 2], AX_X, ALU.max))
                need(dve, turn_ready, U * b + u + 1 - NB)
                nc.vector.tensor_tensor(probs[:, u % NB], scores[:, u % 2], row_max[:, u % NB].unsqueeze(2).to_broadcast([T, UH, T]),
                                        ALU.subtract).then_inc(shifted, 1)

            def scale(b, par, u):
                need(dve, weigh_ready, U * b + u + 1)
                order(nc.vector.reciprocal(rsum[:, u % NB], weighted[:, :, DC]))
                nc.vector.tensor_tensor(attended[:, par, u * UH:(u + 1) * UH, :], weighted[:, :, 0:DC],
                                        rsum[:, u % NB].unsqueeze(2).to_broadcast([T, UH, DC]), ALU.mult).then_inc(scaled, 1)

            def step(b, par, pair):
                rest = not first(b)
                if rest:
                    scale(b - 1, 1 - par, U - 2)
                shift(b, 0)
                if rest:
                    scale(b - 1, 1 - par, U - 1)
                shift(b, 1)
                shift(b, 2)
                scale(b, par, 0)
                shift(b, 3)
                if rest:
                    need(dve, out_ready, b)
                    norm.vector(dve, order, b - 1, out_ps[:])
                scale(b, par, 1)
            each_sequence(dve, step, order, per=2 * (2 * U + norm.CHAIN - 1))
            scale(B - 1, 1, U - 2)
            scale(B - 1, 1, U - 1)
            dve.wait_ge(out_ready, B)
            norm.vector(dve, order, B - 1, out_ps[:])



def mixture_of_experts(nc, keep, io, out):
    E, G, TOPK, TOPG, CAP, F, SCALE = 64, 8, 6, 4, 48, 96, 2.5
    EG = E // G
    N = B * T
    BIG = 1e30
    W = D + E
    PAIRS = E // 2
    SLOTS = 64
    ROUNDS = CAP // 8
    with ExitStack() as ctx:
        sb = lambda name, shape, dt=F32: ctx.enter_context(nc.sbuf_tensor(f"moe_{name}", shape, dt))
        sem = lambda name: new_semaphore(nc, keep, f"moe_{name}")
        table = nc.dram_tensor("moe_table", [N + P, W], F32, kind="Internal").ap()
        sums = [nc.dram_tensor(f"moe_sums_{k}", [N + P, D], F32, kind="Internal").ap() for k in range(2)]
        rows = sb("rows", [P, PAIRS], U32)
        rows_of = sb("rows_of", [SLOTS, E], U32)

        with ExitStack() as inner:
            sbi = lambda name, shape, dt=F32: inner.enter_context(nc.sbuf_tensor(f"moe_{name}", shape, dt))
            psi = lambda name, shape: inner.enter_context(nc.psum_tensor(f"moe_{name}", shape, F32))
            w_route, bias = sbi("w_route", [P, DH, E]), sbi("bias", [P, E])
            ws_gu, ws_down = sbi("ws_gu", [P, DH, 2 * F]), sbi("ws_down", [F, D])
            not_first, lower = sbi("not_first", [P, B * E]), sbi("lower", [P, G * G])
            countdown, slot_no = sbi("countdown", [P, B]), sbi("slot_no", [P, 1])
            zeros = sbi("zeros", [P, W])
            score, biased, work, chosen = sbi("score", [T, B, E]), sbi("biased", [T, B, E]), sbi("work", [T, B, E]), sbi("chosen", [T, B, E])
            equal, prefix, pick = sbi("equal", [T, B, E]), sbi("prefix", [T, B * E]), sbi("pick", [T, B, E])
            best, count, second = sbi("best", [T, B * G]), sbi("count", [T, B * G]), sbi("second", [T, B * G])
            group_score, group_in = sbi("group_score", [T, B * G]), sbi("group_in", [T, B * G])
            ahead, tied = sbi("ahead", [T, B, G, G]), sbi("tied", [T, B, G, G])
            top8, above, total = sbi("top8", [T, B, 8]), sbi("above", [T, B]), sbi("total", [T, B])
            weights = sbi("weights", [T, B, E])
            order_key = sbi("order_key", [T, B, E])
            left = sbi("left", [P, 2, N // 2])
            top, merged, merged_left = sbi("top", [P, CAP]), sbi("merged", [E, 2, CAP]), sbi("merged_left", [E, 2, 2 * CAP])
            twice = sbi("twice", [E, P])
            row_f, empty = sbi("row_f", [P, E]), sbi("empty", [P, E])
            gate, hT = sbi("gate", [F, 2, 512]), sbi("hT", [F, N])
            logits = psi("logits", [T, B, E])
            keysT = psi("keysT", [P, N // 2])
            shared_gate, shared_up = psi("shared_gate", [P, 512]), psi("shared_up", [P, 512])
            shared_out = psi("shared_out", [T, 2, 512])
            loaded, zero_set, logits_ready, score_ready = sem("loaded"), sem("zero_set"), sem("logits_ready"), sem("score_ready")
            key_ready, keyT_ready, twice_ready, twiceT_ready = sem("key_ready"), sem("keyT_ready"), sem("twice_ready"), sem("twiceT_ready")
            weights_ready, stored, tokens_stored, rows_ready = sem("weights_ready"), sem("stored"), sem("tokens_stored"), sem("rows_ready")
            gate_ps_ready, silu_done, h_done, down_done, added = sem("gate_ps_ready"), sem("silu_done"), sem("h_done"), sem("down_done"), sem("added")
            chain = sem("route_chain")
            block = inner.enter_context(nc.Block())

            @block.sync
            def _(sp):
                for dst, src in ((w_route, io["moe_w_route"].rearrange("(c p) e -> p c e", p=P)), (bias, io["moe_bias"].unsqueeze(0).to_broadcast([P, E])),
                                 (not_first, io["moe_not_first"].unsqueeze(0).to_broadcast([P, B * E])),
                                 (lower, io["moe_lower"].unsqueeze(0).to_broadcast([P, G * G])),
                                 (countdown, io["moe_countdown"]), (slot_no, io["moe_slot_no"]),
                                 (ws_gu, io["moe_ws_gu"].rearrange("(c p) f -> p c f", p=P)), (ws_down, io["moe_ws_down"])):
                    sp.dma_start(dst[:], src).then_inc(loaded, 16)
                sp.dma_start(table[0:N, 0:D].rearrange("(b t) d -> t b d", t=T), keep["x_tok"][:]).then_inc(tokens_stored, 16)
                sp.wait_ge(zero_set, 1)
                sp.dma_start(table[N:N + P, :], zeros[:]).then_inc(stored, 16)
                for k in range(2):
                    sp.dma_start(sums[k].rearrange("(b t) d -> t b d", t=T), zeros[:, 0:D].unsqueeze(1).to_broadcast([P, B + 1, D])).then_inc(stored, 16)
                sp.wait_ge(weights_ready, 1)
                sp.dma_start(table[0:N, D:W].rearrange("(b t) e -> t b e", t=T), weights[:]).then_inc(stored, 16)
                sp.wait_ge(stored, 4 * 16)
                sp.wait_ge(tokens_stored, 16)

            LOADED = 8 * 16

            @block.tensor
            def _(pe):
                pe.wait_ge(loaded, LOADED)
                for b in range(B):
                    for c in range(DH):
                        ins = nc.tensor.matmul(logits[:, b, :], keep["xT"][:, c, b * T:(b + 1) * T], w_route[:, c, :], start=(c == 0), stop=(c == DH - 1))
                ins.then_inc(logits_ready, 1)
                pe.wait_ge(key_ready, 1)
                for k in range(B // 2):
                    ins = nc.tensor.transpose(keysT[:, k * T:(k + 1) * T], order_key[:, 2 * k:2 * k + 2, :].rearrange("p b e -> p (b e)"), keep["ident"][:])
                ins.then_inc(keyT_ready, 1)
                pe.wait_ge(twice_ready, 1)
                nc.tensor.transpose(logits[:, 0, :], twice[:], keep["ident"][0:E, 0:E]).then_inc(twiceT_ready, 1)
                for g in range(4):
                    if g:
                        pe.wait_ge(h_done, g)
                    for k, tile in enumerate((shared_gate, shared_up)):
                        for c in range(DH):
                            ins = nc.tensor.matmul(tile[0:F, :], ws_gu[:, c, k * F:(k + 1) * F], keep["xT"][:, c, g * 512:(g + 1) * 512],
                                                   start=(c == 0), stop=(c == DH - 1))
                    ins.then_inc(gate_ps_ready, 1)
                for b in range(B):
                    pe.wait_ge(h_done, b // 4 + 1)
                    if b > 1:
                        pe.wait_ge(added, b - 1)
                    nc.tensor.matmul(shared_out[:, b % 2, 0:D], hT[:, b * T:(b + 1) * T], ws_down[:], start=True, stop=True).then_inc(down_done, 1)

            @block.scalar
            def _(act):
                act.wait_ge(logits_ready, 1)
                nc.scalar.activation(score[:], logits[:], ACT.Sigmoid).then_inc(score_ready, 1)
                for g in range(4):
                    act.wait_ge(gate_ps_ready, g + 1)
                    if g > 1:
                        act.wait_ge(h_done, g - 1)
                    nc.scalar.activation(gate[:, g % 2], shared_gate[0:F, :], ACT.Silu).then_inc(silu_done, 1)

            @block.vector
            def _(dve):
                order = Order(dve, chain)
                tt, ts, tr = nc.vector.tensor_tensor, nc.vector.tensor_scalar, nc.vector.tensor_reduce
                stt = nc.vector.scalar_tensor_tensor
                nc.vector.memset(zeros[:], 0.0).then_inc(zero_set, 1)
                dve.wait_ge(loaded, LOADED)
                dve.wait_ge(score_ready, 1)
                by_group = lambda t: t[:].rearrange("p b (g e) -> p (b g) e", g=G)
                wide = lambda t, n: t[:].unsqueeze(2).to_broadcast([T, t.shape[1], n])
                order(tt(biased[:], score[:], bias[:].unsqueeze(1).to_broadcast([T, B, E]), ALU.add))
                order(tr(best[:], by_group(biased), AX_X, ALU.max))
                order(tt(by_group(equal), by_group(biased), wide(best, EG), ALU.is_equal))
                order(tr(count[:], by_group(equal), AX_X, ALU.add))
                order(stt(work[:].rearrange("p b e -> p (b e)"), equal[:].rearrange("p b e -> p (b e)"), -BIG, biased[:].rearrange("p b e -> p (b e)"), ALU.mult, ALU.add))
                order(tr(second[:], by_group(work), AX_X, ALU.max))
                order(ts(count[:], count[:], 2.0, -BIG, ALU.is_lt, ALU.mult))
                order(tt(count[:], count[:], best[:], ALU.add))
                order(tt(second[:], second[:], count[:], ALU.max))
                order(tt(group_score[:], best[:], second[:], ALU.add))
                gs = group_score[:].rearrange("p (b g) -> p b g", g=G)
                mine, others = gs.unsqueeze(3).to_broadcast([T, B, G, G]), gs.unsqueeze(2).to_broadcast([T, B, G, G])
                order(tt(ahead[:], others, mine, ALU.is_gt))
                order(tt(tied[:], others, mine, ALU.is_equal))
                order(tt(tied[:].rearrange("p b g h -> p b (g h)"), tied[:].rearrange("p b g h -> p b (g h)"),
                         lower[:].unsqueeze(1).to_broadcast([T, B, G * G]), ALU.mult))
                order(tt(ahead[:], ahead[:], tied[:], ALU.add))
                order(tr(group_in[:], ahead[:].rearrange("p b g h -> p (b g) h"), AX_X, ALU.add))
                order(ts(group_in[:], group_in[:], float(TOPG), None, ALU.is_lt))
                order(tt(by_group(work), by_group(biased), wide(group_in, EG), ALU.mult))
                order(ts(group_in[:], group_in[:], 1.0, BIG, ALU.subtract, ALU.mult))
                order(tt(by_group(work), by_group(work), wide(group_in, EG), ALU.add))
                for b in range(B):
                    ins = nc.vector.max(top8[:, b, :], work[:, b, :])
                order(ins)
                sixth = top8[:, :, TOPK - 1].unsqueeze(2).to_broadcast([T, B, E])
                order(tt(pick[:], work[:], sixth, ALU.is_gt))
                order(tt(equal[:], work[:], sixth, ALU.is_equal))
                order(tr(above[:], pick[:], AX_X, ALU.add))
                order(nc.vector.tensor_tensor_scan(prefix[:], not_first[:], equal[:].rearrange("p b e -> p (b e)"), 0.0, ALU.mult, ALU.add))
                pre = prefix[:].rearrange("p (b e) -> p b e", b=B)
                order(tt(pre, pre, wide(above, E), ALU.add))
                order(stt(equal[:].rearrange("p b e -> p (b e)"), prefix[:], float(TOPK), equal[:].rearrange("p b e -> p (b e)"), ALU.is_le, ALU.mult))
                order(tt(chosen[:], pick[:], equal[:], ALU.add))
                tt(order_key[:], chosen[:], wide(countdown, E), ALU.mult).then_inc(key_ready, 1)
                order(tt(work[:], score[:], chosen[:], ALU.mult))
                order(tr(total[:], work[:], AX_X, ALU.add))
                order(nc.vector.reciprocal(total[:], total[:]))
                order(ts(total[:], total[:], SCALE, None, ALU.mult))
                tt(weights[:], work[:], wide(total, E), ALU.mult).then_inc(weights_ready, 1)
                dve.wait_ge(keyT_ready, 1)
                src = keysT[:]
                for r in range(ROUNDS):
                    order(nc.vector.max(top[:, 8 * r:8 * r + 8], src))
                    if r < ROUNDS - 1:
                        order(nc.vector.match_replace(left[:, r % 2, :], top[:, 8 * r:8 * r + 8], src, 0.0))
                        src = left[:, r % 2, :]
                order(nc.vector.tensor_copy(merged[:, 0, :], top[0:E, :]))
                order(nc.vector.tensor_copy(merged[:, 1, :], top[E:P, :]))
                order(nc.vector.memset(twice[:], 0.0))
                src = merged[:].rearrange("p k s -> p (k s)")
                for r in range(ROUNDS):
                    order(nc.vector.max(twice[:, 8 * r:8 * r + 8], src))
                    if r < ROUNDS - 1:
                        order(nc.vector.match_replace(merged_left[:, r % 2, :], twice[:, 8 * r:8 * r + 8], src, 0.0))
                        src = merged_left[:, r % 2, :]
                nc.vector.tensor_copy(twice[:, SLOTS:SLOTS + CAP], twice[:, 0:CAP]).then_inc(twice_ready, 1)
                dve.wait_ge(twiceT_ready, 1)
                order(ts(row_f[:], logits[:, 0, :], -1.0, float(N), ALU.mult, ALU.add))
                order(ts(empty[:], logits[:, 0, :], 0.0, slot_no[:], ALU.is_equal, ALU.mult))
                order(tt(row_f[:], row_f[:], empty[:], ALU.add))
                turned = row_f[:].rearrange("p (q k) -> p q k", k=2)
                nc.vector.tensor_copy(rows[0:SLOTS, :], turned[0:SLOTS, :, 0])
                nc.vector.tensor_copy(rows[SLOTS:P, :], turned[SLOTS:P, :, 1])
                nc.vector.tensor_copy(rows_of[:], row_f[0:SLOTS, :]).then_inc(rows_ready, 1)
                for g in range(4):
                    dve.wait_ge(silu_done, g + 1)
                    tt(hT[:, g * 512:(g + 1) * 512], shared_up[0:F, :], gate[:, g % 2], ALU.mult).then_inc(h_done, 1)
                dve.wait_ge(tokens_stored, 16)
                for b in range(B):
                    dve.wait_ge(down_done, b + 1)
                    tt(keep["x_tok"][:, b, :], shared_out[:, b % 2, 0:D], keep["x_tok"][:, b, :], ALU.add).then_inc(added, 1)

        with ExitStack() as inner:
            sbi = lambda name, shape, dt=F32: inner.enter_context(nc.sbuf_tensor(f"moe_{name}", shape, dt))
            psi = lambda name, shape: inner.enter_context(nc.psum_tensor(f"moe_{name}", shape, F32))
            NW = 8
            w_gu, w_dn = sbi("w_gu", [P, NW, 2, DH, 2 * F]), sbi("w_dn", [F, NW, 2, D])
            gathered = sbi("gathered", [P, PAIRS, W])
            xgT = sbi("xgT", [P, 2, DH, P])
            gate2, h2, hT2 = sbi("gate2", [P, 2, F]), sbi("h2", [P, 2, F]), sbi("hT2", [F, 2, P])
            y2 = sbi("y2", [SLOTS, 4, 2, D])
            xgT_ps, gu_ps, hT_ps = psi("xgT_ps", [P, 2, 512]), psi("gu_ps", [P, 2, 512]), psi("hT_ps", [P, 2, 512])
            y_ps = psi("y_ps", [P, 2, 2, D])
            w_loaded = [sem(f"w_loaded{k}") for k in range(NW)]
            x_gathered = [sem(f"x_gathered{k}") for k in range(4)]
            xT_ready, xT_copied, gu_ready, silu2_ready, h2_ready = sem("xT_ready"), sem("xT_copied"), sem("gu_ready"), sem("silu2_ready"), sem("h2_ready")
            hT_ready, hT_copied, y_ready, y_copied = sem("hT_ready"), sem("hT_copied"), sem("y_ready"), sem("y_copied")
            scattered = [sem("scattered0"), sem("scattered1")]
            block = inner.enter_context(nc.Block())

            @block.sync
            def _(sp):
                for q in range(PAIRS):
                    if q >= NW:
                        sp.wait_ge(y_ready, q - NW + 1)
                    sp.dma_start(w_gu[:, q % NW], io["moe_w_gu"][q]).then_inc(w_loaded[q % NW], 16)
                    sp.dma_start(w_dn[:, q % NW], io["moe_w_down"][q]).then_inc(w_loaded[q % NW], 16)

            @block.gpsimd
            def _(pool):
                AHEAD = 4
                for q in range(PAIRS + AHEAD):
                    if q < PAIRS:
                        if q >= 4:
                            pool.wait_ge(x_gathered[q % 4], 16 * (q // 4))
                        nc.gpsimd.indirect_dma_start(gathered[:, q, :], None, table, bass.IndirectOffsetOnAxis(ap=rows[:, q:q + 1], axis=0)).then_inc(x_gathered[q % 4], 16)
                    if q >= AHEAD:
                        s = q - AHEAD
                        pool.wait_ge(y_copied, s + 1)
                        for k in range(2):
                            if s:
                                pool.wait_ge(scattered[k], 16 * s)
                            nc.gpsimd.indirect_dma_start(sums[k], bass.IndirectOffsetOnAxis(ap=rows_of[0:CAP, 2 * s + k:2 * s + k + 1], axis=0),
                                                         y2[0:CAP, s % 4, k, :], None, compute_op=ALU.add).then_inc(scattered[k], 16)
                for k in range(2):
                    pool.wait_ge(scattered[k], 16 * PAIRS)

            @block.tensor
            def _(pe):
                def first_stage(q):
                    pe.wait_ge(x_gathered[q % 4], 16 * (q // 4 + 1))
                    if q > 1:
                        pe.wait_ge(xT_copied, q - 1)
                    for c in range(DH):
                        ins = nc.tensor.transpose(xgT_ps[:, q % 2, c * P:(c + 1) * P], gathered[:, q, c * P:(c + 1) * P], keep["ident"][:])
                    ins.then_inc(xT_ready, 1)

                def gate_up(q):
                    pe.wait_ge(xT_copied, q + 1)
                    pe.wait_ge(w_loaded[q % NW], 32 * (q // NW + 1))
                    if q > 1:
                        pe.wait_ge(h2_ready, q - 1)
                    for k in range(2):
                        lo = k * SLOTS
                        for c in range(DH):
                            ins = nc.tensor.matmul(gu_ps[lo:lo + SLOTS, q % 2, 0:2 * F], xgT[:, q % 2, c, lo:lo + SLOTS], w_gu[:, q % NW, k, c, :],
                                                   start=(c == 0), stop=(c == DH - 1))
                    ins.then_inc(gu_ready, 1)

                def turn_h(q):
                    pe.wait_ge(h2_ready, q + 1)
                    if q > 1:
                        pe.wait_ge(hT_copied, q - 1)
                    nc.tensor.transpose(hT_ps[0:F, q % 2, 0:P], h2[:, q % 2, :], keep["ident"][:]).then_inc(hT_ready, 1)

                def down(q):
                    pe.wait_ge(hT_copied, q + 1)
                    if q > 1:
                        pe.wait_ge(y_copied, q - 1)
                    for k in range(2):
                        ins = nc.tensor.matmul(y_ps[0:CAP, q % 2, k, :], hT2[:, q % 2, k * SLOTS:k * SLOTS + CAP], w_dn[:, q % NW, k, :], start=True, stop=True)
                    ins.then_inc(y_ready, 1)

                for q in range(PAIRS + 3):
                    if q < PAIRS:
                        first_stage(q)
                    if 1 <= q <= PAIRS:
                        gate_up(q - 1)
                    if 2 <= q <= PAIRS + 1:
                        turn_h(q - 2)
                    if q >= 3:
                        down(q - 3)

            @block.scalar
            def _(act):
                for q in range(PAIRS + 2):
                    if q < PAIRS:
                        act.wait_ge(xT_ready, q + 1)
                        if q > 1:
                            act.wait_ge(gu_ready, q - 1)
                        nc.scalar.copy(xgT[:, q % 2], xgT_ps[:, q % 2, 0:D].rearrange("p (c s) -> p c s", c=DH)).then_inc(xT_copied, 1)
                    if 1 <= q <= PAIRS:
                        s = q - 1
                        act.wait_ge(gu_ready, s + 1)
                        if s > 1:
                            act.wait_ge(h2_ready, s - 1)
                        nc.scalar.activation(gate2[:, s % 2], gu_ps[:, s % 2, 0:F], ACT.Silu).then_inc(silu2_ready, 1)
                    if q >= 2:
                        s = q - 2
                        act.wait_ge(hT_ready, s + 1)
                        if s > 1:
                            act.wait_ge(y_ready, s - 1)
                        nc.scalar.copy(hT2[:, s % 2], hT_ps[0:F, s % 2, 0:P]).then_inc(hT_copied, 1)

            @block.vector
            def _(dve):
                for q in range(PAIRS + 1):
                    if q < PAIRS:
                        dve.wait_ge(silu2_ready, q + 1)
                        if q > 1:
                            dve.wait_ge(hT_ready, q - 1)
                        for k in range(2):
                            lo = k * SLOTS
                            e = D + 2 * q + k
                            ins = nc.vector.scalar_tensor_tensor(h2[lo:lo + SLOTS, q % 2, :], gu_ps[lo:lo + SLOTS, q % 2, F:2 * F],
                                                                 gathered[lo:lo + SLOTS, q, e:e + 1], gate2[lo:lo + SLOTS, q % 2, :], ALU.mult, ALU.mult)
                        ins.then_inc(h2_ready, 1)
                    if q >= 1:
                        s = q - 1
                        dve.wait_ge(y_ready, s + 1)
                        if s >= 4:
                            for k in range(2):
                                dve.wait_ge(scattered[k], 16 * (s - 3))
                        nc.vector.tensor_copy(y2[0:CAP, s % 4], y_ps[0:CAP, s % 2]).then_inc(y_copied, 1)

        with ExitStack() as inner:
            sbi = lambda name, shape, dt=F32: inner.enter_context(nc.sbuf_tensor(f"moe_{name}", shape, dt))
            part = sbi("part", [T, 2, B, D])
            stats, mean_var, var_eps, rstd = sbi("stats", [T, B, 6]), sbi("mean_var", [T, B, 2]), sbi("var_eps", [T, B]), sbi("rstd", [T, B])
            half = sbi("half", [T, B])
            parts_loaded, var_ready, rstd_ready, normed, written, half_set = sem("parts_loaded"), sem("var_ready"), sem("rstd_ready"), sem("normed"), sem("written"), sem("half_set")
            chain = sem("last_chain")
            block = inner.enter_context(nc.Block())
            QB = B // 4

            @block.sync
            def _(sp):
                for k in range(2):
                    sp.dma_start(part[:, k], sums[k][0:N].rearrange("(b t) d -> t b d", t=T)).then_inc(parts_loaded, 16)
                for g in range(4):
                    sp.wait_ge(normed, g + 1)
                    sp.dma_start(out[g * QB:(g + 1) * QB].rearrange("b t d -> t b d"), keep["x_tok"][:, g * QB:(g + 1) * QB, :]).then_inc(written, 16)
                sp.wait_ge(written, 4 * 16)

            @block.gpsimd
            def _(pool):
                nc.gpsimd.memset(half[:], -0.5).then_inc(half_set, 1)
                pool.wait_ge(half_set, 1)
                pool.wait_ge(var_ready, 1)
                nc.gpsimd.tensor_tensor(rstd[:], var_eps[:], half[:], ALU.pow).then_inc(rstd_ready, 1)

            @block.vector
            def _(dve):
                order = Order(dve, chain)
                x = keep["x_tok"]
                for k in range(2):
                    dve.wait_ge(parts_loaded, 32)
                    order(nc.vector.tensor_tensor(x[:], x[:], part[:, k], ALU.add))
                for b in range(B):
                    ins = nc.vector.bn_stats(stats[:, b, :], x[:, b, :])
                order(ins)
                for b in range(B):
                    ins = nc.vector.bn_aggr(mean_var[:, b, :], stats[:, b, :])
                order(ins)
                nc.vector.tensor_scalar(var_eps[:], mean_var[:, :, 1], LN_EPS, None, ALU.add).then_inc(var_ready, 1)
                dve.wait_ge(rstd_ready, 1)
                for b in range(B):
                    ins = nc.vector.tensor_scalar(x[:, b, :], x[:, b, :], mean_var[:, b, 0:1], rstd[:, b:b + 1], ALU.subtract, ALU.mult)
                    if b % QB == QB - 1:
                        ins.then_inc(normed, 1)


def test_time_training(nc, keep, io):
    H, HD, C = 32, 8, 16
    K1 = HD + 1
    NC = T // C
    NG = 4
    HH = H // DH
    EPS = 1e-6
    with ExitStack() as ctx:
        sb = lambda name, shape: ctx.enter_context(nc.sbuf_tensor(f"ttt_{name}", shape, F32))
        sem = lambda name: new_semaphore(nc, keep, f"ttt_{name}")
        k_dram = nc.dram_tensor("ttt_k_by_head", [B, H * HD, T], F32, kind="Internal").ap()
        c_dram = nc.dram_tensor("ttt_c_by_head", [B, H * HD, T], F32, kind="Internal").ap()
        q_feat, k_feat = sb("q_feat", [P, DH, B * T]), sb("k_feat", [P, DH, B * T])
        tok = sb("tok", [P, C])
        g_tok = sb("g_tok", [T, B, H, HD])

        with ExitStack() as seq:
            sbq = lambda name, shape: seq.enter_context(nc.sbuf_tensor(f"ttt_{name}", shape, F32))
            k_seq, c_seq, lr_seq = sbq("k_seq", [P, NG, K1, T]), sbq("c_seq", [P, NG, HD, T]), sbq("lr_seq", [P, NG, T])

            with ExitStack() as inner:
                sbi = lambda name, shape: inner.enter_context(nc.sbuf_tensor(f"ttt_{name}", shape, F32))
                w_qkv, w_lr = sbi("w_qkv", [P, DH, 3 * D]), sbi("w_lr", [P, DH, H])
                lr_bias, gamma, beta = sbi("lr_bias", [H, 1]), sbi("gamma", [P, DH]), sbi("beta", [P, DH])
                gamma_beta = sbi("gamma_beta", [P, DH])
                c_feat, lr = sbi("c_feat", [P, DH, B * T]), sbi("lr", [H, B * T])
                acc = inner.enter_context(nc.psum_tensor("ttt_acc", [P, 7, 512], F32))
                loaded, w_ready, proj_ready, proj_copied, lr_done = sem("loaded"), sem("w_ready"), sem("proj_ready"), sem("proj_copied"), sem("lr_done")
                k_stored, c_stored, seq_loaded = sem("k_stored"), sem("c_stored"), sem("seq_loaded")
                block = inner.enter_context(nc.Block())

                @block.sync
                def _(sp):
                    for dst, src in ((w_qkv[:], io["ttt_w_qkv"].rearrange("(c p) o -> p c o", p=P)), (w_lr[:], io["ttt_w_lr"].rearrange("(c p) h -> p c h", p=P)),
                                     (lr_bias[:], io["ttt_lr_bias"]), (gamma[:], io["ttt_gamma_feat"]), (beta[:], io["ttt_beta_feat"])):
                        sp.dma_start(dst, src).then_inc(loaded, 16)
                    for g in range(NG):
                        sp.wait_ge(proj_copied, g + 1)
                        for src, dram, stored in ((k_feat, k_dram, k_stored), (c_feat, c_dram, c_stored)):
                            for c in range(DH):
                                sp.dma_start(dram[g * NG:(g + 1) * NG, c * P:(c + 1) * P, :].rearrange("b p t -> p b t"),
                                             src[:, c, g * 512:(g + 1) * 512].rearrange("p (b t) -> p b t", t=T)).then_inc(stored, 16)
                        sp.wait_ge(k_stored, 32 * (g + 1))
                        sp.wait_ge(c_stored, 32 * (g + 1))
                        sp.dma_start(k_seq[:, g, 0:HD, :].rearrange("p d t -> p (d t)"),
                                     k_dram[g * NG:(g + 1) * NG].rearrange("b (h d) t -> (b h) (d t)", d=HD)).then_inc(seq_loaded, 16)
                        sp.dma_start(c_seq[:, g].rearrange("p d t -> p (d t)"),
                                     c_dram[g * NG:(g + 1) * NG].rearrange("b (h d) t -> (b h) (d t)", d=HD)).then_inc(seq_loaded, 16)
                    for b in range(NG):
                        sp.dma_start(lr_seq[b * H:(b + 1) * H, :, :], lr[:].rearrange("h (g b t) -> h g b t", b=NG, t=T)[:, :, b, :]).then_inc(seq_loaded, 16)
                    sp.wait_ge(seq_loaded, 16 * 12)

                @block.tensor
                def _(pe):
                    pe.wait_ge(w_ready, 1)
                    for g in range(NG):
                        need(pe, proj_copied, g)
                        need(pe, lr_done, g)
                        rhs = lambda c: keep["xT"][:, c, g * 512:(g + 1) * 512]
                        for n in range(6):
                            for c in range(DH):
                                nc.tensor.matmul(acc[:, n, :], w_qkv[:, c, n * P:(n + 1) * P], rhs(c), start=(c == 0), stop=(c == DH - 1))
                        for c in range(DH):
                            ins = nc.tensor.matmul(acc[0:H, 6, :], w_lr[:, c, :], rhs(c), start=(c == 0), stop=(c == DH - 1))
                        ins.then_inc(proj_ready, 1)

                @block.scalar
                def _(act):
                    act.wait_ge(w_ready, 1)
                    for g in range(NG):
                        act.wait_ge(proj_ready, g + 1)
                        cols = slice(g * 512, (g + 1) * 512)
                        nc.scalar.activation(lr[:, cols], acc[0:H, 6, :], ACT.Sigmoid, bias=lr_bias[:]).then_inc(lr_done, 1)
                        for c in range(DH):
                            nc.scalar.copy(k_feat[:, c, cols], acc[:, 2 + c, :])
                            nc.scalar.activation(c_feat[:, c, cols], acc[:, 4 + c, :], ACT.Identity, bias=gamma_beta[:, c:c + 1], scale=gamma[:, c:c + 1])
                            ins = nc.scalar.copy(q_feat[:, c, cols], acc[:, c, :])
                        ins.then_inc(proj_copied, 1)

                @block.vector
                def _(dve):
                    nc.vector.memset(k_seq[:, :, HD, :], 1.0)
                    dve.wait_ge(loaded, 16 * 5)
                    nc.vector.tensor_tensor(gamma_beta[:], gamma[:], beta[:], ALU.mult)
                    nc.vector.tensor_tensor(w_qkv[:, :, 2 * D:3 * D], w_qkv[:, :, D:2 * D], w_qkv[:, :, 2 * D:3 * D], ALU.subtract).then_inc(w_ready, 1)

            with ExitStack() as inner:
                sbi = lambda name, shape: inner.enter_context(nc.sbuf_tensor(f"ttt_{name}", shape, F32))
                w, w_in = sbi("w", [P, NG, HD, K1]), sbi("w_in", [P, HD * K1])
                gamma2, tok_in, inverse = sbi("gamma2", [P, HD]), sbi("tok_in", [P, C]), sbi("inverse", [P, C])
                neg_last = sbi("neg_last", [P, 1])
                prod = sbi("prod", [P, NG, C * HD * K1])
                z, sq, x_hat, gx, gxx = (sbi(n, [P, NG * C, HD]) for n in ("z", "sq", "x_hat", "gx", "gxx"))
                mu, var, rstd, s1, s2, coef = (sbi(n, [P, NG * C]) for n in ("mu", "var", "rstd", "s1", "s2", "coef"))
                half = sbi("half", [P, NG * C])
                step_w = sbi("step_w", [P, NG, HD, K1])
                g_seq = sbi("g_seq", [P, NG, HD, T])
                turned = inner.enter_context(nc.psum_tensor("ttt_turned", [T, 2, HD, P], F32))
                loaded, half_set, centred, squared, var_ready, rstd_ready = sem("loaded2"), sem("half_set"), sem("centred"), sem("squared"), sem("var_ready"), sem("rstd_ready")
                grads_ready, turn_ready, turn_copied, chain = sem("grads_ready"), sem("turn_ready"), sem("turn_copied"), sem("scan_chain")
                block = inner.enter_context(nc.Block())

                @block.sync
                def _(sp):
                    for b in range(NG):
                        sp.dma_start(w_in[b * H:(b + 1) * H, :], io["ttt_w0_seq"]).then_inc(loaded, 16)
                        sp.dma_start(gamma2[b * H:(b + 1) * H, :], io["ttt_gamma"]).then_inc(loaded, 16)
                    sp.dma_start(tok_in[:], io["ttt_token_idx"].unsqueeze(0).to_broadcast([P, C])).then_inc(loaded, 16)
                    sp.dma_start(inverse[:], io["ttt_inverse"].unsqueeze(0).to_broadcast([P, C])).then_inc(loaded, 16)

                @block.gpsimd
                def _(pool):
                    nc.gpsimd.memset(half[:], -0.5).then_inc(half_set, 1)
                    pool.wait_ge(half_set, 1)
                    with pool.Fori(0, NC) as n:
                        need(pool, var_ready, n + 1)
                        nc.gpsimd.tensor_tensor(rstd[:], var[:], half[:], ALU.pow).then_inc(rstd_ready, 1)

                @block.scalar
                def _(act):
                    with act.Fori(0, NC) as n:
                        need(act, centred, n + 1)
                        nc.scalar.activation(sq[:], z[:], ACT.Square).then_inc(squared, 1)
                    for g in range(NG):
                        act.wait_ge(turn_ready, g + 1)
                        nc.scalar.copy(g_tok[:, g * NG:(g + 1) * NG, :, :].rearrange("t b h o -> t (b h) o"),
                                       turned[:, g % 2].rearrange("t o p -> t p o")).then_inc(turn_copied, 1)

                @block.tensor
                def _(pe):
                    pe.wait_ge(grads_ready, NC)
                    for g in range(NG):
                        if g > 1:
                            pe.wait_ge(turn_copied, g - 1)
                        for o in range(HD):
                            ins = nc.tensor.transpose(turned[:, g % 2, o, :], g_seq[:, g, o, :], keep["ident"][:])
                        ins.then_inc(turn_ready, 1)

                @block.vector
                def _(dve):
                    order = Order(dve, chain)
                    tt, ts, tr, stt = nc.vector.tensor_tensor, nc.vector.tensor_scalar, nc.vector.tensor_reduce, nc.vector.scalar_tensor_tensor
                    dve.wait_ge(loaded, 16 * 10)
                    order(nc.vector.tensor_copy(w[:].rearrange("p g o k -> p g (o k)"), w_in[:].unsqueeze(1).to_broadcast([P, NG, HD * K1])))
                    order(tt(gamma2[:], gamma2[:], gamma2[:], ALU.mult))
                    order(tt(tok[:], tok_in[:], inverse[:], ALU.add))
                    order(ts(tok[:], tok[:], 0.0, None, ALU.max))
                    order(ts(neg_last[:], tok[:, C - 1:C], -1.0, None, ALU.mult))
                    wide = lambda t: t[:].unsqueeze(2).to_broadcast([P, NG * C, HD])
                    CHAIN = 20
                    start = order.k
                    with dve.Fori(0, NC) as n:
                        order.enter(n, CHAIN)
                        now = bass.ts(n, C)
                        for g in range(NG):
                            ins = tt(prod[:, g].rearrange("p (t o k) -> p t o k", t=C, o=HD),
                                     k_seq[:, g, :, now].rearrange("p k t -> p t k").unsqueeze(2).to_broadcast([P, C, HD, K1]),
                                     w[:, g].unsqueeze(1).to_broadcast([P, C, HD, K1]), ALU.mult)
                        order(ins)
                        order(tr(z[:], prod[:].rearrange("p g (t o k) -> p (g t o) k", t=C, o=HD), AX_X, ALU.add))
                        order(tr(mu[:], z[:], AX_X, ALU.add))
                        order(ts(mu[:], mu[:], 1.0 / HD, None, ALU.mult))
                        tt(z[:], z[:], wide(mu), ALU.subtract).then_inc(centred, 1)
                        need(dve, squared, n + 1)
                        order(tr(var[:], sq[:], AX_X, ALU.add))
                        ts(var[:], var[:], 1.0 / HD, EPS, ALU.mult, ALU.add).then_inc(var_ready, 1)
                        need(dve, rstd_ready, n + 1)
                        order(tt(x_hat[:], z[:], wide(rstd), ALU.mult))
                        order(tt(gx[:], x_hat[:], gamma2[:].unsqueeze(1).to_broadcast([P, NG * C, HD]), ALU.mult))
                        order(tt(gx[:].rearrange("p (g t) o -> p g t o", g=NG), gx[:].rearrange("p (g t) o -> p g t o", g=NG),
                                 c_seq[:, :, :, now].rearrange("p g o t -> p g t o"), ALU.add))
                        order(tr(s1[:], gx[:], AX_X, ALU.add))
                        order(tt(gxx[:], gx[:], x_hat[:], ALU.mult))
                        order(tr(s2[:], gxx[:], AX_X, ALU.add))
                        order(ts(s1[:], s1[:], 1.0 / HD, None, ALU.mult))
                        order(ts(s2[:], s2[:], 1.0 / HD, None, ALU.mult))
                        order(tt(gxx[:], x_hat[:], wide(s2), ALU.mult))
                        order(tt(gx[:], gx[:], gxx[:], ALU.subtract))
                        order(tt(gx[:], gx[:], wide(s1), ALU.subtract))
                        order(stt(coef[:].rearrange("p (g t) -> p g t", g=NG), lr_seq[:, :, now], 1.0 / HD, rstd[:].rearrange("p (g t) -> p g t", g=NG), ALU.mult, ALU.mult))
                        tt(g_seq[:, :, :, now].rearrange("p g o t -> p g t o"), gx[:].rearrange("p (g t) o -> p g t o", g=NG),
                           coef[:].rearrange("p (g t) -> p g t", g=NG).unsqueeze(3).to_broadcast([P, NG, C, HD]), ALU.mult).then_inc(grads_ready, 1)
                        need(dve, grads_ready, n + 1)
                        for g in range(NG):
                            ins = tt(prod[:, g].rearrange("p (o k t) -> p o k t", o=HD, k=K1),
                                     k_seq[:, g, :, now].unsqueeze(1).to_broadcast([P, HD, K1, C]),
                                     g_seq[:, g, :, now].unsqueeze(2).to_broadcast([P, HD, K1, C]), ALU.mult)
                        order(ins)
                        order(tr(step_w[:].rearrange("p g o k -> p (g o k)"), prod[:].rearrange("p g (m t) -> p (g m) t", t=C), AX_X, ALU.add))
                        order(stt(w[:].rearrange("p g o k -> p (g o k)"), step_w[:].rearrange("p g o k -> p (g o k)"), neg_last[:], w[:].rearrange("p g o k -> p (g o k)"),
                                  ALU.mult, ALU.add))
                        order.leave(NC)

        with ExitStack() as inner:
            sbi = lambda name, shape: inner.enter_context(nc.sbuf_tensor(f"ttt_{name}", shape, F32))
            psi = lambda name, shape: inner.enter_context(nc.psum_tensor(f"ttt_{name}", shape, F32))
            w0, b0, ones = sbi("w0", [P, DH, P]), sbi("b0", [1, D]), sbi("ones", [1, T])
            w_out, post_w, post_b = sbi("w_out", [P, DH, D]), sbi("post_w", [P, DH]), sbi("post_b", [P, DH])
            gamma_row, beta_row = sbi("gamma_row", [T, D]), sbi("beta_row", [T, D])
            inside, before, mask = sbi("inside", [T, T]), sbi("before", [T, T]), sbi("mask", [T, T])
            neg_last = sbi("neg_last2", [P, 1])
            eps = sbi("eps", [T, 1])
            U, UH, NB = 8, 4, 4
            APPLY_LAG = 3
            PEELED = 4
            q_bd, q_now, k_now = sbi("q_bd", [P, 2, DH, UH, T]), sbi("q_now", [P, 2, DH, T]), sbi("k_now", [P, 2, DH, UH, T])
            masked = sbi("masked", [T, NB, UH, T])
            z, sq, res = sbi("z2", [T, H, HD]), sbi("sq2", [T, H, HD]), sbi("res", [T, D])
            mu, var, std, rstd = sbi("mu2", [T, H]), sbi("var2", [T, H]), sbi("std2", [T, H]), sbi("rstd2", [T, H])
            stats, mean_var, var_eps, rstd_post = sbi("stats", [T, 6]), sbi("mean_var", [T, 2]), sbi("var_eps", [T, 1]), sbi("rstd_post", [T, 1])
            spare = sbi("spare", [T, 1])
            resT = sbi("resT", [P, DH, T])
            scores, z_ps = psi("scores", [T, NB, UH, T]), psi("z_ps", [T, 2, 512])
            turned_ps, out_norm_ps = psi("turned_ps", [P, 2, D]), psi("out_norm_ps", [P, 2, D])
            q_tok_ps, resT_ps = turned_ps[:, 0, :], turned_ps[:, 1, :].rearrange("p (c t) -> p c t", c=DH)
            out_ps, normT = out_norm_ps[:, 0, :], out_norm_ps[:, 1, :]
            loaded, ones_set, mask_ready = sem("loaded3"), sem("ones_set"), sem("mask_ready")
            now_ready, bd_ready, scores_ready, masked_ready, applied = sem("now_ready"), sem("bd_ready"), sem("scores_ready"), sem("masked_ready"), sem("applied")
            centred, squared, var_ready, std_ready, q_read = sem("centred2"), sem("squared2"), sem("var_ready2"), sem("std_ready"), sem("q_read")
            post_var_ready, post_rstd_ready, post_ready = sem("post_var_ready"), sem("post_rstd_ready"), sem("post_ready")
            resT_ready, resT_copied, out_ready, chain = sem("resT_ready"), sem("resT_copied"), sem("out_ready"), sem("out_chain")
            q_ready = sem("q_tok_ready")
            norm = Norm(nc, inner, "ttt_n", keep, normT)
            block = inner.enter_context(nc.Block())
            LOADED = 16 * 9

            @block.sync
            def _(sp):
                for dst, src in ((w0[:], io["ttt_w0_bd"]), (b0[:], io["ttt_b0"].unsqueeze(0)), (w_out[:], io["ttt_w_out"].rearrange("(c p) o -> p c o", p=P)),
                                 (post_w[:], io["ttt_post_w"]), (post_b[:], io["ttt_post_b"]),
                                 (gamma_row[:], io["ttt_gamma"].rearrange("h d -> (h d)").unsqueeze(0).to_broadcast([T, D])),
                                 (beta_row[:], io["ttt_beta"].rearrange("h d -> (h d)").unsqueeze(0).to_broadcast([T, D])),
                                 (inside[:], io["ttt_inside"]), (before[:], io["ttt_before"])):
                    sp.dma_start(dst, src).then_inc(loaded, 16)

            @block.gpsimd
            def _(pool):
                nc.gpsimd.memset(eps[:], EPS)
                nc.gpsimd.memset(ones[:], 1.0).then_inc(ones_set, 1)

                def rstd_after(b):
                    need(pool, post_var_ready, b + 1)
                    nc.gpsimd.tensor_tensor(rstd_post[:], var_eps[:], keep["neg_half"][:], ALU.pow).then_inc(post_rstd_ready, 1)

                def step(b, par, pair):
                    need(pool, applied, U * (b - 1))
                    nc.gpsimd.tensor_copy(q_now[:, par], q_feat[:, :, bass.ts(b, T)])
                    nc.gpsimd.tensor_tensor(k_now[:, par], k_feat[:, :, bass.ts(b, T)].unsqueeze(2).to_broadcast([P, DH, UH, T]),
                                            keep["group_mask"][:].unsqueeze(1).unsqueeze(3).to_broadcast([P, DH, UH, T]), ALU.mult).then_inc(now_ready, 1)
                    if since(b, 2):
                        rstd_after(b - 2)
                        norm.gpsimd(pool, b - 2)
                each_sequence(pool, step, peeled=PEELED)
                for b in range(B - 2, B):
                    rstd_after(b)
                    norm.gpsimd(pool, b)

            @block.scalar
            def _(act):
                act.wait_ge(loaded, LOADED)
                act.wait_ge(ones_set, 1)

                def spread_queries(b, par):
                    need(act, scores_ready, U * (b - 1))
                    for j in range(UH):
                        ins = nc.scalar.mul(q_bd[:, par, :, j, :], q_feat[:, :, bass.ts(b, T)], keep["head_mask"][:, j:j + 1])
                    ins.then_inc(bd_ready, 1)

                def deviation(b):
                    need(act, centred, b + 1)
                    nc.scalar.activation(sq[:], z[:], ACT.Square).then_inc(squared, 1)
                    need(act, var_ready, b + 1)
                    nc.scalar.activation(std[:], var[:], ACT.Sqrt, bias=eps[:], scale=1.0 / HD).then_inc(std_ready, 1)

                def copy_res(b):
                    need(act, resT_ready, b + 1)
                    need(act, out_ready, b)
                    for c in range(DH):
                        ins = nc.scalar.activation(resT[:, c, :], resT_ps[:, c, :], ACT.Identity, bias=post_b[:, c:c + 1], scale=post_w[:, c:c + 1])
                    ins.then_inc(resT_copied, 1)

                def step(b, par, pair):
                    spread_queries(b, par)
                    if since(b, 2):
                        copy_res(b - 2)
                    if since(b, 1):
                        deviation(b - 1)
                    if since(b, 2):
                        norm.scalar(act, b - 2)
                each_sequence(act, step, peeled=PEELED)
                copy_res(B - 2)
                deviation(B - 1)
                norm.scalar(act, B - 2)
                copy_res(B - 1)
                norm.scalar(act, B - 1)
                norm.done(act)

            @block.tensor
            def _(pe):
                pe.wait_ge(loaded, LOADED)
                pe.wait_ge(ones_set, 1)

                def score(b, par, u):
                    if u == 0:
                        need(pe, now_ready, b + 1)
                        need(pe, bd_ready, b + 1)
                    need(pe, masked_ready, U * b + u + 1 - NB)
                    c, r = u // UH, u % UH
                    nc.tensor.matmul(scores[:, u % NB], k_now[:, par, c, r, :], q_bd[:, par, c, :, :], start=True, stop=True).then_inc(scores_ready, 1)

                def begin(b, par):
                    need(pe, centred, b - 1)
                    for c in range(DH):
                        nc.tensor.matmul(z_ps[:, par, c * P:(c + 1) * P], q_now[:, par, c, :], w0[:, c, :], start=(c == 0), stop=False, skip_group_check=True)
                    nc.tensor.matmul(z_ps[:, par, 0:D], ones[:], b0[:], start=False, stop=False, skip_group_check=True)

                def turn_queries(b, par):
                    need(pe, q_read, b)
                    for c in range(DH):
                        ins = nc.tensor.transpose(q_tok_ps[:, c * P:(c + 1) * P], q_now[:, par, c, :], keep["ident"][:])
                    ins.then_inc(q_ready, 1)

                def apply(b, par, u):
                    need(pe, masked_ready, U * b + u + 1)
                    for h in range(UH):
                        hq = u * UH + h
                        ins = nc.tensor.matmul(z_ps[:, par, hq * HD:(hq + 1) * HD], masked[:, u % NB, h, :], g_tok[:, b, hq, :], start=False,
                                               stop=(hq == H - 1), skip_group_check=True)
                    ins.then_inc(applied, 1)

                def turn_res(b):
                    need(pe, post_ready, b + 1)
                    need(pe, resT_copied, b)
                    for c in range(DH):
                        ins = nc.tensor.transpose(resT_ps[:, c, :], res[:, c * P:(c + 1) * P], keep["ident"][:])
                    ins.then_inc(resT_ready, 1)

                def out(b):
                    need(pe, resT_copied, b + 1)
                    need(pe, norm.var_ready, b)
                    for c in range(DH):
                        ins = nc.tensor.matmul(out_ps[:], resT[:, c, :], w_out[:, c, :], start=(c == 0), stop=(c == DH - 1))
                    ins.then_inc(out_ready, 1)

                def step(b, par, pair):
                    for u in range(U):
                        score(b, par, u)
                        lagged(apply, b, par, u, APPLY_LAG, U)
                        if u == 0 and since(b, 2):
                            out(b - 2)
                        if u == 1:
                            begin(b, par)
                        if u == 3 and since(b, 2):
                            norm.tensor(pe, b - 2)
                        if u == 5:
                            turn_queries(b, par)
                        if u == 7 and since(b, 1):
                            turn_res(b - 1)
                each_sequence(pe, step, peeled=PEELED)
                for u in range(APPLY_LAG):
                    lagged(apply, B, 0, u, APPLY_LAG, U)
                out(B - 2)
                norm.tensor(pe, B - 2)
                turn_res(B - 1)
                out(B - 1)
                norm.tensor(pe, B - 1)

            @block.vector
            def _(dve):
                order = Order(dve, chain)
                tt, ts, tr, stt = nc.vector.tensor_tensor, nc.vector.tensor_scalar, nc.vector.tensor_reduce, nc.vector.scalar_tensor_tensor
                dve.wait_ge(loaded, LOADED)
                order(ts(neg_last[:], tok[:, C - 1:C], -1.0, None, ALU.mult))
                order(tt(mask[:].rearrange("p (n i) -> p n i", i=C), inside[:].rearrange("p (n i) -> p n i", i=C), tok[:].unsqueeze(1).to_broadcast([P, NC, C]), ALU.mult))
                order(stt(mask[:], before[:], neg_last[:], mask[:], ALU.mult, ALU.subtract))

                def masks(b, u):
                    need(dve, scores_ready, U * b + u + 1)
                    need(dve, applied, U * b + u + 1 - NB)
                    stt(masked[:, u % NB], scores[:, u % NB], 1.0, mask[:].unsqueeze(1).to_broadcast([T, UH, T]), ALU.add, ALU.mult).then_inc(masked_ready, 1)

                wide = lambda t: t[:].unsqueeze(2).to_broadcast([T, H, HD])

                def centre(b, par):
                    z3 = z_ps[:, par, 0:D].rearrange("p (h d) -> p h d", h=H)
                    need(dve, applied, U * (b + 1))
                    order(tr(mu[:], z3, AX_X, ALU.add))
                    order(ts(mu[:], mu[:], 1.0 / HD, None, ALU.mult))
                    tt(z[:], z3, wide(mu), ALU.subtract).then_inc(centred, 1)

                def variance(b):
                    need(dve, squared, b + 1)
                    tr(var[:], sq[:], AX_X, ALU.add).then_inc(var_ready, 1)

                def head_norm(b):
                    need(dve, std_ready, b + 1)
                    order(nc.vector.reciprocal(rstd[:], std[:]))
                    order(tt(z[:], z[:], wide(rstd), ALU.mult))
                    z2 = z[:].rearrange("p h d -> p (h d)")
                    order(tt(z2, z2, gamma_row[:], ALU.mult))
                    order(tt(z2, z2, beta_row[:], ALU.add))
                    need(dve, resT_ready, b)
                    need(dve, q_ready, b + 1)
                    tt(res[:], z2, q_tok_ps, ALU.add).then_inc(q_read, 1)

                def post_stats(b):
                    need(dve, q_read, b + 1)
                    order(nc.vector.bn_stats(stats[:], res[:]))
                    nc.vector.memset(spare[:], 0.0)
                    order(nc.vector.bn_aggr(mean_var[:], stats[:]))
                    ts(var_eps[:], mean_var[:, 1:2], EPS, None, ALU.add).then_inc(post_var_ready, 1)

                def post_norm(b):
                    need(dve, post_rstd_ready, b + 1)
                    ts(res[:], res[:], mean_var[:, 0:1], rstd_post[:], ALU.subtract, ALU.mult).then_inc(post_ready, 1)

                def block_norm(b):
                    need(dve, out_ready, b + 1)
                    norm.vector_begin(dve, order, b, out_ps)

                def step(b, par, pair):
                    for u in range(U):
                        masks(b, u)
                        if u == 0 and since(b, 2):
                            block_norm(b - 2)
                        if u == 1 and since(b, 2):
                            norm.vector_end(dve, b - 2)
                        if since(b, 1):
                            if u == 2:
                                centre(b - 1, 1 - par)
                            if u == 3:
                                variance(b - 1)
                            if u == 4:
                                head_norm(b - 1)
                            if u == 5:
                                post_stats(b - 1)
                            if u == 6:
                                post_norm(b - 1)
                each_sequence(dve, step, order, per=2 * (8 + norm.CHAIN - 1), peeled=PEELED)
                block_norm(B - 2)
                norm.vector_end(dve, B - 2)
                centre(B - 1, (B - 1) % 2)
                variance(B - 1)
                head_norm(B - 1)
                post_stats(B - 1)
                post_norm(B - 1)
                block_norm(B - 1)
                norm.vector_end(dve, B - 1)


def open_persistent(nc, ctx):
    keep = {"semaphores": []}
    sb = lambda name, shape: ctx.enter_context(nc.sbuf_tensor(name, shape, F32))
    keep["x_tok"] = sb("x_tok", [T, B, D])
    keep["xT"] = sb("xT", [P, DH, B * T])
    keep["ident"] = sb("ident", [P, P])
    keep["neg_half"] = sb("neg_half", [P, 1])
    keep["head_mask"] = sb("head_mask", [P, 4])
    keep["group_mask"] = sb("group_mask", [P, 4])
    return keep


def load_persistent(nc, keep, io):
    with ExitStack() as ctx:
        loaded, set_ = new_semaphore(nc, keep, "first_loaded"), new_semaphore(nc, keep, "half_set")
        block = ctx.enter_context(nc.Block())

        @block.sync
        def _(sp):
            sp.dma_start(keep["xT"][:], io["x_feat"].rearrange("(c p) n -> p c n", p=P)).then_inc(loaded, 16)
            sp.dma_start(keep["ident"][:], io["identity"]).then_inc(loaded, 16)
            sp.dma_start(keep["head_mask"][:], io["head_mask"]).then_inc(loaded, 16)
            sp.dma_start(keep["group_mask"][:], io["group_mask"]).then_inc(loaded, 16)
            sp.dma_start(keep["x_tok"][:], io["x"].rearrange("b t d -> t b d")).then_inc(loaded, 16)
            sp.wait_ge(loaded, 5 * 16)

        @block.vector
        def _(dve):
            nc.vector.memset(keep["neg_half"][:], -0.5).then_inc(set_, 1)
            dve.wait_ge(set_, 1)


def decoder(nc, io, out):
    with ExitStack() as ctx:
        keep = open_persistent(nc, ctx)
        load_persistent(nc, keep, io)
        for phase in (test_time_training, cross_attention_gqa, gated_ffn_int8, batch_axis_attention, latent_cross_attention):
            phase(nc, keep, io)
            give_back_semaphores(nc, keep)
        mixture_of_experts(nc, keep, io, out)


def lay_out(x, ctx, inputs):
    a0 = lambda name: np.asarray(inputs[f"L0_attn_{name}"])
    f0 = lambda name: np.asarray(inputs[f"L0_ffn_{name}"])
    a1 = lambda name: np.asarray(inputs[f"L1_attn_{name}"])
    m1 = lambda name: np.asarray(inputs[f"L1_xattn_{name}"])
    e1 = lambda name: np.asarray(inputs[f"L1_ffn_{name}"])
    feat = lambda v: v.reshape(-1, P).T
    io = {"x": x, "x_feat": x.reshape(B * T, D).T, "ctx": ctx}

    part = np.arange(P)
    io["identity"] = np.eye(P, dtype=np.float32)
    io["group_mask"] = (part[:, None] // 32 == np.arange(4)[None, :]).astype(np.float32)
    io["head_mask"] = (part[:, None] // 8 % 4 == np.arange(4)[None, :]).astype(np.float32)

    heads, hd, chunk = 32, 8, 16
    io["ttt_w_qkv"] = np.concatenate([a0("q_w").T, a0("k_w").T, a0("v_w").T], axis=1)
    io["ttt_w_lr"] = a0("ttt_lr_weight").reshape(heads, D).T
    io["ttt_lr_bias"] = a0("ttt_lr_bias")
    io["ttt_gamma_feat"], io["ttt_beta_feat"] = feat(a0("ttt_norm_weight")), feat(a0("ttt_norm_bias"))
    io["ttt_gamma"], io["ttt_beta"] = a0("ttt_norm_weight"), a0("ttt_norm_bias")
    w_first = a0("W1")
    io["ttt_w0_seq"] = np.concatenate([w_first.transpose(0, 2, 1), a0("b1").transpose(0, 2, 1)], axis=2).reshape(heads, hd * (hd + 1))
    w_bd = np.zeros((P, DH, P), w_first.dtype)
    for h in range(heads):
        r = h % (heads // DH) * hd
        w_bd[r:r + hd, h // (heads // DH), r:r + hd] = w_first[h]
    io["ttt_w0_bd"], io["ttt_b0"] = w_bd, a0("b1").reshape(D)
    io["ttt_token_idx"] = a0("learnable_token_idx")
    io["ttt_inverse"] = np.float32(1) / np.arange(1, chunk + 1, dtype=np.float32)
    io["ttt_w_out"] = a0("o_w").T
    io["ttt_post_w"], io["ttt_post_b"] = feat(a0("post_norm_weight")), feat(a0("post_norm_bias"))
    same, earlier = part[:, None] // chunk == part[None, :] // chunk, part[:, None] // chunk < part[None, :] // chunk
    io["ttt_inside"] = (same & (part[:, None] <= part[None, :])).astype(np.float32)
    io["ttt_before"] = earlier.astype(np.float32)

    by_head = ctx.transpose(0, 2, 1).reshape(B, DH, 4, 1, 8, T)
    io["ctx_rep"] = np.broadcast_to(by_head, (B, DH, 4, 4, 8, T)).reshape(B, DH, P, T)

    words = lambda a: np.ascontiguousarray(a).view(np.int32)
    io["ffn_w_gate"], io["ffn_w_up"], io["ffn_w_down"] = words(f0("w_gate")), words(f0("w_up")), words(f0("w_down"))
    io["ffn_s_gate"], io["ffn_s_up"], io["ffn_s_down"] = feat(f0("s_gate")), feat(f0("s_up")), f0("s_down")

    io["ba_w_qkv"] = np.concatenate([a1("q_proj").T, a1("k_proj").T, a1("v_proj").T], axis=1)
    io["ba_b_qkv"] = np.concatenate([a1("q_bias"), a1("k_bias"), a1("v_bias")])
    io["ba_w_out"], io["ba_b_out"] = a1("out_proj").T, a1("out_bias")

    dc = ctx.shape[2]
    frequency = (np.float32(1) / np.float32(10000) ** (np.arange(0, dc, 2, dtype=np.float32) / np.float32(dc))).astype(np.float32)
    angle = np.arange(T, dtype=np.float32)[:, None] * frequency[None, :]
    sign = np.where(np.arange(dc) < dc // 2, np.float32(-1), np.float32(1))
    io["cosines"] = np.repeat(np.cos(angle), 2, axis=-1)
    io["sines"] = np.repeat(np.sin(angle), 2, axis=-1) * sign
    io["mla_wq"], io["mla_kc_kv"], io["mla_woT"] = m1("Wq"), m1("w_kc_kv"), m1("Wo").T
    io["mla_kc_qT"] = m1("w_kc_q").reshape(16, 128, 2, 96).transpose(3, 2, 0, 1)
    io["mla_qrT"], io["mla_krT"] = m1("W_qr").transpose(2, 0, 1), m1("W_kr").transpose(2, 0, 1)

    experts, groups, f = 64, 8, 96
    io["moe_w_route"], io["moe_bias"] = e1("gate_w"), e1("bias")
    io["moe_not_first"] = (np.arange(B * experts) % experts != 0).astype(np.float32)
    io["moe_lower"] = (np.arange(groups)[None, :] < np.arange(groups)[:, None]).astype(np.float32).reshape(-1)
    io["moe_countdown"] = (B * T - (np.arange(B)[None, :] * T + part[:, None])).astype(np.float32)
    io["moe_slot_no"] = part[:, None].astype(np.float32)
    io["moe_ws_gu"], io["moe_ws_down"] = np.concatenate([e1("ws_gate"), e1("ws_up")], axis=1), e1("ws_down")
    gate_up = np.concatenate([e1("w_gate").reshape(experts // 2, 2, DH, P, f), e1("w_up").reshape(experts // 2, 2, DH, P, f)], axis=-1)
    io["moe_w_gu"] = gate_up.transpose(0, 3, 1, 2, 4)
    io["moe_w_down"] = e1("w_down").reshape(experts // 2, 2, f, D).transpose(0, 2, 1, 3)
    return {name: np.ascontiguousarray(a) for name, a in io.items()}


def kernel(**inputs):
    import concourse.bacc as bacc
    from concourse.bass_utils import run_bass_kernel_spmd

    nc = bacc.Bacc("TRN2", target_bir_lowering=False, num_devices=1)
    arrays = lay_out(np.asarray(inputs["x"]), np.asarray(inputs["ctx_512"]), inputs)
    io = {name: nc.dram_tensor(f"in_{name}", a.shape, mybir.dt.from_np(a.dtype), kind="ExternalInput").ap() for name, a in arrays.items()}
    out = nc.dram_tensor("out", (B, T, D), F32, kind="ExternalOutput").ap()
    decoder(nc, io, out)
    result = run_bass_kernel_spmd(nc, [{f"in_{name}": a for name, a in arrays.items()}], core_ids=[0])
    return result.results[0]["out"]
```

```python
from contextlib import ExitStack

import concourse.bass as bass
import numpy as np
from concourse import mybir

ALU = mybir.AluOpType
ACT = mybir.ActivationFunctionType
F32 = mybir.dt.float32
BF16 = mybir.dt.bfloat16
U32 = mybir.dt.uint32
I8 = mybir.dt.int8
I32 = mybir.dt.int32
AX_X = mybir.AxisListType.X

P = 128
B = 16
T = 128
D = 256
DH = D // P
LN_EPS = 1e-5


def need(eng, sem, value):
    if isinstance(value, int) and value <= 0:
        return
    eng.wait_ge(sem, value)


class Order:

    def __init__(self, eng, sem):
        self.eng, self.sem = eng, sem
        self.base, self.trip, self.per, self.k = 0, 0, 0, 0

    def enter(self, trip, per):
        self.base += self.k
        self.trip, self.per, self.k = trip, per, 0

    def leave(self, trips):
        assert self.k == self.per, (self.k, self.per)
        self.base += trips * self.per
        self.trip, self.per, self.k = 0, 0, 0

    def __call__(self, ins):
        ins.then_inc(self.sem, 1)
        self.k += 1
        self.eng.wait_ge(self.sem, self.base + self.trip * self.per + self.k)


def new_semaphore(nc, keep, name):
    keep["semaphores"].append(nc.alloc_semaphore(name))
    return keep["semaphores"][-1]


def give_back_semaphores(nc, keep):
    nc.clear_and_free_semaphores(keep["semaphores"])
    keep["semaphores"] = []
    nc.all_engine_barrier()


def first(b):
    return isinstance(b, int) and b == 0


def since(b, n):
    return not isinstance(b, int) or b >= n


def lagged(step, b, par, u, lag, units):
    k = u - lag
    if k >= 0:
        if not (isinstance(b, int) and b == B):
            step(b, par, k)
    elif not first(b):
        step(b - 1, 1 - par, k + units)


def refined_rstd(nc, order, rstd, std, var_eps, spare):
    order(nc.vector.reciprocal(rstd, std))
    order(nc.vector.scalar_tensor_tensor(spare, rstd, -0.5, rstd, ALU.mult, ALU.mult))
    order(nc.vector.tensor_tensor(spare, spare, var_eps, ALU.mult))
    return nc.vector.scalar_tensor_tensor(rstd, spare, 1.5, rstd, ALU.add, ALU.mult)


def each_sequence(eng, step, order=None, per=0, peeled=2):
    for b in range(peeled):
        step(b, b % 2, b // 2)
    trips = (B - peeled) // 2
    with eng.Fori(0, trips) as i:
        if order:
            order.enter(i, per)
        for par in range(2):
            step(2 * i + peeled + par, par, i + peeled // 2)
        if order:
            order.leave(trips)


class Norm:

    CHAIN = 4

    def __init__(self, nc, ctx, tag, keep, turned_psum):
        self.nc, self.x_tok, self.xT, self.ident, self.neg_half = nc, keep["x_tok"], keep["xT"], keep["ident"], keep["neg_half"]
        sb = lambda name, shape: ctx.enter_context(nc.sbuf_tensor(f"{tag}_{name}", shape, F32))
        sem = lambda name: new_semaphore(nc, keep, f"{tag}_{name}")
        self.total, self.stats, self.mean_var = sb("total", [P, D]), sb("stats", [P, 6]), sb("mean_var", [P, 2])
        self.spare = sb("spare", [P, 1])
        self.var_eps, self.rstd, self.normed = sb("var_eps", [P, 1]), sb("rstd", [P, 1]), sb("normed", [P, D])
        self.turned = turned_psum
        self.var_ready, self.rstd_ready = sem("var_ready"), sem("rstd_ready")
        self.norm_ready, self.kept = sem("norm_ready"), sem("kept")
        self.turn_ready, self.turn_copied = sem("turn_ready"), sem("turn_copied")

    def vector(self, eng, order, b, y):
        self.vector_begin(eng, order, b, y)
        self.vector_end(eng, b)

    def vector_begin(self, eng, order, b, y):
        nc = self.nc
        order(nc.vector.tensor_tensor(self.total[:], y, self.x_tok[:, b, :], ALU.add))
        order(nc.vector.bn_stats(self.stats[:], self.total[:]))
        nc.vector.memset(self.spare[:], 0.0)
        order(nc.vector.bn_aggr(self.mean_var[:], self.stats[:]))
        nc.vector.tensor_scalar(self.var_eps[:], self.mean_var[:, 1:2], LN_EPS, None, ALU.add).then_inc(self.var_ready, 1)

    def vector_end(self, eng, b):
        nc = self.nc
        need(eng, self.rstd_ready, b + 1)
        need(eng, self.kept, b)
        need(eng, self.turn_ready, b)
        nc.vector.tensor_scalar(self.normed[:], self.total[:], self.mean_var[:, 0:1], self.rstd[:],
                                ALU.subtract, ALU.mult).then_inc(self.norm_ready, 1)
        need(eng, self.norm_ready, b + 1)

    def gpsimd(self, eng, b):
        nc = self.nc
        need(eng, self.var_ready, b + 1)
        nc.gpsimd.tensor_tensor(self.rstd[:], self.var_eps[:], self.neg_half[:], ALU.pow).then_inc(self.rstd_ready, 1)
        need(eng, self.norm_ready, b + 1)
        nc.gpsimd.tensor_copy(self.x_tok[:, b, :], self.normed[:]).then_inc(self.kept, 1)

    def tensor(self, eng, b):
        need(eng, self.norm_ready, b + 1)
        need(eng, self.turn_copied, b)
        for c in range(DH):
            ins = self.nc.tensor.transpose(self.turned[:, c * T:(c + 1) * T], self.normed[:, c * P:(c + 1) * P], self.ident[:])
        ins.then_inc(self.turn_ready, 1)

    def scalar(self, eng, b):
        need(eng, self.turn_ready, b + 1)
        self.nc.scalar.copy(self.xT[:, :, bass.ts(b, T)], self.turned[:].rearrange("p (c t) -> p c t", c=DH)).then_inc(self.turn_copied, 1)

    def done(self, eng):
        eng.wait_ge(self.kept, B)
        eng.wait_ge(self.turn_copied, B)


def cross_attention_gqa(nc, keep, io):
    NQ, NKV, HD = 32, 8, 8
    G = NQ // NKV
    UH = G
    U = NQ // UH
    NB = 4
    TURN_LAG, WEIGH_LAG = 3, 4
    SKEW = 4
    with ExitStack() as ctx:
        sb = lambda name, shape: ctx.enter_context(nc.sbuf_tensor(f"gqa_{name}", shape, F32))
        ps = lambda name, shape: ctx.enter_context(nc.psum_tensor(f"gqa_{name}", shape, F32))
        sem = lambda name: new_semaphore(nc, keep, f"gqa_{name}")
        q_feat = sb("q_feat", [P, 2, DH, NKV // DH, T])
        keys = sb("keys", [P, 2, DH, G, T])
        keys_in = sb("keys_in", [P, 2, DH, T])
        ctx_in = sb("ctx_in", [T, B, NKV * HD])
        values = sb("values", [T, 2, NKV, HD + 1])
        probs = sb("probs", [T, NB, UH, T])
        probsT = sb("probsT", [T, NB, UH, T])
        row_max = sb("row_max", [T, NB, UH])
        rsum = sb("rsum", [T, NQ])
        attended = sb("attended", [T, NQ, HD])
        scores = ps("scores", [T, NB, UH, T])
        turned = ps("turned", [T, 2, UH, T])
        weighted = ps("weighted", [T, NQ * (HD + 1)])
        normT = ps("normT", [P, DH * T])
        keys_ready, keys_loaded, ctx_loaded, ones_set = sem("keys_ready"), [sem("keys_loaded0"), sem("keys_loaded1")], sem("ctx_loaded"), sem("ones_set")
        q_ready, v_ready = sem("q_ready"), sem("v_ready")
        scores_ready, shifted, max_ready = sem("scores_ready"), sem("shifted"), sem("max_ready")
        exp_ready, turn_ready, turn_copied, weigh_ready, out_read, chain = (
            sem("exp_ready"), sem("turn_ready"), sem("turn_copied"), sem("weigh_ready"), sem("out_read"), sem("chain"))
        norm = Norm(nc, ctx, "gqa_n", keep, normT)
        weighted3 = weighted[:].rearrange("p (h e) -> p h e", h=NQ)
        HKV = NKV // DH
        ROWS = G * HD

        block = ctx.enter_context(nc.Block())

        @block.sync
        def _(sp):
            sp.dma_start(ctx_in[:], io["ctx"].rearrange("b t d -> t b d")).then_inc(ctx_loaded, 16)
            def step(b, par, pair):
                need(sp, keys_ready, b - 1)
                sp.dma_start(keys_in[:, par], io["ctx_rep"][b].rearrange("c p t -> p c t")).then_inc(keys_loaded[par], 16)
            each_sequence(sp, step)

        @block.gpsimd
        def _(pool):
            nc.gpsimd.memset(values[:, :, :, HD:HD + 1], 1.0).then_inc(ones_set, 1)
            pool.wait_ge(ctx_loaded, 16)

            def step(b, par, pair):
                need(pool, scores_ready, U * (b - 1))
                nc.gpsimd.tensor_tensor(q_feat[:, par], keep["xT"][:, :, bass.ts(b, T)].unsqueeze(2).to_broadcast([P, DH, HKV, T]),
                                        keep["group_mask"][:].unsqueeze(1).unsqueeze(3).to_broadcast([P, DH, HKV, T]), ALU.mult).then_inc(q_ready, 1)
                need(pool, weigh_ready, U * (b - 1))
                nc.gpsimd.tensor_copy(values[:, par, :, 0:HD], ctx_in[:, b, :].rearrange("p (k d) -> p k d", k=NKV)).then_inc(v_ready, 1)
                if not first(b):
                    norm.gpsimd(pool, b - 1)
            each_sequence(pool, step)
            norm.gpsimd(pool, B - 1)

        @block.tensor
        def _(pe):
            def score(b, par, u):
                if u == 0:
                    need(pe, keys_ready, b + 1)
                    need(pe, q_ready, b + 1)
                need(pe, shifted, U * b + u + 1 - NB)
                half, r = u // HKV, u % HKV
                nc.tensor.matmul(scores[:, u % NB], q_feat[:, par, half, r, :], keys[:, par, half, :, :],
                                 start=True, stop=True).then_inc(scores_ready, 1)

            def turn(b, par, u):
                need(pe, exp_ready, U * b + u + 1)
                need(pe, turn_copied, U * b + u - 1)
                for h in range(UH):
                    ins = nc.tensor.transpose(turned[:, u % 2, h, :], probs[:, u % NB, h, :], keep["ident"][:])
                ins.then_inc(turn_ready, 1)

            def weigh(b, par, u):
                if u == 0:
                    need(pe, v_ready, b + 1)
                    need(pe, out_read, b)
                need(pe, turn_copied, U * b + u + 1)
                for h in range(UH):
                    ins = nc.tensor.matmul(weighted3[:, u * UH + h, :], probsT[:, u % NB, h, :], values[:, par, u, :],
                                           start=True, stop=True)
                ins.then_inc(weigh_ready, 1)

            pe.wait_ge(ones_set, 1)

            def step(b, par, pair):
                for u in range(U):
                    score(b, par, u)
                    lagged(turn, b, par, u, TURN_LAG, U)
                    lagged(weigh, b, par, u, WEIGH_LAG, U)
                    if u == U - 1 and not first(b):
                        norm.tensor(pe, b - 1)
            each_sequence(pe, step)
            for u in range(WEIGH_LAG):
                if u < TURN_LAG:
                    lagged(turn, B, 0, u, TURN_LAG, U)
                lagged(weigh, B, 0, u, WEIGH_LAG, U)
            norm.tensor(pe, B - 1)

        @block.scalar
        def _(act):
            def spread_keys(b, par, pair):
                act.wait_ge(keys_loaded[par], 16 * (pair + 1))
                need(act, scores_ready, U * (b - 1))
                for j in range(G):
                    ins = nc.scalar.mul(keys[:, par, :, j, :], keys_in[:, par], keep["head_mask"][:, j:j + 1])
                ins.then_inc(keys_ready, 1)

            def copy_turned(b, par, u):
                need(act, turn_ready, U * b + u + 1)
                need(act, weigh_ready, U * b + u + 1 - NB)
                nc.scalar.copy(probsT[:, u % NB], turned[:, u % 2]).then_inc(turn_copied, 1)

            def exponential(b, par, u):
                need(act, shifted, U * b + u + 1)
                nc.scalar.activation(probs[:, u % NB], probs[:, u % NB], ACT.Exp, scale=HD ** -0.5).then_inc(exp_ready, 1)

            def step(b, par, pair):
                spread_keys(b, par, pair)
                for u in range(U):
                    lagged(copy_turned, b, par, u, TURN_LAG + SKEW, U)
                    lagged(exponential, b, par, u, SKEW, U)
                    if u == SKEW and since(b, 2):
                        norm.scalar(act, b - 2)
            each_sequence(act, step)
            for u in range(TURN_LAG + SKEW):
                lagged(copy_turned, B, 0, u, TURN_LAG + SKEW, U)
                if u < SKEW:
                    lagged(exponential, B, 0, u, SKEW, U)
                if u == SKEW:
                    norm.scalar(act, B - 2)
            norm.scalar(act, B - 1)
            norm.done(act)

        @block.vector
        def _(dve):
            order = Order(dve, chain)

            def divide(b):
                need(dve, weigh_ready, U * (b + 1))
                order(nc.vector.reciprocal(rsum[:], weighted3[:, :, HD]))
                nc.vector.tensor_tensor(attended[:], weighted3[:, :, 0:HD], rsum[:].unsqueeze(2).to_broadcast([T, NQ, HD]),
                                        ALU.mult).then_inc(out_read, 1)

            def add(b):
                need(dve, out_read, b + 1)
                norm.vector_begin(dve, order, b, attended[:].rearrange("p h e -> p (h e)"))

            def step(b, par, pair):
                for u in range(U):
                    need(dve, scores_ready, U * b + u + 1)
                    order(nc.vector.tensor_reduce(row_max[:, u % NB], scores[:, u % NB], AX_X, ALU.max))
                    need(dve, turn_ready, U * b + u + 1 - NB)
                    nc.vector.tensor_tensor(probs[:, u % NB], scores[:, u % NB],
                                            row_max[:, u % NB].unsqueeze(2).to_broadcast([T, UH, T]), ALU.subtract).then_inc(shifted, 1)
                    if u == WEIGH_LAG - 1 and not first(b):
                        divide(b - 1)
                    if u == WEIGH_LAG and not first(b):
                        add(b - 1)
                    if u == WEIGH_LAG + 1 and not first(b):
                        norm.vector_end(dve, b - 1)
            each_sequence(dve, step, order, per=2 * (U + 4))
            divide(B - 1)
            add(B - 1)
            norm.vector_end(dve, B - 1)


def gated_ffn_int8(nc, keep, io):
    F = io["ffn_w_gate"].shape[1] * 4
    FT = F // P
    GB = 4
    GT = GB * T
    NG = B // GB
    PARTS = 3
    with ExitStack() as ctx:
        sb = lambda name, shape, dt=F32: ctx.enter_context(nc.sbuf_tensor(f"ff_{name}", shape, dt))
        ps = lambda name, shape: ctx.enter_context(nc.psum_tensor(f"ff_{name}", shape, F32))
        sem = lambda name: new_semaphore(nc, keep, f"ff_{name}")
        w_in = sb("w_in", [P, DH, 2, F // 4], I32)
        wd_in = sb("wd_in", [P, FT, D // 4], I32)
        w_up = sb("w_gate_up", [P, DH, 2, F], BF16)
        w_down = sb("w_down", [P, FT, D], BF16)
        s_in = sb("s_in", [P, 2, FT])
        s_down = sb("s_down", [P, D])
        x_parts = sb("x_parts", [P, 2, PARTS, DH, GT], BF16)
        x_rest = sb("x_rest", [P, DH, GT])
        gate = sb("gate", [P, 2, GT])
        fused = sb("fused", [P, 2, GT])
        h_rest = sb("h_rest", [P, 2, GT])
        h_parts = sb("h_parts", [P, 2, PARTS, FT, GT], BF16)
        y = sb("y", [P, D])
        gate_ps, up_ps = ps("gate_ps", [P, 2, GT]), ps("up_ps", [P, 2, GT])
        down_ps = ps("down_ps", [P, 2, 512])
        normT = ps("normT", [P, DH * T])
        loaded, cast_done, x_split, x_first, x_second = sem("loaded"), sem("cast_done"), sem("x_split"), sem("x_first"), sem("x_second")
        gate_ready, up_ready, silu_ready, fused_ready, h_first, h_second, h_split = (
            sem("gate_ready"), sem("up_ready"), sem("silu_ready"), sem("fused_ready"), sem("h_first"), sem("h_second"), sem("h_split"))
        h_rest_ready, x_rest_ready = sem("h_rest_ready"), sem("x_rest_ready")
        down_ready, y_ready, chain = sem("down_ready"), sem("y_ready"), sem("chain")
        norm = Norm(nc, ctx, "ff_n", keep, normT)

        block = ctx.enter_context(nc.Block())

        @block.sync
        def _(sp):
            for k, name in enumerate(("ffn_w_gate", "ffn_w_up")):
                sp.dma_start(w_in[:, :, k, :], io[name].rearrange("(c p) f -> p c f", p=P)).then_inc(loaded, 16)
            sp.dma_start(wd_in[:], io["ffn_w_down"].rearrange("(f p) d -> p f d", p=P)).then_inc(loaded, 16)
            for k, name in enumerate(("ffn_s_gate", "ffn_s_up")):
                sp.dma_start(s_in[:, k, :], io[name]).then_inc(loaded, 16)
            sp.dma_start(s_down[:], io["ffn_s_down"].unsqueeze(0).to_broadcast([P, D])).then_inc(loaded, 16)

        LOADED = 6 * 16

        @block.gpsimd
        def _(pool):
            def step(b):
                norm.gpsimd(pool, b)
            with pool.Fori(0, B) as b:
                step(b)

        TILES = FT * NG
        SPLIT_AT = 3
        begins = lambda b: FT * (b // GB + 1) + (FT // GB) * (b % GB) + 1
        END = begins(B - 1) + 4
        sequence_at = lambda n: next((b for b in range(B) if begins(b) == n), None)
        group_to_split = lambda n: n // FT + 1 if n % FT == SPLIT_AT and n // FT + 1 < NG else None

        @block.scalar
        def _(act):
            act.wait_ge(loaded, LOADED)
            nc.scalar.copy(w_up[:, 0], w_in[:, 0].bitcast(I8)).then_inc(cast_done, 1)

            def split_first(g):
                need(act, up_ready, FT * (g - 1))
                nc.scalar.copy(x_parts[:, g % 2, 0], keep["xT"][:, :, bass.ts(g, GT)]).then_inc(x_first, 1)

            def split_second(g):
                act.wait_ge(x_rest_ready, g + 1)
                nc.scalar.copy(x_parts[:, g % 2, 1], x_rest[:]).then_inc(x_second, 1)

            def silu(n):
                act.wait_ge(gate_ready, n + 1)
                need(act, fused_ready, n - 1)
                nc.scalar.activation(gate[:, n % 2], gate_ps[:, n % 2], ACT.Silu, scale=s_in[:, 0, n % FT:n % FT + 1]).then_inc(silu_ready, 1)

            def hidden_first(n):
                act.wait_ge(fused_ready, n + 1)
                need(act, down_ready, GB * (n // FT - 1))
                nc.scalar.copy(h_parts[:, n // FT % 2, 0, n % FT, :], fused[:, n % 2]).then_inc(h_first, 1)

            def hidden_second(n):
                act.wait_ge(h_rest_ready, n + 1)
                nc.scalar.copy(h_parts[:, n // FT % 2, 1, n % FT, :], h_rest[:, n % 2]).then_inc(h_second, 1)

            split_first(0)
            split_second(0)
            for n in range(END):
                if n < TILES:
                    silu(n)
                if 1 <= n <= TILES:
                    hidden_second(n - 1)
                if n < TILES:
                    hidden_first(n)
                if group_to_split(n):
                    split_first(group_to_split(n))
                if group_to_split(n - 1):
                    split_second(group_to_split(n - 1))
                if sequence_at(n - 3) is not None:
                    norm.scalar(act, sequence_at(n - 3))
            norm.done(act)

        @block.vector
        def _(dve):
            order = Order(dve, chain)
            dve.wait_ge(loaded, LOADED)
            nc.vector.tensor_copy(w_up[:, 1], w_in[:, 1].bitcast(I8)).then_inc(cast_done, 1)
            nc.vector.tensor_copy(w_down[:], wd_in[:].bitcast(I8)).then_inc(cast_done, 1)

            def split_rest(g):
                dve.wait_ge(x_first, g + 1)
                need(dve, x_split, g)
                nc.vector.tensor_tensor(x_rest[:], keep["xT"][:, :, bass.ts(g, GT)], x_parts[:, g % 2, 0], ALU.subtract).then_inc(x_rest_ready, 1)

            def split_third(g):
                dve.wait_ge(x_second, g + 1)
                nc.vector.tensor_tensor(x_parts[:, g % 2, 2], x_rest[:], x_parts[:, g % 2, 1], ALU.subtract).then_inc(x_split, 1)

            def fuse(n):
                dve.wait_ge(silu_ready, n + 1)
                dve.wait_ge(up_ready, n + 1)
                need(dve, h_first, n - 1)
                nc.vector.scalar_tensor_tensor(fused[:, n % 2], up_ps[:, n % 2], s_in[:, 1, n % FT:n % FT + 1], gate[:, n % 2],
                                               ALU.mult, ALU.mult).then_inc(fused_ready, 1)

            def hidden_rest(n):
                dve.wait_ge(h_first, n + 1)
                nc.vector.tensor_tensor(h_rest[:, n % 2], fused[:, n % 2], h_parts[:, n // FT % 2, 0, n % FT, :], ALU.subtract).then_inc(h_rest_ready, 1)

            def hidden_third(n):
                dve.wait_ge(h_second, n + 1)
                nc.vector.tensor_tensor(h_parts[:, n // FT % 2, 2, n % FT, :], h_rest[:, n % 2], h_parts[:, n // FT % 2, 1, n % FT, :],
                                        ALU.subtract).then_inc(h_split, 1)

            def scale_and_add(b):
                dve.wait_ge(down_ready, b + 1)
                nc.vector.tensor_tensor(y[:], down_ps[:, b % 2, 0:D], s_down[:], ALU.mult).then_inc(y_ready, 1)
                dve.wait_ge(y_ready, b + 1)
                norm.vector_begin(dve, order, b, y[:])

            split_rest(0)
            split_third(0)
            for n in range(END):
                b = sequence_at(n - 1)
                if n < TILES:
                    fuse(n)
                if 1 <= n <= TILES:
                    hidden_third(n - 1)
                if b is not None:
                    scale_and_add(b)
                if n < TILES:
                    hidden_rest(n)
                if group_to_split(n):
                    split_rest(group_to_split(n))
                if group_to_split(n - 1):
                    split_third(group_to_split(n - 1))
                if b is not None:
                    norm.vector_end(dve, b)

        @block.tensor
        def _(pe):
            def up(n):
                g, f = n // FT, n % FT
                if f == 0:
                    pe.wait_ge(x_first, g + 1)
                    pe.wait_ge(x_split, g + 1)
                for k, tile in enumerate((gate_ps, up_ps)):
                    need(pe, silu_ready if k == 0 else fused_ready, n - 1)
                    for c in range(DH):
                        for part in range(PARTS):
                            ins = nc.tensor.matmul(tile[:, n % 2], w_up[:, c, k, f * P:(f + 1) * P], x_parts[:, g % 2, part, c, :],
                                                   start=(c == 0 and part == 0), stop=(c == DH - 1 and part == PARTS - 1))
                    ins.then_inc(up_ready if k else gate_ready, 1)

            def down(b):
                g, j = b // GB, b % GB
                pe.wait_ge(h_split, FT * (g + 1))
                need(pe, y_ready, b - 1)
                for f in range(FT):
                    for part in range(PARTS):
                        ins = nc.tensor.matmul(down_ps[:, b % 2, 0:D], h_parts[:, g % 2, part, f, j * T:(j + 1) * T], w_down[:, f, :],
                                               start=(f == 0 and part == 0), stop=(f == FT - 1 and part == PARTS - 1))
                ins.then_inc(down_ready, 1)

            pe.wait_ge(cast_done, 3)
            for n in range(END):
                if n < TILES:
                    up(n)
                if sequence_at(n) is not None:
                    down(sequence_at(n))
                if sequence_at(n - 3) is not None:
                    norm.tensor(pe, sequence_at(n - 3))


class LatentWeights:

    H, K, DC, DQ, R = 16, 128, 64, 192, 64

    def __init__(self, nc, ctx):
        sb = lambda name, shape: ctx.enter_context(nc.sbuf_tensor(f"mla_{name}", shape, F32))
        H, DC = self.H, self.DC
        self.nc = nc
        self.to_keys = sb("to_keys", [P, DH, H, DC])
        self.to_out = sb("to_out", [P, H // 2, D])
        self.keys = sb("keys", [P, B, 2, T])
        self.values = sb("values", [T, B, DC + 1])

    def open(self, ctx, keep, io, acc):
        nc, H, K, DC, DQ, R = self.nc, self.H, self.K, self.DC, self.DQ, self.R
        sb = lambda name, shape: ctx.enter_context(nc.sbuf_tensor(f"mla_{name}", shape, F32))
        sem = lambda name: new_semaphore(nc, keep, f"mla_{name}")
        self.io, self.acc, self.ident, self.QH = io, acc, keep["ident"], DQ // 2
        first, second = sb("first", [P, H * D]), sb("second", [P, H * D])
        self.qrT = first[0:R, 0:H * DQ].rearrange("p (h d) -> p h d", h=H)
        self.krT = first[0:R, H * DQ:H * D].rearrange("p (h d) -> p h d", h=H)
        self.wq = first[:].rearrange("p (h d) -> p h d", h=H)
        self.kc_qT = second[0:self.QH, :].rearrange("p (c h k) -> p c h k", c=2, h=H)
        self.woT = second[:].rearrange("p (h d) -> p h d", h=H)
        self.t2, self.kc_kv = sb("t2", [K, H, DC]), sb("kc_kv", [K, H, DC])
        self.cosines, self.sines = sb("cosines", [T, DC]), sb("sines", [T, DC])
        self.t1 = self.keys[0:self.QH].rearrange("p b k t -> p (b k t)")[:, 0:2 * H * DC].rearrange("p (c h d) -> p c h d", c=2, h=H)
        out_flat = self.to_out[:].rearrange("p q n -> p (q n)")
        self.kv = out_flat[:, 0:B * DC].rearrange("p (b d) -> p b d", b=B)
        self.turned_kv = out_flat[:, B * DC:2 * B * DC].rearrange("p (b d) -> p b d", b=B)
        self.both = self.to_keys[:].rearrange("p c h d -> p (c h d)").rearrange("p (b k d) -> p b k d", b=B, k=2)
        self.loaded, self.wq_loaded, self.woT_loaded = sem("loaded"), sem("wq_loaded"), sem("woT_loaded")
        self.done, self.copied, self.both_ready, self.chain = sem("job_done"), sem("job_copied"), sem("both_ready"), sem("turn_chain")
        self.zeroed = sem("zeroed")
        self.JOBS = ["t1_0", "t1_1", "t2_0", "keysT_0", "keysT_1", "keys_0", "keys_1", "out_0", "out_1"]

    def sync(self, sp):
        io, K = self.io, self.K
        inputs = ((self.qrT, io["mla_qrT"]), (self.krT, io["mla_krT"]), (self.kc_qT, io["mla_kc_qT"]),
                  (self.kv, io["ctx"].rearrange("b t d -> t b d")), (self.cosines[:], io["cosines"]), (self.sines[:], io["sines"]),
                  (self.kc_kv[:], io["mla_kc_kv"].rearrange("h k d -> k h d")))
        for dst, src in inputs:
            sp.dma_start(dst, src).then_inc(self.loaded, 16)
        self.LOADED = 16 * len(inputs)
        sp.wait_ge(self.done, 2)
        sp.dma_start(self.wq, io["mla_wq"].rearrange("(h k) i -> k h i", k=K)).then_inc(self.wq_loaded, 16)
        sp.wait_ge(self.done, 3)
        sp.dma_start(self.woT, io["mla_woT"].rearrange("(h k) n -> k h n", k=K)).then_inc(self.woT_loaded, 16)

    def tensor(self, pe):
        nc, H, DC = self.nc, self.H, self.DC
        for i, job in enumerate(self.JOBS):
            name, c = job.split("_")
            c = int(c)
            tile = self.acc[:, i % 2]
            per_head = tile.rearrange("p (h d) -> p h d", h=H)
            need(pe, self.copied, i - 1)
            if name == "t1":
                pe.wait_ge(self.loaded, self.LOADED)
                for h in range(H):
                    ins = nc.tensor.matmul(per_head[0:self.QH, h, :], self.qrT[:, h, c * self.QH:(c + 1) * self.QH], self.krT[:, h, :], start=True, stop=True)
            elif name == "t2":
                pe.wait_ge(self.copied, i)
                for h in range(H):
                    for k in range(2):
                        ins = nc.tensor.matmul(per_head[:, h, :], self.kc_qT[:, k, h, :], self.t1[:, k, h, :], start=(k == 0), stop=(k == 1))
            elif name == "keysT":
                pe.wait_ge(self.both_ready, 1)
                for b in range(B // 2):
                    ins = nc.tensor.transpose(tile[:, b * T:(b + 1) * T], self.both[:, c * B // 2 + b].rearrange("p k d -> p (k d)"), self.ident[:])
            elif name == "keys":
                pe.wait_ge(self.wq_loaded, 16)
                for h in range(H):
                    ins = nc.tensor.matmul(per_head[:, h, :], self.wq[:, h, c * P:(c + 1) * P], self.t2[:, h, :], start=True, stop=True)
            else:
                pe.wait_ge(self.woT_loaded, 16)
                per_pair = tile.rearrange("p (q n) -> p q n", q=H // 4)
                for h in range(c * H // 2, (c + 1) * H // 2):
                    r = (h % 2) * DC
                    ins = nc.tensor.matmul(per_pair[r:r + DC, (h - c * H // 2) // 2, :], self.kc_kv[:, h, :], self.woT[:, h, :], start=True, stop=True)
            ins.then_inc(self.done, 1)

    def scalar(self, act, start, stop):
        nc, H, DC = self.nc, self.H, self.DC
        for i in range(start, stop):
            name, c = self.JOBS[i].split("_")
            c = int(c)
            tile = self.acc[:, i % 2]
            act.wait_ge(self.done, i + 1)
            if name == "t1":
                ins = nc.scalar.copy(self.t1[:, c].rearrange("p h d -> p (h d)"), tile[0:self.QH])
            elif name == "t2":
                ins = nc.scalar.copy(self.t2[:].rearrange("p h d -> p (h d)"), tile)
            elif name == "keysT":
                act.wait_ge(self.zeroed, 2)
                turned = tile.rearrange("p (b t) -> p b t", b=B // 2)
                for k in range(2):
                    rows = slice(k * DC, (k + 1) * DC)
                    ins = nc.scalar.copy(self.keys[rows, c * B // 2:(c + 1) * B // 2, k, :], turned[rows])
            elif name == "keys":
                ins = nc.scalar.copy(self.to_keys[:, c].rearrange("p h d -> p (h d)"), tile)
            else:
                ins = nc.scalar.copy(self.to_out[:, c * H // 4:(c + 1) * H // 4].rearrange("p q n -> p (q n)"), tile)
            ins.then_inc(self.copied, 1)

    def gpsimd(self, pool):
        nc, DC = self.nc, self.DC
        HALF = DC // 2
        order = Order(pool, self.chain)
        order(nc.gpsimd.memset(self.values[:, :, DC:DC + 1], 1.0))
        pool.wait_ge(self.loaded, self.LOADED)
        per_b = lambda table, lo, hi: table[:, lo:hi].unsqueeze(1).to_broadcast([T, B, hi - lo])
        order(nc.gpsimd.tensor_tensor(self.values[:, :, 0:DC], self.kv, per_b(self.cosines, 0, DC), ALU.mult))
        order(nc.gpsimd.tensor_tensor(self.turned_kv[:, :, 0:HALF], self.kv[:, :, HALF:DC], per_b(self.sines, 0, HALF), ALU.mult))
        order(nc.gpsimd.tensor_tensor(self.turned_kv[:, :, HALF:DC], self.kv[:, :, 0:HALF], per_b(self.sines, HALF, DC), ALU.mult))
        order(nc.gpsimd.tensor_tensor(self.values[:, :, 0:DC], self.values[:, :, 0:DC], self.turned_kv, ALU.add))
        nc.gpsimd.tensor_copy(self.both, self.values[:, :, 0:DC].unsqueeze(2).to_broadcast([T, B, 2, DC])).then_inc(self.both_ready, 1)
        pool.wait_ge(self.both_ready, 1)
        pool.wait_ge(self.done, 3)
        nc.gpsimd.memset(self.keys[0:DC, :, 1, :], 0.0).then_inc(self.zeroed, 1)
        pool.wait_ge(self.zeroed, 1)
        nc.gpsimd.memset(self.keys[DC:P, :, 0, :], 0.0).then_inc(self.zeroed, 1)


def batch_axis_attention(nc, keep, io, latent):
    H = 16
    HD = D // H
    L = B
    MASKED = -10000.0
    with ExitStack() as ctx:
        sb = lambda name, shape: ctx.enter_context(nc.sbuf_tensor(f"bat_{name}", shape, F32))
        ps = lambda name, shape: ctx.enter_context(nc.psum_tensor(f"bat_{name}", shape, F32))
        sem = lambda name: new_semaphore(nc, keep, f"bat_{name}")
        w_qkv = sb("w_qkv", [P, DH, 3 * D])
        row_stats = sb("row_stats", [T, 3 * D])
        b_qkv = row_stats[0:1, :]
        row_max, row_sum = row_stats[:, 0:L * H], row_stats[:, L * H:2 * L * H]
        w_out = sb("w_out", [P, DH, D])
        b_out = sb("b_out", [1, D])
        ones = sb("ones", [1, T])
        x_feat = sb("x_feat", [P, 2, DH, T])
        q, k, v = sb("q", [T, L, D]), sb("k", [T, L, D]), sb("v", [T, L, D])
        prod = sb("prod", [T, L, D])
        s = sb("s", [T, L, H, L])
        later = k
        weighted = (q, prod)
        attT = sb("attT", [P, 2, D])
        qkv_ps = ps("qkv_ps", [T, 2, 1024])
        attT_ps, out_norm_ps = ps("attT_ps", [P, 2, 512]), ps("out_norm_ps", [T, 2, 512])
        out_ps, normT = out_norm_ps[:, 0, 0:D], out_norm_ps[:, 1, 0:D]
        loaded, ones_set, x_ready, qkv_ready, qkv_copied = sem("loaded"), sem("ones_set"), sem("x_ready"), sem("qkv_ready"), sem("qkv_copied")
        shifted, exp_ready, weighted_ready, attT_ready, attT_copied, out_ready = (
            sem("shifted"), sem("exp_ready"), sem("weighted_ready"), sem("attT_ready"), sem("attT_copied"), sem("out_ready"))
        chain = sem("chain")
        norm = Norm(nc, ctx, "ba_n", keep, normT)
        latent.open(ctx, keep, io, qkv_ps)

        block = ctx.enter_context(nc.Block())

        @block.sync
        def _(sp):
            sp.dma_start(w_qkv[:], io["ba_w_qkv"].rearrange("(c p) o -> p c o", p=P)).then_inc(loaded, 16)
            sp.dma_start(b_qkv, io["ba_b_qkv"].unsqueeze(0)).then_inc(loaded, 16)
            sp.dma_start(w_out[:], io["ba_w_out"].rearrange("(c p) o -> p c o", p=P)).then_inc(loaded, 16)
            sp.dma_start(b_out[:], io["ba_b_out"].unsqueeze(0)).then_inc(loaded, 16)
            latent.sync(sp)

        @block.gpsimd
        def _(pool):
            nc.gpsimd.memset(ones[:], 1.0).then_inc(ones_set, 1)

            def step(l, par, pair):
                need(pool, qkv_ready, l - 1)
                nc.gpsimd.tensor_copy(x_feat[:, par], keep["xT"][:, :, bass.ts(l, T)]).then_inc(x_ready, 1)
            each_sequence(pool, step)
            latent.gpsimd(pool)
            with pool.Fori(0, L) as l:
                norm.gpsimd(pool, l)

        @block.tensor
        def _(pe):
            pe.wait_ge(loaded, 4 * 16)
            pe.wait_ge(ones_set, 1)

            def project(l, par, pair):
                need(pe, x_ready, l + 1)
                need(pe, qkv_copied, l - 1)
                for lo, n in ((0, 512), (512, 256)):
                    for c in range(DH):
                        nc.tensor.matmul(qkv_ps[:, par, lo:lo + n], x_feat[:, par, c, :], w_qkv[:, c, lo:lo + n],
                                         start=(c == 0), stop=False)
                    ins = nc.tensor.matmul(qkv_ps[:, par, lo:lo + n], ones[:], b_qkv[:, lo:lo + n], start=False, stop=True)
                ins.then_inc(qkv_ready, 1)
            each_sequence(pe, project)
            pe.wait_ge(qkv_copied, L)
            latent.tensor(pe)

            def add_up(l):
                pe.wait_ge(weighted_ready, l + 1)
                need(pe, attT_copied, l - 1)
                slots = min(l + 2, L)
                for c in range(DH):
                    for j in range(slots):
                        ins = nc.tensor.matmul(attT_ps[:, l % 2, c * T:(c + 1) * T], weighted[l % 2][:, j, c * P:(c + 1) * P], keep["ident"][:],
                                               start=(j == 0), stop=(j == slots - 1))
                ins.then_inc(attT_ready, 1)

            def out(l):
                pe.wait_ge(attT_copied, l + 1)
                need(pe, norm.var_ready, l)
                for c in range(DH):
                    nc.tensor.matmul(out_ps, attT[:, l % 2, c * T:(c + 1) * T], w_out[:, c, :], start=(c == 0), stop=False)
                nc.tensor.matmul(out_ps, ones[:], b_out[:], start=False, stop=True).then_inc(out_ready, 1)

            for l in range(L):
                if l >= 3:
                    norm.tensor(pe, l - 3)
                add_up(l)
                if l >= 1:
                    out(l - 1)
            out(L - 1)
            for l in range(L - 3, L):
                norm.tensor(pe, l)

        @block.scalar
        def _(act):
            def copy_qkv(l, par, pair):
                need(act, qkv_ready, l + 1)
                nc.scalar.mul(q[:, l, :], qkv_ps[:, par, 0:D], HD ** -0.5)
                nc.scalar.copy(k[:, l, :], qkv_ps[:, par, D:2 * D])
                nc.scalar.copy(v[:, l, :], qkv_ps[:, par, 2 * D:3 * D]).then_inc(qkv_copied, 1)
            each_sequence(act, copy_qkv)
            latent.scalar(act, 0, 7)
            act.wait_ge(shifted, 1)
            nc.scalar.activation(s[:], s[:], ACT.Exp).then_inc(exp_ready, 1)
            latent.scalar(act, 7, len(latent.JOBS))
            for l in range(L):
                if l >= 3:
                    norm.scalar(act, l - 3)
                act.wait_ge(attT_ready, l + 1)
                need(act, out_ready, l - 1)
                nc.scalar.copy(attT[:, l % 2, :], attT_ps[:, l % 2, 0:D]).then_inc(attT_copied, 1)
            for l in range(L - 3, L):
                norm.scalar(act, l)
            norm.done(act)

        @block.vector
        def _(dve):
            order = Order(dve, chain)
            by_head = lambda t: t.rearrange("p (h d) -> p h d", h=H)
            order(nc.vector.memset(s[:], MASKED))
            for l in range(L):
                dve.wait_ge(qkv_copied, l + 1)
                order(nc.vector.tensor_tensor(prod[:, 0:l + 1, :], k[:, 0:l + 1, :],
                                              q[:, l, :].unsqueeze(1).to_broadcast([T, l + 1, D]), ALU.mult))
                order(nc.vector.tensor_reduce(s[:, l, :, 0:l + 1].rearrange("p h k -> p k h"),
                                              prod[:, 0:l + 1, :].rearrange("p k (h d) -> p k h d", h=H), AX_X, ALU.add))
            rows = s[:].rearrange("p l h k -> p (l h) k")
            order(nc.vector.tensor_reduce(row_max, rows, AX_X, ALU.max))
            nc.vector.tensor_tensor(rows, rows, row_max.unsqueeze(2).to_broadcast([T, L * H, L]), ALU.subtract).then_inc(shifted, 1)
            order(nc.vector.tensor_copy(later[:, L - 2, :], v[:, L - 1, :]))
            for l in range(L - 3, -1, -1):
                order(nc.vector.tensor_tensor(later[:, l, :], later[:, l + 1, :], v[:, l + 1, :], ALU.add))
            dve.wait_ge(exp_ready, 1)
            order(nc.vector.tensor_reduce(row_sum, rows, AX_X, ALU.add))
            order(nc.vector.reciprocal(row_sum, row_sum))
            order(nc.vector.tensor_tensor(rows, rows, row_sum.unsqueeze(2).to_broadcast([T, L * H, L]), ALU.mult))

            def weigh(l):
                need(dve, attT_ready, l - 1)
                buf = weighted[l % 2]
                if l < L - 1:
                    nc.vector.tensor_tensor(by_head(buf[:, l + 1, :]), by_head(later[:, l, :]),
                                            s[:, l, :, L - 1].unsqueeze(2).to_broadcast([T, H, HD]), ALU.mult)
                v_h = v[:, 0:l + 1, :].rearrange("p k (h d) -> p k h d", h=H)
                p_h = s[:, l, :, 0:l + 1].rearrange("p h k -> p k h").unsqueeze(3).to_broadcast([T, l + 1, H, HD])
                nc.vector.tensor_tensor(buf[:, 0:l + 1, :].rearrange("p k (h d) -> p k h d", h=H), v_h, p_h, ALU.mult).then_inc(weighted_ready, 1)

            def add_norm(l):
                dve.wait_ge(out_ready, l + 1)
                norm.vector(dve, order, l, out_ps)

            for l in range(L):
                weigh(l)
                if l >= 2:
                    add_norm(l - 2)
            for l in range(L - 2, L):
                add_norm(l)


def latent_cross_attention(nc, keep, io, latent):
    H, DC = latent.H, latent.DC
    UH = 4
    U = H // UH
    PAIRS = H // 2
    to_keys, to_out, keys, values = latent.to_keys, latent.to_out, latent.keys, latent.values
    with ExitStack() as ctx:
        sb = lambda name, shape: ctx.enter_context(nc.sbuf_tensor(f"mla_{name}", shape, F32))
        sem = lambda name: new_semaphore(nc, keep, f"mla_{name}")

        ps = lambda name, shape: ctx.enter_context(nc.psum_tensor(f"mla_{name}", shape, F32))
        q_feat = sb("q_feat", [P, 2, PAIRS, T])
        NB = 4
        probs, probsT, row_max = sb("probs", [T, NB, UH, T]), sb("probsT", [T, NB, UH, T]), sb("row_max", [T, NB, UH])
        rsum = sb("rsum", [T, NB, UH])
        attended = sb("attended", [T, 2, H, DC])
        attT = sb("attT", [P, 2, PAIRS, T])
        scores, turned = ps("scores", [T, 2, UH, T]), ps("turned", [T, 2, UH, T])
        weighted = ps("weighted", [T, UH, DC + 1])
        shared = ps("shared", [P, PAIRS // 2, T])
        out_ps, normT = ps("out_ps", [T, D]), ps("normT", [P, D])
        q_done, q_copied, scores_ready, shifted, exp_ready = sem("q_done"), sem("q_copied"), sem("scores_ready"), sem("shifted"), sem("exp_ready")
        turn_ready, turn_copied, weigh_ready, scaled = sem("turn_ready"), sem("turn_copied"), sem("weigh_ready"), sem("scaled")
        attT_ready, attT_copied, out_ready, chain = sem("attT_ready"), sem("attT_copied"), sem("out_ready"), sem("chain")
        norm = Norm(nc, ctx, "mla_n", keep, normT)
        TURN_LAG, WEIGH_LAG = 1, 2
        block = ctx.enter_context(nc.Block())

        @block.gpsimd
        def _(pool):
            with pool.Fori(0, B) as b:
                norm.gpsimd(pool, b)

        @block.tensor
        def _(pe):
            def project(b, r):
                if r == 0:
                    need(pe, attT_copied, 2 * (b - 1))
                else:
                    need(pe, q_copied, 2 * b + 1)
                for k in range(PAIRS // 2):
                    pair = r * PAIRS // 2 + k
                    for c in range(DH):
                        ins = nc.tensor.matmul(shared[:, k, :], to_keys[:, c, 2 * pair:2 * pair + 2, :], keep["xT"][:, c, bass.ts(b, T)],
                                               start=(c == 0), stop=(c == DH - 1))
                ins.then_inc(q_done, 1)

            def score(b, par, u):
                if u % 2 == 0:
                    need(pe, q_copied, 2 * b + u // 2 + 1)
                need(pe, shifted, U * b + u - 1)
                for k in range(UH // 2):
                    ins = nc.tensor.matmul(scores[:, u % 2, 2 * k:2 * k + 2, :], q_feat[:, par, u * UH // 2 + k, :], keys[:, b, :, :],
                                           start=True, stop=True)
                ins.then_inc(scores_ready, 1)

            def turn(b, par, u):
                need(pe, exp_ready, U * b + u + 1)
                need(pe, turn_copied, U * b + u - 1)
                for h in range(UH):
                    ins = nc.tensor.transpose(turned[:, u % 2, h, :], probs[:, u % NB, h, :], keep["ident"][:])
                ins.then_inc(turn_ready, 1)

            def weigh(b, par, u):
                need(pe, turn_copied, U * b + u + 1)
                need(pe, scaled, U * b + u)
                for h in range(UH):
                    ins = nc.tensor.matmul(weighted[:, h, :], probsT[:, u % NB, h, :], values[:, b, :], start=True, stop=True)
                ins.then_inc(weigh_ready, 1)

            def turn_out(b, par, r):
                if r == 0:
                    need(pe, q_copied, 2 * b + 4)
                    need(pe, scaled, U * (b + 1))
                else:
                    need(pe, attT_copied, 2 * b + 1)
                for k in range(PAIRS // 2):
                    pair = r * PAIRS // 2 + k
                    ins = nc.tensor.transpose(shared[:, k, :], attended[:, par, 2 * pair:2 * pair + 2, :].rearrange("p h d -> p (h d)"),
                                              keep["ident"][:])
                ins.then_inc(attT_ready, 1)

            def project_out(b, par):
                need(pe, attT_copied, 2 * b + 2)
                need(pe, norm.var_ready, b)
                for k in range(PAIRS):
                    ins = nc.tensor.matmul(out_ps[:], attT[:, par, k, :], to_out[:, k, :], start=(k == 0), stop=(k == PAIRS - 1))
                ins.then_inc(out_ready, 1)

            def step(b, par, pair):
                rest = not first(b)
                project(b, 0)
                if rest:
                    turn(b - 1, 1 - par, U - 1)
                    weigh(b - 1, 1 - par, U - 2)
                project(b, 1)
                score(b, par, 0)
                if rest:
                    weigh(b - 1, 1 - par, U - 1)
                score(b, par, 1)
                turn(b, par, 0)
                if rest:
                    turn_out(b - 1, 1 - par, 0)
                score(b, par, 2)
                if rest:
                    turn_out(b - 1, 1 - par, 1)
                turn(b, par, 1)
                weigh(b, par, 0)
                score(b, par, 3)
                if rest:
                    project_out(b - 1, 1 - par)
                turn(b, par, 2)
                weigh(b, par, 1)
                if rest:
                    norm.tensor(pe, b - 1)
            each_sequence(pe, step)
            last = B - 1
            turn(last, 1, U - 1)
            weigh(last, 1, U - 2)
            weigh(last, 1, U - 1)
            pe.wait_ge(scaled, U * B)
            for r in range(2):
                if r:
                    pe.wait_ge(attT_copied, 2 * last + 1)
                for k in range(PAIRS // 2):
                    q = r * PAIRS // 2 + k
                    ins = nc.tensor.transpose(shared[:, k, :], attended[:, 1, 2 * q:2 * q + 2, :].rearrange("p h d -> p (h d)"), keep["ident"][:])
                ins.then_inc(attT_ready, 1)
            project_out(last, 1)
            norm.tensor(pe, last)

        @block.scalar
        def _(act):
            def copy_q(b, par, r):
                need(act, q_done, 2 * b + r + 1)
                need(act, scores_ready, U * (b - 1))
                nc.scalar.copy(q_feat[:, par, r * PAIRS // 2:(r + 1) * PAIRS // 2, :], shared[:]).then_inc(q_copied, 1)

            def exp(b, u):
                need(act, shifted, U * b + u + 1)
                nc.scalar.activation(probs[:, u % NB], probs[:, u % NB], ACT.Exp).then_inc(exp_ready, 1)

            def copy_turned(b, u):
                need(act, turn_ready, U * b + u + 1)
                need(act, weigh_ready, U * b + u + 1 - NB)
                nc.scalar.copy(probsT[:, u % NB], turned[:, u % 2]).then_inc(turn_copied, 1)

            def copy_out(b, par, r):
                need(act, attT_ready, 2 * b + r + 1)
                nc.scalar.copy(attT[:, par, r * PAIRS // 2:(r + 1) * PAIRS // 2, :], shared[:]).then_inc(attT_copied, 1)

            def step(b, par, pair):
                rest = not first(b)
                copy_q(b, par, 0)
                if rest:
                    copy_turned(b - 1, U - 1)
                copy_q(b, par, 1)
                exp(b, 0)
                exp(b, 1)
                copy_turned(b, 0)
                if rest:
                    copy_out(b - 1, 1 - par, 0)
                    copy_out(b - 1, 1 - par, 1)
                copy_turned(b, 1)
                exp(b, 2)
                exp(b, 3)
                copy_turned(b, 2)
                if rest:
                    norm.scalar(act, b - 1)
            each_sequence(act, step)
            copy_turned(B - 1, U - 1)
            copy_out(B - 1, 1, 0)
            copy_out(B - 1, 1, 1)
            norm.scalar(act, B - 1)
            norm.done(act)

        @block.vector
        def _(dve):
            order = Order(dve, chain)

            def shift(b, u):
                need(dve, scores_ready, U * b + u + 1)
                order(nc.vector.tensor_reduce(row_max[:, u % NB], scores[:, u % 2], AX_X, ALU.max))
                need(dve, turn_ready, U * b + u + 1 - NB)
                nc.vector.tensor_tensor(probs[:, u % NB], scores[:, u % 2], row_max[:, u % NB].unsqueeze(2).to_broadcast([T, UH, T]),
                                        ALU.subtract).then_inc(shifted, 1)

            def scale(b, par, u):
                need(dve, weigh_ready, U * b + u + 1)
                order(nc.vector.reciprocal(rsum[:, u % NB], weighted[:, :, DC]))
                nc.vector.tensor_tensor(attended[:, par, u * UH:(u + 1) * UH, :], weighted[:, :, 0:DC],
                                        rsum[:, u % NB].unsqueeze(2).to_broadcast([T, UH, DC]), ALU.mult).then_inc(scaled, 1)

            def step(b, par, pair):
                rest = not first(b)
                if rest:
                    scale(b - 1, 1 - par, U - 2)
                shift(b, 0)
                if rest:
                    scale(b - 1, 1 - par, U - 1)
                shift(b, 1)
                shift(b, 2)
                scale(b, par, 0)
                shift(b, 3)
                if rest:
                    need(dve, out_ready, b)
                    norm.vector(dve, order, b - 1, out_ps[:])
                scale(b, par, 1)
            each_sequence(dve, step, order, per=2 * (2 * U + norm.CHAIN - 1))
            scale(B - 1, 1, U - 2)
            scale(B - 1, 1, U - 1)
            dve.wait_ge(out_ready, B)
            norm.vector(dve, order, B - 1, out_ps[:])



def mixture_of_experts(nc, keep, io, out):
    E, G, TOPK, TOPG, CAP, F, SCALE = 64, 8, 6, 4, 48, 96, 2.5
    EG = E // G
    N = B * T
    BIG = 1e30
    W = D + E
    PAIRS = E // 2
    SLOTS = 64
    ROUNDS = CAP // 8
    with ExitStack() as ctx:
        sb = lambda name, shape, dt=F32: ctx.enter_context(nc.sbuf_tensor(f"moe_{name}", shape, dt))
        sem = lambda name: new_semaphore(nc, keep, f"moe_{name}")
        table = nc.dram_tensor("moe_table", [N + P, W], F32, kind="Internal").ap()
        sums = [nc.dram_tensor(f"moe_sums_{k}", [N + P, D], F32, kind="Internal").ap() for k in range(2)]
        rows = sb("rows", [P, PAIRS], U32)
        rows_of = sb("rows_of", [SLOTS, E], U32)
        NW = 18
        w_gu, w_dn = sb("w_gu", [P, NW, 2, DH, 2 * F]), sb("w_dn", [F, NW, 2, D])
        w_loaded = [sem(f"w_loaded{k}") for k in range(NW)]

        def load_experts(sp, q):
            sp.dma_start(w_gu[:, q % NW], io["moe_w_gu"][q]).then_inc(w_loaded[q % NW], 16)
            sp.dma_start(w_dn[:, q % NW], io["moe_w_down"][q]).then_inc(w_loaded[q % NW], 16)

        with ExitStack() as inner:
            sbi = lambda name, shape, dt=F32: inner.enter_context(nc.sbuf_tensor(f"moe_{name}", shape, dt))
            psi = lambda name, shape: inner.enter_context(nc.psum_tensor(f"moe_{name}", shape, F32))
            w_route, bias = sbi("w_route", [P, DH, E]), sbi("bias", [P, E])
            ws_gu, ws_down = sbi("ws_gu", [P, DH, 2 * F]), sbi("ws_down", [F, D])
            not_first, lower = sbi("not_first", [P, B * E]), sbi("lower", [P, G * G])
            countdown, slot_no = sbi("countdown", [P, B]), sbi("slot_no", [P, 1])
            zeros = sbi("zeros", [P, W])
            score, biased, work, chosen = sbi("score", [T, B, E]), sbi("biased", [T, B, E]), sbi("work", [T, B, E]), sbi("chosen", [T, B, E])
            equal, prefix, pick = sbi("equal", [T, B, E]), sbi("prefix", [T, B * E]), sbi("pick", [T, B, E])
            best, count, second = sbi("best", [T, B * G]), sbi("count", [T, B * G]), sbi("second", [T, B * G])
            group_score, group_in = sbi("group_score", [T, B * G]), sbi("group_in", [T, B * G])
            ahead, tied = sbi("ahead", [T, B, G, G]), sbi("tied", [T, B, G, G])
            top8, above, total = sbi("top8", [T, B, 8]), sbi("above", [T, B]), sbi("total", [T, B])
            weights = sbi("weights", [T, B, E])
            order_key = sbi("order_key", [T, B, E])
            left = sbi("left", [P, 2, N // 2])
            top, merged, merged_left = sbi("top", [P, CAP]), sbi("merged", [E, 2, CAP]), sbi("merged_left", [E, 2, 2 * CAP])
            twice = sbi("twice", [E, P])
            row_f, empty = sbi("row_f", [P, E]), sbi("empty", [P, E])
            gate, up, hT = sbi("gate", [F, 2, 512]), sbi("up", [F, 2, 512]), sbi("hT", [F, N])
            shared_y = sbi("shared_y", [T, 2, D])
            logits = psi("logits", [T, B, E])
            keysT = psi("keysT", [P, N // 2])
            shared_gate, shared_up = psi("shared_gate", [P, 512]), psi("shared_up", [P, 512])
            shared_out = psi("shared_out", [T, 2, 512])
            loaded, zero_set, logits_ready, score_ready = sem("loaded"), sem("zero_set"), sem("logits_ready"), sem("score_ready")
            key_ready, keyT_ready, twice_ready, twiceT_ready = sem("key_ready"), sem("keyT_ready"), sem("twice_ready"), sem("twiceT_ready")
            weights_ready, stored, tokens_stored, rows_ready = sem("weights_ready"), sem("stored"), sem("tokens_stored"), sem("rows_ready")
            gate_ps_ready, up_copied, h_done, down_done, added = sem("gate_ps_ready"), sem("up_copied"), sem("h_done"), sem("down_done"), sem("added")
            down_copied = sem("down_copied")
            chain = sem("route_chain")
            block = inner.enter_context(nc.Block())

            @block.sync
            def _(sp):
                for dst, src in ((w_route, io["moe_w_route"].rearrange("(c p) e -> p c e", p=P)), (bias, io["moe_bias"].unsqueeze(0).to_broadcast([P, E])),
                                 (not_first, io["moe_not_first"].unsqueeze(0).to_broadcast([P, B * E])),
                                 (lower, io["moe_lower"].unsqueeze(0).to_broadcast([P, G * G])),
                                 (countdown, io["moe_countdown"]), (slot_no, io["moe_slot_no"]),
                                 (ws_gu, io["moe_ws_gu"].rearrange("(c p) f -> p c f", p=P)), (ws_down, io["moe_ws_down"])):
                    sp.dma_start(dst[:], src).then_inc(loaded, 16)
                sp.dma_start(table[0:N, 0:D].rearrange("(b t) d -> t b d", t=T), keep["x_tok"][:]).then_inc(tokens_stored, 16)
                sp.wait_ge(zero_set, 1)
                sp.dma_start(table[N:N + P, :], zeros[:]).then_inc(stored, 16)
                for k in range(2):
                    sp.dma_start(sums[k].rearrange("(b t) d -> t b d", t=T), zeros[:, 0:D].unsqueeze(1).to_broadcast([P, B + 1, D])).then_inc(stored, 16)
                for q in range(NW):
                    load_experts(sp, q)
                sp.wait_ge(weights_ready, 1)
                sp.dma_start(table[0:N, D:W].rearrange("(b t) e -> t b e", t=T), weights[:]).then_inc(stored, 16)
                sp.wait_ge(stored, 4 * 16)
                sp.wait_ge(tokens_stored, 16)

            LOADED = 8 * 16

            @block.tensor
            def _(pe):
                pe.wait_ge(loaded, LOADED)
                for b in range(B):
                    for c in range(DH):
                        ins = nc.tensor.matmul(logits[:, b, :], keep["xT"][:, c, b * T:(b + 1) * T], w_route[:, c, :], start=(c == 0), stop=(c == DH - 1))
                ins.then_inc(logits_ready, 1)
                for g in range(4):
                    if g:
                        pe.wait_ge(up_copied, g)
                    for k, tile in enumerate((shared_gate, shared_up)):
                        for c in range(DH):
                            ins = nc.tensor.matmul(tile[0:F, :], ws_gu[:, c, k * F:(k + 1) * F], keep["xT"][:, c, g * 512:(g + 1) * 512],
                                                   start=(c == 0), stop=(c == DH - 1))
                    ins.then_inc(gate_ps_ready, 1)
                for b in range(B):
                    pe.wait_ge(h_done, b // 4 + 1)
                    if b > 1:
                        pe.wait_ge(down_copied, b - 1)
                    nc.tensor.matmul(shared_out[:, b % 2, 0:D], hT[:, b * T:(b + 1) * T], ws_down[:], start=True, stop=True).then_inc(down_done, 1)
                pe.wait_ge(key_ready, 1)
                for k in range(B // 2):
                    ins = nc.tensor.transpose(keysT[:, k * T:(k + 1) * T], order_key[:, 2 * k:2 * k + 2, :].rearrange("p b e -> p (b e)"), keep["ident"][:])
                ins.then_inc(keyT_ready, 1)
                pe.wait_ge(twice_ready, 1)
                nc.tensor.transpose(logits[:, 0, :], twice[:], keep["ident"][0:E, 0:E]).then_inc(twiceT_ready, 1)
            @block.gpsimd
            def _(pool):
                for g in range(4):
                    pool.wait_ge(up_copied, g + 1)
                    nc.gpsimd.tensor_tensor(hT[:, g * 512:(g + 1) * 512], up[:, g % 2], gate[:, g % 2], ALU.mult).then_inc(h_done, 1)
                pool.wait_ge(tokens_stored, 16)
                for b in range(B):
                    pool.wait_ge(down_copied, b + 1)
                    nc.gpsimd.tensor_tensor(keep["x_tok"][:, b, :], shared_y[:, b % 2], keep["x_tok"][:, b, :], ALU.add).then_inc(added, 1)

            @block.scalar
            def _(act):
                act.wait_ge(logits_ready, 1)
                nc.scalar.activation(score[:], logits[:], ACT.Sigmoid).then_inc(score_ready, 1)
                for g in range(4):
                    act.wait_ge(gate_ps_ready, g + 1)
                    if g > 1:
                        act.wait_ge(h_done, g - 1)
                    nc.scalar.activation(gate[:, g % 2], shared_gate[0:F, :], ACT.Silu)
                    nc.scalar.copy(up[:, g % 2], shared_up[0:F, :]).then_inc(up_copied, 1)
                for b in range(B):
                    act.wait_ge(down_done, b + 1)
                    if b > 1:
                        act.wait_ge(added, b - 1)
                    nc.scalar.copy(shared_y[:, b % 2], shared_out[:, b % 2, 0:D]).then_inc(down_copied, 1)

            @block.vector
            def _(dve):
                order = Order(dve, chain)
                tt, ts, tr = nc.vector.tensor_tensor, nc.vector.tensor_scalar, nc.vector.tensor_reduce
                stt = nc.vector.scalar_tensor_tensor
                nc.vector.memset(zeros[:], 0.0).then_inc(zero_set, 1)
                dve.wait_ge(loaded, LOADED)
                dve.wait_ge(score_ready, 1)
                by_group = lambda t: t[:].rearrange("p b (g e) -> p (b g) e", g=G)
                wide = lambda t, n: t[:].unsqueeze(2).to_broadcast([T, t.shape[1], n])
                order(tt(biased[:], score[:], bias[:].unsqueeze(1).to_broadcast([T, B, E]), ALU.add))
                order(tr(best[:], by_group(biased), AX_X, ALU.max))
                order(tt(by_group(equal), by_group(biased), wide(best, EG), ALU.is_equal))
                order(tr(count[:], by_group(equal), AX_X, ALU.add))
                order(stt(work[:].rearrange("p b e -> p (b e)"), equal[:].rearrange("p b e -> p (b e)"), -BIG, biased[:].rearrange("p b e -> p (b e)"), ALU.mult, ALU.add))
                order(tr(second[:], by_group(work), AX_X, ALU.max))
                order(ts(count[:], count[:], 2.0, -BIG, ALU.is_lt, ALU.mult))
                order(tt(count[:], count[:], best[:], ALU.add))
                order(tt(second[:], second[:], count[:], ALU.max))
                order(tt(group_score[:], best[:], second[:], ALU.add))
                gs = group_score[:].rearrange("p (b g) -> p b g", g=G)
                mine, others = gs.unsqueeze(3).to_broadcast([T, B, G, G]), gs.unsqueeze(2).to_broadcast([T, B, G, G])
                order(tt(ahead[:], others, mine, ALU.is_gt))
                order(tt(tied[:], others, mine, ALU.is_equal))
                order(tt(tied[:].rearrange("p b g h -> p b (g h)"), tied[:].rearrange("p b g h -> p b (g h)"),
                         lower[:].unsqueeze(1).to_broadcast([T, B, G * G]), ALU.mult))
                order(tt(ahead[:], ahead[:], tied[:], ALU.add))
                order(tr(group_in[:], ahead[:].rearrange("p b g h -> p (b g) h"), AX_X, ALU.add))
                order(ts(group_in[:], group_in[:], float(TOPG), None, ALU.is_lt))
                order(tt(by_group(work), by_group(biased), wide(group_in, EG), ALU.mult))
                order(ts(group_in[:], group_in[:], 1.0, BIG, ALU.subtract, ALU.mult))
                order(tt(by_group(work), by_group(work), wide(group_in, EG), ALU.add))
                for b in range(B):
                    ins = nc.vector.max(top8[:, b, :], work[:, b, :])
                order(ins)
                sixth = top8[:, :, TOPK - 1].unsqueeze(2).to_broadcast([T, B, E])
                order(tt(pick[:], work[:], sixth, ALU.is_gt))
                order(tt(equal[:], work[:], sixth, ALU.is_equal))
                order(tr(above[:], pick[:], AX_X, ALU.add))
                order(nc.vector.tensor_tensor_scan(prefix[:], not_first[:], equal[:].rearrange("p b e -> p (b e)"), 0.0, ALU.mult, ALU.add))
                pre = prefix[:].rearrange("p (b e) -> p b e", b=B)
                order(tt(pre, pre, wide(above, E), ALU.add))
                order(stt(equal[:].rearrange("p b e -> p (b e)"), prefix[:], float(TOPK), equal[:].rearrange("p b e -> p (b e)"), ALU.is_le, ALU.mult))
                order(tt(chosen[:], pick[:], equal[:], ALU.add))
                tt(order_key[:], chosen[:], wide(countdown, E), ALU.mult).then_inc(key_ready, 1)
                order(tt(work[:], score[:], chosen[:], ALU.mult))
                order(tr(total[:], work[:], AX_X, ALU.add))
                order(nc.vector.reciprocal(total[:], total[:]))
                order(ts(total[:], total[:], SCALE, None, ALU.mult))
                tt(weights[:], work[:], wide(total, E), ALU.mult).then_inc(weights_ready, 1)
                dve.wait_ge(keyT_ready, 1)
                src = keysT[:]
                for r in range(ROUNDS):
                    order(nc.vector.max(top[:, 8 * r:8 * r + 8], src))
                    if r < ROUNDS - 1:
                        order(nc.vector.match_replace(left[:, r % 2, :], top[:, 8 * r:8 * r + 8], src, 0.0))
                        src = left[:, r % 2, :]
                order(nc.vector.tensor_copy(merged[:, 0, :], top[0:E, :]))
                order(nc.vector.tensor_copy(merged[:, 1, :], top[E:P, :]))
                order(nc.vector.memset(twice[:], 0.0))
                src = merged[:].rearrange("p k s -> p (k s)")
                for r in range(ROUNDS):
                    order(nc.vector.max(twice[:, 8 * r:8 * r + 8], src))
                    if r < ROUNDS - 1:
                        order(nc.vector.match_replace(merged_left[:, r % 2, :], twice[:, 8 * r:8 * r + 8], src, 0.0))
                        src = merged_left[:, r % 2, :]
                nc.vector.tensor_copy(twice[:, SLOTS:SLOTS + CAP], twice[:, 0:CAP]).then_inc(twice_ready, 1)
                dve.wait_ge(twiceT_ready, 1)
                order(ts(row_f[:], logits[:, 0, :], -1.0, float(N), ALU.mult, ALU.add))
                order(ts(empty[:], logits[:, 0, :], 0.0, slot_no[:], ALU.is_equal, ALU.mult))
                order(tt(row_f[:], row_f[:], empty[:], ALU.add))
                turned = row_f[:].rearrange("p (q k) -> p q k", k=2)
                nc.vector.tensor_copy(rows[0:SLOTS, :], turned[0:SLOTS, :, 0])
                nc.vector.tensor_copy(rows[SLOTS:P, :], turned[SLOTS:P, :, 1])
                nc.vector.tensor_copy(rows_of[:], row_f[0:SLOTS, :]).then_inc(rows_ready, 1)

        with ExitStack() as inner:
            sbi = lambda name, shape, dt=F32: inner.enter_context(nc.sbuf_tensor(f"moe_{name}", shape, dt))
            psi = lambda name, shape: inner.enter_context(nc.psum_tensor(f"moe_{name}", shape, F32))
            gathered = sbi("gathered", [P, PAIRS, W])
            xgT = sbi("xgT", [P, 2, DH, P])
            gate2, h2, hT2 = sbi("gate2", [P, 2, F]), sbi("h2", [P, 2, F]), sbi("hT2", [F, 2, P])
            y2 = sbi("y2", [SLOTS, 4, 2, D])
            xgT_ps, gu_ps, hT_ps = psi("xgT_ps", [P, 2, 512]), psi("gu_ps", [P, 2, 512]), psi("hT_ps", [P, 2, 512])
            y_ps = psi("y_ps", [P, 2, 2, D])
            x_gathered = [sem(f"x_gathered{k}") for k in range(8)]
            xT_ready, xT_copied, gu_ready, silu2_ready, h2_ready = sem("xT_ready"), sem("xT_copied"), sem("gu_ready"), sem("silu2_ready"), sem("h2_ready")
            hT_ready, hT_copied, y_ready, y_copied = sem("hT_ready"), sem("hT_copied"), sem("y_ready"), sem("y_copied")
            scattered = [sem("scattered0"), sem("scattered1")]
            block = inner.enter_context(nc.Block())

            @block.sync
            def _(sp):
                for q in range(NW, PAIRS):
                    sp.wait_ge(y_ready, q - NW + 1)
                    load_experts(sp, q)

            @block.gpsimd
            def _(pool):
                AHEAD = 6
                for q in range(PAIRS + AHEAD):
                    if q < PAIRS:
                        if q >= 8:
                            pool.wait_ge(x_gathered[q % 8], 16 * (q // 8))
                        nc.gpsimd.indirect_dma_start(gathered[:, q, :], None, table, bass.IndirectOffsetOnAxis(ap=rows[:, q:q + 1], axis=0)).then_inc(x_gathered[q % 8], 16)
                    if q >= AHEAD:
                        s = q - AHEAD
                        pool.wait_ge(y_copied, s + 1)
                        for k in range(2):
                            if s:
                                pool.wait_ge(scattered[k], 16 * s)
                            nc.gpsimd.indirect_dma_start(sums[k], bass.IndirectOffsetOnAxis(ap=rows_of[0:CAP, 2 * s + k:2 * s + k + 1], axis=0),
                                                         y2[0:CAP, s % 4, k, :], None, compute_op=ALU.add).then_inc(scattered[k], 16)
                for k in range(2):
                    pool.wait_ge(scattered[k], 16 * PAIRS)

            @block.tensor
            def _(pe):
                def first_stage(q):
                    pe.wait_ge(x_gathered[q % 8], 16 * (q // 8 + 1))
                    if q > 1:
                        pe.wait_ge(xT_copied, q - 1)
                    for c in range(DH):
                        ins = nc.tensor.transpose(xgT_ps[:, q % 2, c * P:(c + 1) * P], gathered[:, q, c * P:(c + 1) * P], keep["ident"][:])
                    ins.then_inc(xT_ready, 1)

                def gate_up(q):
                    pe.wait_ge(xT_copied, q + 1)
                    pe.wait_ge(w_loaded[q % NW], 32 * (q // NW + 1))
                    if q > 1:
                        pe.wait_ge(h2_ready, q - 1)
                    for k in range(2):
                        lo = k * SLOTS
                        for c in range(DH):
                            ins = nc.tensor.matmul(gu_ps[lo:lo + SLOTS, q % 2, 0:2 * F], xgT[:, q % 2, c, lo:lo + SLOTS], w_gu[:, q % NW, k, c, :],
                                                   start=(c == 0), stop=(c == DH - 1))
                    ins.then_inc(gu_ready, 1)

                def turn_h(q):
                    pe.wait_ge(h2_ready, q + 1)
                    if q > 1:
                        pe.wait_ge(hT_copied, q - 1)
                    nc.tensor.transpose(hT_ps[0:F, q % 2, 0:P], h2[:, q % 2, :], keep["ident"][:]).then_inc(hT_ready, 1)

                def down(q):
                    pe.wait_ge(hT_copied, q + 1)
                    if q > 1:
                        pe.wait_ge(y_copied, q - 1)
                    for k in range(2):
                        ins = nc.tensor.matmul(y_ps[0:CAP, q % 2, k, :], hT2[:, q % 2, k * SLOTS:k * SLOTS + CAP], w_dn[:, q % NW, k, :], start=True, stop=True)
                    ins.then_inc(y_ready, 1)

                for q in range(PAIRS + 3):
                    if q < PAIRS:
                        first_stage(q)
                    if 1 <= q <= PAIRS:
                        gate_up(q - 1)
                    if 2 <= q <= PAIRS + 1:
                        turn_h(q - 2)
                    if q >= 3:
                        down(q - 3)

            @block.scalar
            def _(act):
                for q in range(PAIRS + 2):
                    if q < PAIRS:
                        act.wait_ge(xT_ready, q + 1)
                        if q > 1:
                            act.wait_ge(gu_ready, q - 1)
                        nc.scalar.copy(xgT[:, q % 2], xgT_ps[:, q % 2, 0:D].rearrange("p (c s) -> p c s", c=DH)).then_inc(xT_copied, 1)
                    if 1 <= q <= PAIRS:
                        s = q - 1
                        act.wait_ge(gu_ready, s + 1)
                        if s > 1:
                            act.wait_ge(h2_ready, s - 1)
                        nc.scalar.activation(gate2[:, s % 2], gu_ps[:, s % 2, 0:F], ACT.Silu).then_inc(silu2_ready, 1)
                    if q >= 2:
                        s = q - 2
                        act.wait_ge(hT_ready, s + 1)
                        if s > 1:
                            act.wait_ge(y_ready, s - 1)
                        nc.scalar.copy(hT2[:, s % 2], hT_ps[0:F, s % 2, 0:P]).then_inc(hT_copied, 1)

            @block.vector
            def _(dve):
                for q in range(PAIRS + 1):
                    if q < PAIRS:
                        dve.wait_ge(silu2_ready, q + 1)
                        if q > 1:
                            dve.wait_ge(hT_ready, q - 1)
                        for k in range(2):
                            lo = k * SLOTS
                            e = D + 2 * q + k
                            ins = nc.vector.scalar_tensor_tensor(h2[lo:lo + SLOTS, q % 2, :], gu_ps[lo:lo + SLOTS, q % 2, F:2 * F],
                                                                 gathered[lo:lo + SLOTS, q, e:e + 1], gate2[lo:lo + SLOTS, q % 2, :], ALU.mult, ALU.mult)
                        ins.then_inc(h2_ready, 1)
                    if q >= 1:
                        s = q - 1
                        dve.wait_ge(y_ready, s + 1)
                        if s >= 4:
                            for k in range(2):
                                dve.wait_ge(scattered[k], 16 * (s - 3))
                        nc.vector.tensor_copy(y2[0:CAP, s % 4], y_ps[0:CAP, s % 2]).then_inc(y_copied, 1)

        with ExitStack() as inner:
            sbi = lambda name, shape, dt=F32: inner.enter_context(nc.sbuf_tensor(f"moe_{name}", shape, dt))
            part = sbi("part", [T, 2, B, D])
            stats, mean_var, var_eps, rstd = sbi("stats", [T, B, 6]), sbi("mean_var", [T, B, 2]), sbi("var_eps", [T, B]), sbi("rstd", [T, B])
            NG, QB = 4, B // 4
            half = sbi("half", [T, QB])
            parts_loaded = [sem(f"parts_loaded{g}") for g in range(NG)]
            var_ready, rstd_ready, normed, written, half_set, chain = sem("var_ready"), sem("rstd_ready"), sem("normed"), sem("written"), sem("half_set"), sem("last_chain")
            group = lambda g: slice(g * QB, (g + 1) * QB)
            block = inner.enter_context(nc.Block())

            @block.sync
            def _(sp):
                for g in range(NG):
                    for k in range(2):
                        sp.dma_start(part[:, k, group(g)], sums[k][g * QB * T:(g + 1) * QB * T].rearrange("(b t) d -> t b d", t=T)).then_inc(parts_loaded[g], 16)
                for g in range(NG):
                    sp.wait_ge(normed, g + 1)
                    sp.dma_start(out[group(g)].rearrange("b t d -> t b d"), keep["x_tok"][:, group(g), :]).then_inc(written, 16)
                sp.wait_ge(written, NG * 16)

            @block.gpsimd
            def _(pool):
                nc.gpsimd.memset(half[:], -0.5).then_inc(half_set, 1)
                pool.wait_ge(half_set, 1)
                for g in range(NG):
                    pool.wait_ge(var_ready, g + 1)
                    nc.gpsimd.tensor_tensor(rstd[:, group(g)], var_eps[:, group(g)], half[:], ALU.pow).then_inc(rstd_ready, 1)

            @block.vector
            def _(dve):
                order = Order(dve, chain)
                x = keep["x_tok"]

                def statistics(g):
                    dve.wait_ge(parts_loaded[g], 32)
                    for k in range(2):
                        order(nc.vector.tensor_tensor(x[:, group(g)], x[:, group(g)], part[:, k, group(g)], ALU.add))
                    for b in range(g * QB, (g + 1) * QB):
                        ins = nc.vector.bn_stats(stats[:, b, :], x[:, b, :])
                    order(ins)
                    for b in range(g * QB, (g + 1) * QB):
                        ins = nc.vector.bn_aggr(mean_var[:, b, :], stats[:, b, :])
                    order(ins)
                    nc.vector.tensor_scalar(var_eps[:, group(g)], mean_var[:, group(g), 1], LN_EPS, None, ALU.add).then_inc(var_ready, 1)

                def apply(g):
                    dve.wait_ge(rstd_ready, g + 1)
                    for b in range(g * QB, (g + 1) * QB):
                        ins = nc.vector.tensor_scalar(x[:, b, :], x[:, b, :], mean_var[:, b, 0:1], rstd[:, b:b + 1], ALU.subtract, ALU.mult)
                    ins.then_inc(normed, 1)

                for g in range(NG):
                    statistics(g)
                    if g:
                        apply(g - 1)
                apply(NG - 1)


def test_time_training(nc, keep, io):
    H, HD, C = 32, 8, 16
    K1 = HD + 1
    NC = T // C
    NG = 4
    HH = H // DH
    EPS = 1e-6
    with ExitStack() as ctx:
        sb = lambda name, shape: ctx.enter_context(nc.sbuf_tensor(f"ttt_{name}", shape, F32))
        sem = lambda name: new_semaphore(nc, keep, f"ttt_{name}")
        k_dram = nc.dram_tensor("ttt_k_by_head", [B, H * HD, T], F32, kind="Internal").ap()
        c_dram = nc.dram_tensor("ttt_c_by_head", [B, H * HD, T], F32, kind="Internal").ap()
        q_feat, k_feat = sb("q_feat", [P, DH, B * T]), sb("k_feat", [P, DH, B * T])
        tok = sb("tok", [P, C])
        w0, b0, w_out = sb("w0", [P, DH, P]), sb("b0", [1, D]), sb("w_out", [P, DH, D])
        post_w, post_b = sb("post_w", [P, DH]), sb("post_b", [P, DH])
        gamma_row, beta_row = sb("gamma_row", [T, D]), sb("beta_row", [T, D])
        inside, before = sb("inside", [T, T]), sb("before", [T, T])
        w_in, gamma2 = sb("w_in", [P, HD * K1]), sb("gamma2", [P, HD])
        tok_in, inverse, eps = sb("tok_in", [P, C]), sb("inverse", [P, C]), sb("eps", [P, 1])
        g_tok = sb("g_tok", [T, B, H, HD])

        with ExitStack() as seq:
            sbq = lambda name, shape: seq.enter_context(nc.sbuf_tensor(f"ttt_{name}", shape, F32))
            k_seq, c_seq, lr_seq = sbq("k_seq", [P, NG, K1, T]), sbq("c_seq", [P, NG, HD, T]), sbq("lr_seq", [P, NG, T])

            with ExitStack() as inner:
                sbi = lambda name, shape: inner.enter_context(nc.sbuf_tensor(f"ttt_{name}", shape, F32))
                w_qkv, w_lr = sbi("w_qkv", [P, DH, 3 * D]), sbi("w_lr", [P, DH, H])
                lr_bias, gamma, beta = sbi("lr_bias", [H, 1]), sbi("gamma", [P, DH]), sbi("beta", [P, DH])
                gamma_beta = sbi("gamma_beta", [P, DH])
                c_feat, lr = sbi("c_feat", [P, DH, B * T]), sbi("lr", [H, B * T])
                BANKS = 8
                acc = inner.enter_context(nc.psum_tensor("ttt_acc", [P, BANKS, 512], F32))
                w_loaded, xT_loaded, later_loaded, set_ = sem("w_loaded"), [sem(f"xT_loaded{g}") for g in range(NG)], sem("later_loaded"), sem("set")
                w_ready, proj_ready, proj_copied = sem("w_ready"), sem("proj_ready"), sem("proj_copied")
                k_stored, c_stored, seq_loaded = sem("k_stored"), sem("c_stored"), sem("seq_loaded")
                block = inner.enter_context(nc.Block())
                JOBS = ("lr", "k0", "k1", "c0", "c1", "q0", "q1")
                NJ = len(JOBS)
                KC_DONE = 5

                @block.sync
                def _(sp):
                    cols = lambda g: slice(g * 512, (g + 1) * 512)
                    xT_in = io["x_feat"].rearrange("(c p) n -> p c n", p=P)
                    sp.dma_start(keep["xT"][:, :, cols(0)], xT_in[:, :, cols(0)]).then_inc(xT_loaded[0], 16)
                    for dst, src in ((w_lr[:], io["ttt_w_lr"].rearrange("(c p) h -> p c h", p=P)), (w_qkv[:], io["ttt_w_qkv"].rearrange("(c p) o -> p c o", p=P)),
                                     (lr_bias[:], io["ttt_lr_bias"]), (gamma[:], io["ttt_gamma_feat"]), (beta[:], io["ttt_beta_feat"])):
                        sp.dma_start(dst, src).then_inc(w_loaded, 16)
                    for g in range(1, NG):
                        sp.dma_start(keep["xT"][:, :, cols(g)], xT_in[:, :, cols(g)]).then_inc(xT_loaded[g], 16)
                    for g in range(NG):
                        sp.wait_ge(proj_copied, NJ * g + KC_DONE)
                        for src, dram, stored in ((k_feat, k_dram, k_stored), (c_feat, c_dram, c_stored)):
                            for c in range(DH):
                                sp.dma_start(dram[g * NG:(g + 1) * NG, c * P:(c + 1) * P, :].rearrange("b p t -> p b t"),
                                             src[:, c, cols(g)].rearrange("p (b t) -> p b t", t=T)).then_inc(stored, 16)
                        sp.wait_ge(k_stored, 32 * (g + 1))
                        sp.wait_ge(c_stored, 32 * (g + 1))
                        sp.dma_start(k_seq[:, g, 0:HD, :].rearrange("p d t -> p (d t)"),
                                     k_dram[g * NG:(g + 1) * NG].rearrange("b (h d) t -> (b h) (d t)", d=HD)).then_inc(seq_loaded, 16)
                        sp.dma_start(c_seq[:, g].rearrange("p d t -> p (d t)"),
                                     c_dram[g * NG:(g + 1) * NG].rearrange("b (h d) t -> (b h) (d t)", d=HD)).then_inc(seq_loaded, 16)
                    for b in range(NG):
                        sp.dma_start(lr_seq[b * H:(b + 1) * H, :, :], lr[:].rearrange("h (g b t) -> h g b t", b=NG, t=T)[:, :, b, :]).then_inc(seq_loaded, 16)
                    sp.wait_ge(seq_loaded, 16 * 12)

                @block.gpsimd
                def _(pool):
                    later = [(keep["x_tok"][:], io["x"].rearrange("b t d -> t b d")), (keep["ident"][:], io["identity"]),
                             (keep["head_mask"][:], io["head_mask"]), (keep["group_mask"][:], io["group_mask"]),
                             (tok_in[:], io["ttt_token_idx"].unsqueeze(0).to_broadcast([P, C])), (inverse[:], io["ttt_inverse"].unsqueeze(0).to_broadcast([P, C])),
                             (w0[:], io["ttt_w0_bd"]), (b0[:], io["ttt_b0"].unsqueeze(0)), (w_out[:], io["ttt_w_out"].rearrange("(c p) o -> p c o", p=P)),
                             (post_w[:], io["ttt_post_w"]), (post_b[:], io["ttt_post_b"]),
                             (gamma_row[:], io["ttt_gamma"].rearrange("h d -> (h d)").unsqueeze(0).to_broadcast([T, D])),
                             (beta_row[:], io["ttt_beta"].rearrange("h d -> (h d)").unsqueeze(0).to_broadcast([T, D])),
                             (inside[:], io["ttt_inside"]), (before[:], io["ttt_before"])]
                    for b in range(NG):
                        later.append((w_in[b * H:(b + 1) * H, :], io["ttt_w0_seq"]))
                        later.append((gamma2[b * H:(b + 1) * H, :], io["ttt_gamma"]))
                    nc.gpsimd.memset(keep["neg_half"][:], -0.5)
                    nc.gpsimd.memset(eps[:], EPS).then_inc(set_, 1)
                    pool.wait_ge(xT_loaded[NG - 1], 16)
                    for dst, src in later:
                        pool.dma_start(dst, src).then_inc(later_loaded, 16)
                    pool.wait_ge(set_, 1)
                    pool.wait_ge(later_loaded, 16 * len(later))

                @block.tensor
                def _(pe):
                    column = {"q": 0, "k": D, "c": 2 * D}
                    for g in range(NG):
                        pe.wait_ge(xT_loaded[g], 16)
                        for n, job in enumerate(JOBS):
                            j = NJ * g + n
                            if j == 0:
                                pe.wait_ge(w_loaded, 16 * 5)
                            if j == JOBS.index("c0"):
                                pe.wait_ge(w_ready, 1)
                            need(pe, proj_copied, j + 1 - BANKS)
                            for c in range(DH):
                                if job == "lr":
                                    weights, tile = w_lr[:, c, :], acc[0:H, j % BANKS, :]
                                else:
                                    lo = column[job[0]] + int(job[1]) * P
                                    weights, tile = w_qkv[:, c, lo:lo + P], acc[:, j % BANKS, :]
                                ins = nc.tensor.matmul(tile, weights, keep["xT"][:, c, g * 512:(g + 1) * 512], start=(c == 0), stop=(c == DH - 1))
                            ins.then_inc(proj_ready, 1)

                @block.scalar
                def _(act):
                    act.wait_ge(w_ready, 1)
                    for g in range(NG):
                        cols = slice(g * 512, (g + 1) * 512)
                        for n, job in enumerate(JOBS):
                            j = NJ * g + n
                            tile = acc[:, j % BANKS, :]
                            act.wait_ge(proj_ready, j + 1)
                            if job == "lr":
                                ins = nc.scalar.activation(lr[:, cols], acc[0:H, j % BANKS, :], ACT.Sigmoid, bias=lr_bias[:])
                            elif job[0] == "c":
                                c = int(job[1])
                                ins = nc.scalar.activation(c_feat[:, c, cols], tile, ACT.Identity, bias=gamma_beta[:, c:c + 1], scale=gamma[:, c:c + 1])
                            else:
                                kept = k_feat if job[0] == "k" else q_feat
                                ins = nc.scalar.copy(kept[:, int(job[1]), cols], tile)
                            ins.then_inc(proj_copied, 1)

                @block.vector
                def _(dve):
                    nc.vector.memset(k_seq[:, :, HD, :], 1.0)
                    dve.wait_ge(w_loaded, 16 * 5)
                    nc.vector.tensor_tensor(gamma_beta[:], gamma[:], beta[:], ALU.mult)
                    nc.vector.tensor_tensor(w_qkv[:, :, 2 * D:3 * D], w_qkv[:, :, D:2 * D], w_qkv[:, :, 2 * D:3 * D], ALU.subtract).then_inc(w_ready, 1)

            with ExitStack() as inner:
                sbi = lambda name, shape: inner.enter_context(nc.sbuf_tensor(f"ttt_{name}", shape, F32))
                w, neg_last = sbi("w", [P, NG, HD, K1]), sbi("neg_last", [P, 1])
                prod = sbi("prod", [P, NG, C * HD * K1])
                z, sq, x_hat, gx, gxx = (sbi(n, [P, NG * C, HD]) for n in ("z", "sq", "x_hat", "gx", "gxx"))
                std, var, rstd, s1, s2, coef = (sbi(n, [P, NG * C]) for n in ("std", "var", "rstd", "s1", "s2", "coef"))
                mu, var_eps = sbi("mu", [P, NG * C]), sbi("var_eps1", [P, NG * C])
                step_w = sbi("step_w", [P, NG, HD, K1])
                g_seq = sbi("g_seq", [P, NG, HD, T])
                turned = inner.enter_context(nc.psum_tensor("ttt_turned", [T, 2, HD, P], F32))
                var_ready, std_ready = sem("var_ready"), sem("std_ready")
                grads_ready, turn_ready, turn_copied, chain = sem("grads_ready"), sem("turn_ready"), sem("turn_copied"), sem("scan_chain")
                block = inner.enter_context(nc.Block())

                @block.scalar
                def _(act):
                    with act.Fori(0, NC) as n:
                        need(act, var_ready, n + 1)
                        nc.scalar.activation(std[:], var[:], ACT.Sqrt, bias=eps[:], scale=1.0 / HD).then_inc(std_ready, 1)
                    for g in range(NG):
                        act.wait_ge(turn_ready, g + 1)
                        nc.scalar.copy(g_tok[:, g * NG:(g + 1) * NG, :, :].rearrange("t b h o -> t (b h) o"),
                                       turned[:, g % 2].rearrange("t o p -> t p o")).then_inc(turn_copied, 1)

                @block.tensor
                def _(pe):
                    pe.wait_ge(grads_ready, NC)
                    for g in range(NG):
                        if g > 1:
                            pe.wait_ge(turn_copied, g - 1)
                        for o in range(HD):
                            ins = nc.tensor.transpose(turned[:, g % 2, o, :], g_seq[:, g, o, :], keep["ident"][:])
                        ins.then_inc(turn_ready, 1)

                @block.vector
                def _(dve):
                    order = Order(dve, chain)
                    tt, ts, tr, stt = nc.vector.tensor_tensor, nc.vector.tensor_scalar, nc.vector.tensor_reduce, nc.vector.scalar_tensor_tensor
                    order(nc.vector.tensor_copy(w[:].rearrange("p g o k -> p g (o k)"), w_in[:].unsqueeze(1).to_broadcast([P, NG, HD * K1])))
                    order(tt(gamma2[:], gamma2[:], gamma2[:], ALU.mult))
                    order(tt(tok[:], tok_in[:], inverse[:], ALU.add))
                    order(ts(tok[:], tok[:], 0.0, None, ALU.max))
                    order(ts(neg_last[:], tok[:, C - 1:C], -1.0, None, ALU.mult))
                    wide = lambda t: t[:].unsqueeze(2).to_broadcast([P, NG * C, HD])
                    CHAIN = 23
                    start = order.k
                    with dve.Fori(0, NC) as n:
                        order.enter(n, CHAIN)
                        now = bass.ts(n, C)
                        for g in range(NG):
                            ins = tt(prod[:, g].rearrange("p (t o k) -> p t o k", t=C, o=HD),
                                     k_seq[:, g, :, now].rearrange("p k t -> p t k").unsqueeze(2).to_broadcast([P, C, HD, K1]),
                                     w[:, g].unsqueeze(1).to_broadcast([P, C, HD, K1]), ALU.mult)
                        order(ins)
                        order(tr(z[:], prod[:].rearrange("p g (t o k) -> p (g t o) k", t=C, o=HD), AX_X, ALU.add))
                        order(tr(mu[:], z[:], AX_X, ALU.add))
                        order(stt(z[:], wide(mu), -1.0 / HD, z[:], ALU.mult, ALU.add))
                        order(tt(sq[:], z[:], z[:], ALU.mult))
                        tr(var[:], sq[:], AX_X, ALU.add).then_inc(var_ready, 1)
                        need(dve, var_ready, n + 1)
                        ts(var_eps[:], var[:], 1.0 / HD, EPS, ALU.mult, ALU.add)
                        order(tt(gx[:], z[:], gamma2[:].unsqueeze(1).to_broadcast([P, NG * C, HD]), ALU.mult))
                        need(dve, std_ready, n + 1)
                        order(refined_rstd(nc, order, rstd[:], std[:], var_eps[:], s1[:]))
                        order(tt(x_hat[:], z[:], wide(rstd), ALU.mult))
                        order(tt(gx[:], gx[:], wide(rstd), ALU.mult))
                        order(tt(gx[:].rearrange("p (g t) o -> p g t o", g=NG), gx[:].rearrange("p (g t) o -> p g t o", g=NG),
                                 c_seq[:, :, :, now].rearrange("p g o t -> p g t o"), ALU.add))
                        order(tr(s1[:], gx[:], AX_X, ALU.add))
                        order(tt(gxx[:], gx[:], x_hat[:], ALU.mult))
                        order(tr(s2[:], gxx[:], AX_X, ALU.add))
                        order(tt(gxx[:], x_hat[:], wide(s2), ALU.mult))
                        order(stt(gx[:], gxx[:], -1.0 / HD, gx[:], ALU.mult, ALU.add))
                        order(stt(gx[:], wide(s1), -1.0 / HD, gx[:], ALU.mult, ALU.add))
                        order(stt(coef[:].rearrange("p (g t) -> p g t", g=NG), lr_seq[:, :, now], 1.0 / HD, rstd[:].rearrange("p (g t) -> p g t", g=NG), ALU.mult, ALU.mult))
                        tt(g_seq[:, :, :, now].rearrange("p g o t -> p g t o"), gx[:].rearrange("p (g t) o -> p g t o", g=NG),
                           coef[:].rearrange("p (g t) -> p g t", g=NG).unsqueeze(3).to_broadcast([P, NG, C, HD]), ALU.mult).then_inc(grads_ready, 1)
                        need(dve, grads_ready, n + 1)
                        for g in range(NG):
                            ins = tt(prod[:, g].rearrange("p (o k t) -> p o k t", o=HD, k=K1),
                                     k_seq[:, g, :, now].unsqueeze(1).to_broadcast([P, HD, K1, C]),
                                     g_seq[:, g, :, now].unsqueeze(2).to_broadcast([P, HD, K1, C]), ALU.mult)
                        order(ins)
                        order(tr(step_w[:].rearrange("p g o k -> p (g o k)"), prod[:].rearrange("p g (m t) -> p (g m) t", t=C), AX_X, ALU.add))
                        order(stt(w[:].rearrange("p g o k -> p (g o k)"), step_w[:].rearrange("p g o k -> p (g o k)"), neg_last[:], w[:].rearrange("p g o k -> p (g o k)"),
                                  ALU.mult, ALU.add))
                        order.leave(NC)

        with ExitStack() as inner:
            sbi = lambda name, shape: inner.enter_context(nc.sbuf_tensor(f"ttt_{name}", shape, F32))
            psi = lambda name, shape: inner.enter_context(nc.psum_tensor(f"ttt_{name}", shape, F32))
            ones, mask = sbi("ones", [1, T]), sbi("mask", [T, T])
            neg_last = sbi("neg_last2", [P, 1])
            U, UH, NB = 8, 4, 4
            APPLY_LAG = 3
            PEELED = 4
            q_bd, q_now, k_now = sbi("q_bd", [P, 2, DH, UH, T]), sbi("q_now", [P, 2, DH, T]), sbi("k_now", [P, 2, DH, UH, T])
            masked = sbi("masked", [T, NB, UH, T])
            z, sq, res = sbi("z2", [T, H, HD]), sbi("sq2", [T, H, HD]), sbi("res", [T, D])
            mu, var, std, rstd = sbi("mu2", [T, H]), sbi("var2", [T, H]), sbi("std2", [T, H]), sbi("rstd2", [T, H])
            head_var_eps = sbi("head_var_eps", [T, H])
            stats, mean_var, var_eps, rstd_post = sbi("stats", [T, 6]), sbi("mean_var", [T, 2]), sbi("var_eps", [T, 1]), sbi("rstd_post", [T, 1])
            spare = sbi("spare", [T, 1])
            resT = sbi("resT", [P, DH, T])
            scores, z_ps = psi("scores", [T, NB, UH, T]), psi("z_ps", [T, 2, 512])
            turned_ps, out_norm_ps = psi("turned_ps", [P, 2, D]), psi("out_norm_ps", [P, 2, D])
            q_tok_ps, resT_ps = turned_ps[:, 0, :], turned_ps[:, 1, :].rearrange("p (c t) -> p c t", c=DH)
            out_ps, normT = out_norm_ps[:, 0, :], out_norm_ps[:, 1, :]
            ones_set = sem("ones_set")
            now_ready, bd_ready, scores_ready, masked_ready, applied = sem("now_ready"), sem("bd_ready"), sem("scores_ready"), sem("masked_ready"), sem("applied")
            centred, squared, var_ready, std_ready, q_read = sem("centred2"), sem("squared2"), sem("var_ready2"), sem("std_ready2"), sem("q_read")
            post_var_ready, post_rstd_ready, post_ready = sem("post_var_ready"), sem("post_rstd_ready"), sem("post_ready")
            resT_ready, resT_copied, out_ready, chain = sem("resT_ready"), sem("resT_copied"), sem("out_ready"), sem("out_chain")
            q_ready = sem("q_tok_ready")
            norm = Norm(nc, inner, "ttt_n", keep, normT)
            block = inner.enter_context(nc.Block())
            @block.gpsimd
            def _(pool):
                nc.gpsimd.memset(ones[:], 1.0).then_inc(ones_set, 1)

                def square(b):
                    need(pool, centred, b + 1)
                    nc.gpsimd.tensor_tensor(sq[:], z[:], z[:], ALU.mult).then_inc(squared, 1)

                def rstd_after(b):
                    need(pool, post_var_ready, b + 1)
                    nc.gpsimd.tensor_tensor(rstd_post[:], var_eps[:], keep["neg_half"][:], ALU.pow).then_inc(post_rstd_ready, 1)

                def step(b, par, pair):
                    need(pool, applied, U * (b - 1))
                    nc.gpsimd.tensor_copy(q_now[:, par], q_feat[:, :, bass.ts(b, T)])
                    nc.gpsimd.tensor_tensor(k_now[:, par], k_feat[:, :, bass.ts(b, T)].unsqueeze(2).to_broadcast([P, DH, UH, T]),
                                            keep["group_mask"][:].unsqueeze(1).unsqueeze(3).to_broadcast([P, DH, UH, T]), ALU.mult).then_inc(now_ready, 1)
                    if since(b, 2):
                        rstd_after(b - 2)
                        norm.gpsimd(pool, b - 2)
                    if since(b, 1):
                        square(b - 1)
                each_sequence(pool, step, peeled=PEELED)
                for b in range(B - 2, B):
                    rstd_after(b)
                    norm.gpsimd(pool, b)
                    if b == B - 2:
                        square(B - 1)

            @block.scalar
            def _(act):

                def spread_queries(b, par):
                    need(act, scores_ready, U * (b - 1))
                    for j in range(UH):
                        ins = nc.scalar.mul(q_bd[:, par, :, j, :], q_feat[:, :, bass.ts(b, T)], keep["head_mask"][:, j:j + 1])
                    ins.then_inc(bd_ready, 1)

                def deviation(b):
                    need(act, var_ready, b + 1)
                    nc.scalar.activation(std[:], var[:], ACT.Sqrt, bias=eps[:], scale=1.0 / HD).then_inc(std_ready, 1)

                def copy_res(b):
                    need(act, resT_ready, b + 1)
                    need(act, out_ready, b)
                    for c in range(DH):
                        ins = nc.scalar.activation(resT[:, c, :], resT_ps[:, c, :], ACT.Identity, bias=post_b[:, c:c + 1], scale=post_w[:, c:c + 1])
                    ins.then_inc(resT_copied, 1)

                def step(b, par, pair):
                    spread_queries(b, par)
                    if since(b, 2):
                        copy_res(b - 2)
                    if since(b, 1):
                        deviation(b - 1)
                    if since(b, 2):
                        norm.scalar(act, b - 2)
                each_sequence(act, step, peeled=PEELED)
                copy_res(B - 2)
                deviation(B - 1)
                norm.scalar(act, B - 2)
                copy_res(B - 1)
                norm.scalar(act, B - 1)
                norm.done(act)

            @block.tensor
            def _(pe):
                pe.wait_ge(ones_set, 1)

                def score(b, par, u):
                    if u == 0:
                        need(pe, now_ready, b + 1)
                        need(pe, bd_ready, b + 1)
                    need(pe, masked_ready, U * b + u + 1 - NB)
                    c, r = u // UH, u % UH
                    nc.tensor.matmul(scores[:, u % NB], k_now[:, par, c, r, :], q_bd[:, par, c, :, :], start=True, stop=True).then_inc(scores_ready, 1)

                def begin(b, par):
                    need(pe, centred, b - 1)
                    for c in range(DH):
                        nc.tensor.matmul(z_ps[:, par, c * P:(c + 1) * P], q_now[:, par, c, :], w0[:, c, :], start=(c == 0), stop=False, skip_group_check=True)
                    nc.tensor.matmul(z_ps[:, par, 0:D], ones[:], b0[:], start=False, stop=False, skip_group_check=True)

                def turn_queries(b, par):
                    need(pe, q_read, b)
                    for c in range(DH):
                        ins = nc.tensor.transpose(q_tok_ps[:, c * P:(c + 1) * P], q_now[:, par, c, :], keep["ident"][:])
                    ins.then_inc(q_ready, 1)

                def apply(b, par, u):
                    need(pe, masked_ready, U * b + u + 1)
                    for h in range(UH):
                        hq = u * UH + h
                        ins = nc.tensor.matmul(z_ps[:, par, hq * HD:(hq + 1) * HD], masked[:, u % NB, h, :], g_tok[:, b, hq, :], start=False,
                                               stop=(hq == H - 1), skip_group_check=True)
                    ins.then_inc(applied, 1)

                def turn_res(b):
                    need(pe, post_ready, b + 1)
                    need(pe, resT_copied, b)
                    for c in range(DH):
                        ins = nc.tensor.transpose(resT_ps[:, c, :], res[:, c * P:(c + 1) * P], keep["ident"][:])
                    ins.then_inc(resT_ready, 1)

                def out(b):
                    need(pe, resT_copied, b + 1)
                    need(pe, norm.var_ready, b)
                    for c in range(DH):
                        ins = nc.tensor.matmul(out_ps[:], resT[:, c, :], w_out[:, c, :], start=(c == 0), stop=(c == DH - 1))
                    ins.then_inc(out_ready, 1)

                def step(b, par, pair):
                    for u in range(U):
                        score(b, par, u)
                        lagged(apply, b, par, u, APPLY_LAG, U)
                        if u == 0 and since(b, 2):
                            turn_res(b - 2)
                        if u == 1:
                            begin(b, par)
                            if since(b, 2):
                                out(b - 2)
                        if u == 4 and since(b, 2):
                            norm.tensor(pe, b - 2)
                        if u == 6:
                            turn_queries(b, par)
                each_sequence(pe, step, peeled=PEELED)
                for u in range(APPLY_LAG):
                    lagged(apply, B, 0, u, APPLY_LAG, U)
                for b in range(B - 2, B):
                    turn_res(b)
                    out(b)
                    norm.tensor(pe, b)

            @block.vector
            def _(dve):
                order = Order(dve, chain)
                tt, ts, tr, stt = nc.vector.tensor_tensor, nc.vector.tensor_scalar, nc.vector.tensor_reduce, nc.vector.scalar_tensor_tensor
                order(ts(neg_last[:], tok[:, C - 1:C], -1.0, None, ALU.mult))
                order(tt(mask[:].rearrange("p (n i) -> p n i", i=C), inside[:].rearrange("p (n i) -> p n i", i=C), tok[:].unsqueeze(1).to_broadcast([P, NC, C]), ALU.mult))
                order(stt(mask[:], before[:], neg_last[:], mask[:], ALU.mult, ALU.subtract))

                def masks(b, u):
                    need(dve, scores_ready, U * b + u + 1)
                    need(dve, applied, U * b + u + 1 - NB)
                    stt(masked[:, u % NB], scores[:, u % NB], 1.0, mask[:].unsqueeze(1).to_broadcast([T, UH, T]), ALU.add, ALU.mult).then_inc(masked_ready, 1)

                wide = lambda t: t[:].unsqueeze(2).to_broadcast([T, H, HD])

                def centre(b, par):
                    z3 = z_ps[:, par, 0:D].rearrange("p (h d) -> p h d", h=H)
                    need(dve, applied, U * (b + 1))
                    order(tr(mu[:], z3, AX_X, ALU.add))
                    order(ts(mu[:], mu[:], 1.0 / HD, None, ALU.mult))
                    tt(z[:], z3, wide(mu), ALU.subtract).then_inc(centred, 1)

                def variance(b):
                    need(dve, squared, b + 1)
                    tr(var[:], sq[:], AX_X, ALU.add).then_inc(var_ready, 1)
                    need(dve, var_ready, b + 1)
                    order(ts(head_var_eps[:], var[:], 1.0 / HD, EPS, ALU.mult, ALU.add))

                def head_norm(b):
                    need(dve, std_ready, b + 1)
                    order(refined_rstd(nc, order, rstd[:], std[:], head_var_eps[:], mu[:]))
                    order(tt(z[:], z[:], wide(rstd), ALU.mult))

                def residual(b):
                    z2 = z[:].rearrange("p h d -> p (h d)")
                    order(tt(z2, z2, gamma_row[:], ALU.mult))
                    order(tt(z2, z2, beta_row[:], ALU.add))
                    need(dve, resT_ready, b)
                    need(dve, q_ready, b + 1)
                    tt(res[:], z2, q_tok_ps, ALU.add).then_inc(q_read, 1)

                def post_stats(b):
                    need(dve, q_read, b + 1)
                    order(nc.vector.bn_stats(stats[:], res[:]))
                    nc.vector.memset(spare[:], 0.0)
                    order(nc.vector.bn_aggr(mean_var[:], stats[:]))
                    ts(var_eps[:], mean_var[:, 1:2], EPS, None, ALU.add).then_inc(post_var_ready, 1)

                def post_norm(b):
                    need(dve, post_rstd_ready, b + 1)
                    ts(res[:], res[:], mean_var[:, 0:1], rstd_post[:], ALU.subtract, ALU.mult).then_inc(post_ready, 1)

                def block_norm(b):
                    need(dve, out_ready, b + 1)
                    norm.vector_begin(dve, order, b, out_ps)

                def step(b, par, pair):
                    for u in range(U):
                        masks(b, u)
                        if u == 1 and since(b, 2):
                            block_norm(b - 2)
                        if u == 2 and since(b, 2):
                            norm.vector_end(dve, b - 2)
                        if since(b, 1):
                            if u == 2:
                                centre(b - 1, 1 - par)
                            if u == 3:
                                variance(b - 1)
                            if u == 4:
                                head_norm(b - 1)
                            if u == 5:
                                residual(b - 1)
                            if u == 6:
                                post_stats(b - 1)
                            if u == 7:
                                post_norm(b - 1)
                each_sequence(dve, step, order, per=2 * (12 + norm.CHAIN - 1), peeled=PEELED)
                block_norm(B - 2)
                norm.vector_end(dve, B - 2)
                centre(B - 1, (B - 1) % 2)
                variance(B - 1)
                head_norm(B - 1)
                residual(B - 1)
                post_stats(B - 1)
                post_norm(B - 1)
                block_norm(B - 1)
                norm.vector_end(dve, B - 1)


def open_persistent(nc, ctx):
    keep = {"semaphores": []}
    sb = lambda name, shape: ctx.enter_context(nc.sbuf_tensor(name, shape, F32))
    keep["x_tok"] = sb("x_tok", [T, B, D])
    keep["xT"] = sb("xT", [P, DH, B * T])
    keep["ident"] = sb("ident", [P, P])
    keep["neg_half"] = sb("neg_half", [P, 1])
    keep["head_mask"] = sb("head_mask", [P, 4])
    keep["group_mask"] = sb("group_mask", [P, 4])
    return keep


def decoder(nc, io, out):
    with ExitStack() as ctx:
        keep = open_persistent(nc, ctx)
        for phase in (test_time_training, cross_attention_gqa, gated_ffn_int8):
            phase(nc, keep, io)
            give_back_semaphores(nc, keep)
        with ExitStack() as both:
            latent = LatentWeights(nc, both)
            for phase in (batch_axis_attention, latent_cross_attention):
                phase(nc, keep, io, latent)
                give_back_semaphores(nc, keep)
        mixture_of_experts(nc, keep, io, out)


def lay_out(x, ctx, inputs):
    a0 = lambda name: np.asarray(inputs[f"L0_attn_{name}"])
    f0 = lambda name: np.asarray(inputs[f"L0_ffn_{name}"])
    a1 = lambda name: np.asarray(inputs[f"L1_attn_{name}"])
    m1 = lambda name: np.asarray(inputs[f"L1_xattn_{name}"])
    e1 = lambda name: np.asarray(inputs[f"L1_ffn_{name}"])
    feat = lambda v: v.reshape(-1, P).T
    io = {"x": x, "x_feat": x.reshape(B * T, D).T, "ctx": ctx}

    part = np.arange(P)
    io["identity"] = np.eye(P, dtype=np.float32)
    io["group_mask"] = (part[:, None] // 32 == np.arange(4)[None, :]).astype(np.float32)
    io["head_mask"] = (part[:, None] // 8 % 4 == np.arange(4)[None, :]).astype(np.float32)

    heads, hd, chunk = 32, 8, 16
    io["ttt_w_qkv"] = np.concatenate([a0("q_w").T, a0("k_w").T, a0("v_w").T], axis=1)
    io["ttt_w_lr"] = a0("ttt_lr_weight").reshape(heads, D).T
    io["ttt_lr_bias"] = a0("ttt_lr_bias")
    io["ttt_gamma_feat"], io["ttt_beta_feat"] = feat(a0("ttt_norm_weight")), feat(a0("ttt_norm_bias"))
    io["ttt_gamma"], io["ttt_beta"] = a0("ttt_norm_weight"), a0("ttt_norm_bias")
    w_first = a0("W1")
    io["ttt_w0_seq"] = np.concatenate([w_first.transpose(0, 2, 1), a0("b1").transpose(0, 2, 1)], axis=2).reshape(heads, hd * (hd + 1))
    w_bd = np.zeros((P, DH, P), w_first.dtype)
    for h in range(heads):
        r = h % (heads // DH) * hd
        w_bd[r:r + hd, h // (heads // DH), r:r + hd] = w_first[h]
    io["ttt_w0_bd"], io["ttt_b0"] = w_bd, a0("b1").reshape(D)
    io["ttt_token_idx"] = a0("learnable_token_idx")
    io["ttt_inverse"] = np.float32(1) / np.arange(1, chunk + 1, dtype=np.float32)
    io["ttt_w_out"] = a0("o_w").T
    io["ttt_post_w"], io["ttt_post_b"] = feat(a0("post_norm_weight")), feat(a0("post_norm_bias"))
    same, earlier = part[:, None] // chunk == part[None, :] // chunk, part[:, None] // chunk < part[None, :] // chunk
    io["ttt_inside"] = (same & (part[:, None] <= part[None, :])).astype(np.float32)
    io["ttt_before"] = earlier.astype(np.float32)

    by_head = ctx.transpose(0, 2, 1).reshape(B, DH, 4, 1, 8, T)
    io["ctx_rep"] = np.broadcast_to(by_head, (B, DH, 4, 4, 8, T)).reshape(B, DH, P, T)

    words = lambda a: np.ascontiguousarray(a).view(np.int32)
    io["ffn_w_gate"], io["ffn_w_up"], io["ffn_w_down"] = words(f0("w_gate")), words(f0("w_up")), words(f0("w_down"))
    io["ffn_s_gate"], io["ffn_s_up"], io["ffn_s_down"] = feat(f0("s_gate")), feat(f0("s_up")), f0("s_down")

    io["ba_w_qkv"] = np.concatenate([a1("q_proj").T, a1("k_proj").T, a1("v_proj").T], axis=1)
    io["ba_b_qkv"] = np.concatenate([a1("q_bias"), a1("k_bias"), a1("v_bias")])
    io["ba_w_out"], io["ba_b_out"] = a1("out_proj").T, a1("out_bias")

    dc = ctx.shape[2]
    frequency = (np.float32(1) / np.float32(10000) ** (np.arange(0, dc, 2, dtype=np.float32) / np.float32(dc))).astype(np.float32)
    angle = np.arange(T, dtype=np.float32)[:, None] * frequency[None, :]
    sign = np.where(np.arange(dc) < dc // 2, np.float32(-1), np.float32(1))
    io["cosines"] = np.repeat(np.cos(angle), 2, axis=-1)
    io["sines"] = np.repeat(np.sin(angle), 2, axis=-1) * sign
    io["mla_wq"], io["mla_kc_kv"], io["mla_woT"] = m1("Wq"), m1("w_kc_kv"), m1("Wo").T
    io["mla_kc_qT"] = m1("w_kc_q").reshape(16, 128, 2, 96).transpose(3, 2, 0, 1)
    io["mla_qrT"], io["mla_krT"] = m1("W_qr").transpose(2, 0, 1), m1("W_kr").transpose(2, 0, 1)

    experts, groups, f = 64, 8, 96
    io["moe_w_route"], io["moe_bias"] = e1("gate_w"), e1("bias")
    io["moe_not_first"] = (np.arange(B * experts) % experts != 0).astype(np.float32)
    io["moe_lower"] = (np.arange(groups)[None, :] < np.arange(groups)[:, None]).astype(np.float32).reshape(-1)
    io["moe_countdown"] = (B * T - (np.arange(B)[None, :] * T + part[:, None])).astype(np.float32)
    io["moe_slot_no"] = part[:, None].astype(np.float32)
    io["moe_ws_gu"], io["moe_ws_down"] = np.concatenate([e1("ws_gate"), e1("ws_up")], axis=1), e1("ws_down")
    gate_up = np.concatenate([e1("w_gate").reshape(experts // 2, 2, DH, P, f), e1("w_up").reshape(experts // 2, 2, DH, P, f)], axis=-1)
    io["moe_w_gu"] = gate_up.transpose(0, 3, 1, 2, 4)
    io["moe_w_down"] = e1("w_down").reshape(experts // 2, 2, f, D).transpose(0, 2, 1, 3)
    return {name: np.ascontiguousarray(a) for name, a in io.items()}


def kernel(**inputs):
    import concourse.bacc as bacc
    from concourse.bass_utils import run_bass_kernel_spmd

    nc = bacc.Bacc("TRN2", target_bir_lowering=False, num_devices=1)
    arrays = lay_out(np.asarray(inputs["x"]), np.asarray(inputs["ctx_512"]), inputs)
    io = {name: nc.dram_tensor(f"in_{name}", a.shape, mybir.dt.from_np(a.dtype), kind="ExternalInput").ap() for name, a in arrays.items()}
    out = nc.dram_tensor("out", (B, T, D), F32, kind="ExternalOutput").ap()
    decoder(nc, io, out)
    result = run_bass_kernel_spmd(nc, [{f"in_{name}": a for name, a in arrays.items()}], core_ids=[0])
    return result.results[0]["out"]
```

```python
from contextlib import ExitStack

import concourse.bass as bass
import numpy as np
from concourse import mybir

ALU = mybir.AluOpType
ACT = mybir.ActivationFunctionType
F32 = mybir.dt.float32
BF16 = mybir.dt.bfloat16
U32 = mybir.dt.uint32
I8 = mybir.dt.int8
I32 = mybir.dt.int32
AX_X = mybir.AxisListType.X

P = 128
B = 16
T = 128
D = 256
DH = D // P
LN_EPS = 1e-5


def need(eng, sem, value):
    if isinstance(value, int) and value <= 0:
        return
    eng.wait_ge(sem, value)


class Order:

    def __init__(self, eng, sem):
        self.eng, self.sem = eng, sem
        self.base, self.trip, self.per, self.k = 0, 0, 0, 0

    def enter(self, trip, per):
        self.base += self.k
        self.trip, self.per, self.k = trip, per, 0

    def leave(self, trips):
        assert self.k == self.per, (self.k, self.per)
        self.base += trips * self.per
        self.trip, self.per, self.k = 0, 0, 0

    def __call__(self, ins):
        ins.then_inc(self.sem, 1)
        self.k += 1
        self.eng.wait_ge(self.sem, self.base + self.trip * self.per + self.k)


def new_semaphore(nc, keep, name):
    keep["semaphores"].append(nc.alloc_semaphore(name))
    return keep["semaphores"][-1]


def give_back_semaphores(nc, keep):
    nc.clear_and_free_semaphores(keep["semaphores"])
    keep["semaphores"] = []
    nc.all_engine_barrier()


def first(b):
    return isinstance(b, int) and b == 0


def since(b, n):
    return not isinstance(b, int) or b >= n


def lagged(step, b, par, u, lag, units):
    k = u - lag
    if k >= 0:
        if not (isinstance(b, int) and b == B):
            step(b, par, k)
    elif not first(b):
        step(b - 1, 1 - par, k + units)


def refined_rstd(nc, order, rstd, std, var_eps, spare):
    order(nc.vector.reciprocal(rstd, std))
    order(nc.vector.scalar_tensor_tensor(spare, rstd, -0.5, rstd, ALU.mult, ALU.mult))
    order(nc.vector.tensor_tensor(spare, spare, var_eps, ALU.mult))
    return nc.vector.scalar_tensor_tensor(rstd, spare, 1.5, rstd, ALU.add, ALU.mult)


def live(b):
    return not isinstance(b, int) or 0 <= b < B


def each_sequence(eng, step, order=None, per=0, peeled=2):
    for b in range(peeled):
        step(b, b % 2, b // 2)
    trips = (B - peeled) // 2
    with eng.Fori(0, trips) as i:
        if order:
            order.enter(i, per)
        for par in range(2):
            step(2 * i + peeled + par, par, i + peeled // 2)
        if order:
            order.leave(trips)


def fetch(sp, loads, fetched):
    for dst, src in loads:
        sp.dma_start(dst, src).then_inc(fetched, 16)
    sp.wait_ge(fetched, 16 * len(loads))


class Norm:

    CHAIN = 4

    def __init__(self, nc, ctx, tag, keep, turned_psum):
        self.nc, self.x_tok, self.xT, self.ident, self.neg_half = nc, keep["x_tok"], keep["xT"], keep["ident"], keep["neg_half"]
        sb = lambda name, shape: ctx.enter_context(nc.sbuf_tensor(f"{tag}_{name}", shape, F32))
        sem = lambda name: new_semaphore(nc, keep, f"{tag}_{name}")
        self.total, self.stats, self.mean_var = sb("total", [P, D]), sb("stats", [P, 6]), sb("mean_var", [P, 2])
        self.spare = sb("spare", [P, 1])
        self.var_eps, self.rstd, self.normed = sb("var_eps", [P, 1]), sb("rstd", [P, 1]), sb("normed", [P, D])
        self.turned = turned_psum
        self.var_ready, self.rstd_ready = sem("var_ready"), sem("rstd_ready")
        self.norm_ready, self.kept = sem("norm_ready"), sem("kept")
        self.turn_ready, self.turn_copied = sem("turn_ready"), sem("turn_copied")

    def vector(self, eng, order, b, y):
        self.vector_begin(eng, order, b, y)
        self.vector_end(eng, b)

    def vector_begin(self, eng, order, b, y):
        nc = self.nc
        order(nc.vector.tensor_tensor(self.total[:], y, self.x_tok[:, b, :], ALU.add))
        order(nc.vector.bn_stats(self.stats[:], self.total[:]))
        nc.vector.memset(self.spare[:], 0.0)
        order(nc.vector.bn_aggr(self.mean_var[:], self.stats[:]))
        nc.vector.tensor_scalar(self.var_eps[:], self.mean_var[:, 1:2], LN_EPS, None, ALU.add).then_inc(self.var_ready, 1)

    def vector_end(self, eng, b):
        nc = self.nc
        need(eng, self.rstd_ready, b + 1)
        need(eng, self.kept, b)
        need(eng, self.turn_ready, b)
        nc.vector.tensor_scalar(self.normed[:], self.total[:], self.mean_var[:, 0:1], self.rstd[:],
                                ALU.subtract, ALU.mult).then_inc(self.norm_ready, 1)
        need(eng, self.norm_ready, b + 1)

    def gpsimd(self, eng, b):
        nc = self.nc
        need(eng, self.var_ready, b + 1)
        nc.gpsimd.tensor_tensor(self.rstd[:], self.var_eps[:], self.neg_half[:], ALU.pow).then_inc(self.rstd_ready, 1)
        need(eng, self.norm_ready, b + 1)
        nc.gpsimd.tensor_copy(self.x_tok[:, b, :], self.normed[:]).then_inc(self.kept, 1)

    def tensor(self, eng, b):
        need(eng, self.norm_ready, b + 1)
        need(eng, self.turn_copied, b)
        for c in range(DH):
            ins = self.nc.tensor.transpose(self.turned[:, c * T:(c + 1) * T], self.normed[:, c * P:(c + 1) * P], self.ident[:])
        ins.then_inc(self.turn_ready, 1)

    def scalar(self, eng, b):
        need(eng, self.turn_ready, b + 1)
        self.nc.scalar.copy(self.xT[:, :, bass.ts(b, T)], self.turned[:].rearrange("p (c t) -> p c t", c=DH)).then_inc(self.turn_copied, 1)

    def done(self, eng):
        eng.wait_ge(self.kept, B)
        eng.wait_ge(self.turn_copied, B)


def cross_attention_gqa(nc, keep, io, next_loads=()):
    NQ, NKV, HD = 32, 8, 8
    G = NQ // NKV
    UH = G
    U = NQ // UH
    NB = 4
    TURN_LAG, WEIGH_LAG = 3, 4
    SKEW = 4
    with ExitStack() as ctx:
        sb = lambda name, shape: ctx.enter_context(nc.sbuf_tensor(f"gqa_{name}", shape, F32))
        ps = lambda name, shape: ctx.enter_context(nc.psum_tensor(f"gqa_{name}", shape, F32))
        sem = lambda name: new_semaphore(nc, keep, f"gqa_{name}")
        q_feat = sb("q_feat", [P, 2, DH, NKV // DH, T])
        keys = sb("keys", [P, 2, DH, G, T])
        keys_in = sb("keys_in", [P, 2, DH, T])
        ctx_in = sb("ctx_in", [T, B, NKV * HD])
        values = sb("values", [T, 2, NKV, HD + 1])
        probs = sb("probs", [T, NB, UH, T])
        probsT = sb("probsT", [T, NB, UH, T])
        row_max = sb("row_max", [T, NB, UH])
        rsum = sb("rsum", [T, NQ])
        attended = sb("attended", [T, NQ, HD])
        scores = ps("scores", [T, NB, UH, T])
        turned = ps("turned", [T, 2, UH, T])
        weighted = ps("weighted", [T, NQ * (HD + 1)])
        normT = ps("normT", [P, DH * T])
        keys_ready, keys_loaded, ctx_loaded, ones_set = sem("keys_ready"), [sem("keys_loaded0"), sem("keys_loaded1")], sem("ctx_loaded"), sem("ones_set")
        q_ready, v_ready = sem("q_ready"), sem("v_ready")
        scores_ready, shifted, max_ready = sem("scores_ready"), sem("shifted"), sem("max_ready")
        exp_ready, turn_ready, turn_copied, weigh_ready, out_read, chain = (
            sem("exp_ready"), sem("turn_ready"), sem("turn_copied"), sem("weigh_ready"), sem("out_read"), sem("chain"))
        norm = Norm(nc, ctx, "gqa_n", keep, normT)
        fetched = sem("fetched")
        weighted3 = weighted[:].rearrange("p (h e) -> p h e", h=NQ)
        HKV = NKV // DH
        ROWS = G * HD

        block = ctx.enter_context(nc.Block())

        @block.sync
        def _(sp):
            def step(b, par, pair):
                need(sp, keys_ready, b - 1)
                sp.dma_start(keys_in[:, par], io["ctx_rep"][b].rearrange("c p t -> p c t")).then_inc(keys_loaded[par], 16)
                if first(b):
                    sp.dma_start(ctx_in[:], io["ctx"].rearrange("b t d -> t b d")).then_inc(ctx_loaded, 16)
            each_sequence(sp, step)
            if next_loads:
                fetch(sp, next_loads, fetched)

        @block.gpsimd
        def _(pool):
            nc.gpsimd.memset(values[:, :, :, HD:HD + 1], 1.0).then_inc(ones_set, 1)
            pool.wait_ge(ctx_loaded, 16)

            def step(b, par, pair):
                need(pool, scores_ready, U * (b - 1))
                nc.gpsimd.tensor_tensor(q_feat[:, par], keep["xT"][:, :, bass.ts(b, T)].unsqueeze(2).to_broadcast([P, DH, HKV, T]),
                                        keep["group_mask"][:].unsqueeze(1).unsqueeze(3).to_broadcast([P, DH, HKV, T]), ALU.mult).then_inc(q_ready, 1)
                need(pool, weigh_ready, U * (b - 1))
                nc.gpsimd.tensor_copy(values[:, par, :, 0:HD], ctx_in[:, b, :].rearrange("p (k d) -> p k d", k=NKV)).then_inc(v_ready, 1)
                if not first(b):
                    norm.gpsimd(pool, b - 1)
            each_sequence(pool, step)
            norm.gpsimd(pool, B - 1)

        @block.tensor
        def _(pe):
            def score(b, par, u):
                if u == 0:
                    need(pe, keys_ready, b + 1)
                    need(pe, q_ready, b + 1)
                need(pe, shifted, U * b + u + 1 - NB)
                half, r = u // HKV, u % HKV
                nc.tensor.matmul(scores[:, u % NB], q_feat[:, par, half, r, :], keys[:, par, half, :, :],
                                 start=True, stop=True).then_inc(scores_ready, 1)

            def turn(b, par, u):
                need(pe, exp_ready, U * b + u + 1)
                need(pe, turn_copied, U * b + u - 1)
                for h in range(UH):
                    ins = nc.tensor.transpose(turned[:, u % 2, h, :], probs[:, u % NB, h, :], keep["ident"][:])
                ins.then_inc(turn_ready, 1)

            def weigh(b, par, u):
                if u == 0:
                    need(pe, v_ready, b + 1)
                    need(pe, out_read, b)
                need(pe, turn_copied, U * b + u + 1)
                for h in range(UH):
                    ins = nc.tensor.matmul(weighted3[:, u * UH + h, :], probsT[:, u % NB, h, :], values[:, par, u, :],
                                           start=True, stop=True)
                ins.then_inc(weigh_ready, 1)

            pe.wait_ge(ones_set, 1)

            def step(b, par, pair):
                for u in range(U):
                    score(b, par, u)
                    lagged(turn, b, par, u, TURN_LAG, U)
                    lagged(weigh, b, par, u, WEIGH_LAG, U)
                    if u == U - 1 and not first(b):
                        norm.tensor(pe, b - 1)
            each_sequence(pe, step)
            for u in range(WEIGH_LAG):
                if u < TURN_LAG:
                    lagged(turn, B, 0, u, TURN_LAG, U)
                lagged(weigh, B, 0, u, WEIGH_LAG, U)
            norm.tensor(pe, B - 1)

        @block.scalar
        def _(act):
            def spread_keys(b, par, pair):
                act.wait_ge(keys_loaded[par], 16 * (pair + 1))
                need(act, scores_ready, U * (b - 1))
                for j in range(G):
                    ins = nc.scalar.mul(keys[:, par, :, j, :], keys_in[:, par], keep["head_mask"][:, j:j + 1])
                ins.then_inc(keys_ready, 1)

            def copy_turned(b, par, u):
                need(act, turn_ready, U * b + u + 1)
                need(act, weigh_ready, U * b + u + 1 - NB)
                nc.scalar.copy(probsT[:, u % NB], turned[:, u % 2]).then_inc(turn_copied, 1)

            def exponential(b, par, u):
                need(act, shifted, U * b + u + 1)
                nc.scalar.activation(probs[:, u % NB], probs[:, u % NB], ACT.Exp, scale=HD ** -0.5).then_inc(exp_ready, 1)

            def step(b, par, pair):
                spread_keys(b, par, pair)
                for u in range(U):
                    lagged(copy_turned, b, par, u, TURN_LAG + SKEW, U)
                    lagged(exponential, b, par, u, SKEW, U)
                    if u == SKEW and since(b, 2):
                        norm.scalar(act, b - 2)
            each_sequence(act, step)
            for u in range(TURN_LAG + SKEW):
                lagged(copy_turned, B, 0, u, TURN_LAG + SKEW, U)
                if u < SKEW:
                    lagged(exponential, B, 0, u, SKEW, U)
                if u == SKEW:
                    norm.scalar(act, B - 2)
            norm.scalar(act, B - 1)
            norm.done(act)

        @block.vector
        def _(dve):
            order = Order(dve, chain)

            def divide(b):
                need(dve, weigh_ready, U * (b + 1))
                order(nc.vector.reciprocal(rsum[:], weighted3[:, :, HD]))
                nc.vector.tensor_tensor(attended[:], weighted3[:, :, 0:HD], rsum[:].unsqueeze(2).to_broadcast([T, NQ, HD]),
                                        ALU.mult).then_inc(out_read, 1)

            def add(b):
                need(dve, out_read, b + 1)
                norm.vector_begin(dve, order, b, attended[:].rearrange("p h e -> p (h e)"))

            def step(b, par, pair):
                for u in range(U):
                    need(dve, scores_ready, U * b + u + 1)
                    order(nc.vector.tensor_reduce(row_max[:, u % NB], scores[:, u % NB], AX_X, ALU.max))
                    need(dve, turn_ready, U * b + u + 1 - NB)
                    nc.vector.tensor_tensor(probs[:, u % NB], scores[:, u % NB],
                                            row_max[:, u % NB].unsqueeze(2).to_broadcast([T, UH, T]), ALU.subtract).then_inc(shifted, 1)
                    if u == WEIGH_LAG - 1 and not first(b):
                        divide(b - 1)
                    if u == WEIGH_LAG and not first(b):
                        add(b - 1)
                    if u == WEIGH_LAG + 1 and not first(b):
                        norm.vector_end(dve, b - 1)
            each_sequence(dve, step, order, per=2 * (U + 4))
            divide(B - 1)
            add(B - 1)
            norm.vector_end(dve, B - 1)


class FfnInputs:

    def __init__(self, nc, ctx, io):
        F = io["ffn_w_gate"].shape[1] * 4
        FT = F // P
        sb = lambda name, shape, dt=F32: ctx.enter_context(nc.sbuf_tensor(f"ff_{name}", shape, dt))
        self.w_in, self.wd_in = sb("w_in", [P, DH, 2, F // 4], I32), sb("wd_in", [P, FT, D // 4], I32)
        self.s_in, self.s_down = sb("s_in", [P, 2, FT]), sb("s_down", [P, D])
        self.loads = [(self.w_in[:, :, k, :], io[name].rearrange("(c p) f -> p c f", p=P)) for k, name in enumerate(("ffn_w_gate", "ffn_w_up"))]
        self.loads += [(self.wd_in[:], io["ffn_w_down"].rearrange("(f p) d -> p f d", p=P))]
        self.loads += [(self.s_in[:, k, :], io[name]) for k, name in enumerate(("ffn_s_gate", "ffn_s_up"))]
        self.loads += [(self.s_down[:], io["ffn_s_down"].unsqueeze(0).to_broadcast([P, D]))]


class BatchAxisInputs:

    def __init__(self, nc, ctx, io):
        sb = lambda name, shape: ctx.enter_context(nc.sbuf_tensor(f"bat_{name}", shape, F32))
        self.w_qkv, self.w_out = sb("w_qkv", [P, DH, 3 * D]), sb("w_out", [P, DH, D])
        self.row_stats, self.b_out = sb("row_stats", [T, 3 * D]), sb("b_out", [1, D])
        self.b_qkv = self.row_stats[0:1, :]
        self.loads = [(self.w_qkv[:], io["ba_w_qkv"].rearrange("(c p) o -> p c o", p=P)), (self.b_qkv, io["ba_b_qkv"].unsqueeze(0)),
                      (self.w_out[:], io["ba_w_out"].rearrange("(c p) o -> p c o", p=P)), (self.b_out[:], io["ba_b_out"].unsqueeze(0))]


def gated_ffn_int8(nc, keep, io, inputs, next_loads=()):
    F = io["ffn_w_gate"].shape[1] * 4
    FT = F // P
    GB = 4
    GT = GB * T
    NG = B // GB
    PARTS = 3
    with ExitStack() as ctx:
        sb = lambda name, shape, dt=F32: ctx.enter_context(nc.sbuf_tensor(f"ff_{name}", shape, dt))
        ps = lambda name, shape: ctx.enter_context(nc.psum_tensor(f"ff_{name}", shape, F32))
        sem = lambda name: new_semaphore(nc, keep, f"ff_{name}")
        w_in, wd_in, s_in, s_down = inputs.w_in, inputs.wd_in, inputs.s_in, inputs.s_down
        w_up = sb("w_gate_up", [P, DH, 2, F], BF16)
        w_down = sb("w_down", [P, FT, D], BF16)
        x_parts = sb("x_parts", [P, 2, PARTS, DH, GT], BF16)
        x_rest = sb("x_rest", [P, DH, GT])
        gate = sb("gate", [P, 2, GT])
        fused = sb("fused", [P, 2, GT])
        h_rest = sb("h_rest", [P, 2, GT])
        h_parts = sb("h_parts", [P, 2, PARTS, FT, GT], BF16)
        y = sb("y", [P, D])
        gate_ps, up_ps = ps("gate_ps", [P, 2, GT]), ps("up_ps", [P, 2, GT])
        down_ps = ps("down_ps", [P, 2, 512])
        normT = ps("normT", [P, DH * T])
        fetched, cast_done, x_split, x_first, x_second = sem("fetched"), sem("cast_done"), sem("x_split"), sem("x_first"), sem("x_second")
        gate_ready, up_ready, silu_ready, fused_ready, h_first, h_second, h_split = (
            sem("gate_ready"), sem("up_ready"), sem("silu_ready"), sem("fused_ready"), sem("h_first"), sem("h_second"), sem("h_split"))
        h_rest_ready, x_rest_ready = sem("h_rest_ready"), sem("x_rest_ready")
        down_ready, y_ready, chain = sem("down_ready"), sem("y_ready"), sem("chain")
        norm = Norm(nc, ctx, "ff_n", keep, normT)

        block = ctx.enter_context(nc.Block())

        @block.sync
        def _(sp):
            if next_loads:
                fetch(sp, next_loads, fetched)

        @block.gpsimd
        def _(pool):
            def step(b):
                norm.gpsimd(pool, b)
            with pool.Fori(0, B) as b:
                step(b)

        TILES = FT * NG
        SPLIT_AT = 3
        begins = lambda b: FT * (b // GB + 1) + (FT // GB) * (b % GB) + 1
        END = begins(B - 1) + 4
        sequence_at = lambda n: next((b for b in range(B) if begins(b) == n), None)
        group_to_split = lambda n: n // FT + 1 if n % FT == SPLIT_AT and n // FT + 1 < NG else None

        @block.scalar
        def _(act):
            nc.scalar.copy(w_up[:, 0], w_in[:, 0].bitcast(I8)).then_inc(cast_done, 1)

            def split_first(g):
                need(act, up_ready, FT * (g - 1))
                nc.scalar.copy(x_parts[:, g % 2, 0], keep["xT"][:, :, bass.ts(g, GT)]).then_inc(x_first, 1)

            def split_second(g):
                act.wait_ge(x_rest_ready, g + 1)
                nc.scalar.copy(x_parts[:, g % 2, 1], x_rest[:]).then_inc(x_second, 1)

            def silu(n):
                act.wait_ge(gate_ready, n + 1)
                need(act, fused_ready, n - 1)
                nc.scalar.activation(gate[:, n % 2], gate_ps[:, n % 2], ACT.Silu, scale=s_in[:, 0, n % FT:n % FT + 1]).then_inc(silu_ready, 1)

            def hidden_first(n):
                act.wait_ge(fused_ready, n + 1)
                need(act, down_ready, GB * (n // FT - 1))
                nc.scalar.copy(h_parts[:, n // FT % 2, 0, n % FT, :], fused[:, n % 2]).then_inc(h_first, 1)

            def hidden_second(n):
                act.wait_ge(h_rest_ready, n + 1)
                nc.scalar.copy(h_parts[:, n // FT % 2, 1, n % FT, :], h_rest[:, n % 2]).then_inc(h_second, 1)

            split_first(0)
            split_second(0)
            for n in range(END):
                if n < TILES:
                    silu(n)
                if 1 <= n <= TILES:
                    hidden_second(n - 1)
                if n < TILES:
                    hidden_first(n)
                if group_to_split(n):
                    split_first(group_to_split(n))
                if group_to_split(n - 1):
                    split_second(group_to_split(n - 1))
                if sequence_at(n - 3) is not None:
                    norm.scalar(act, sequence_at(n - 3))
            norm.done(act)

        @block.vector
        def _(dve):
            order = Order(dve, chain)
            nc.vector.tensor_copy(w_up[:, 1], w_in[:, 1].bitcast(I8)).then_inc(cast_done, 1)
            nc.vector.tensor_copy(w_down[:], wd_in[:].bitcast(I8)).then_inc(cast_done, 1)

            def split_rest(g):
                dve.wait_ge(x_first, g + 1)
                need(dve, x_split, g)
                nc.vector.tensor_tensor(x_rest[:], keep["xT"][:, :, bass.ts(g, GT)], x_parts[:, g % 2, 0], ALU.subtract).then_inc(x_rest_ready, 1)

            def split_third(g):
                dve.wait_ge(x_second, g + 1)
                nc.vector.tensor_tensor(x_parts[:, g % 2, 2], x_rest[:], x_parts[:, g % 2, 1], ALU.subtract).then_inc(x_split, 1)

            def fuse(n):
                dve.wait_ge(silu_ready, n + 1)
                dve.wait_ge(up_ready, n + 1)
                need(dve, h_first, n - 1)
                nc.vector.scalar_tensor_tensor(fused[:, n % 2], up_ps[:, n % 2], s_in[:, 1, n % FT:n % FT + 1], gate[:, n % 2],
                                               ALU.mult, ALU.mult).then_inc(fused_ready, 1)

            def hidden_rest(n):
                dve.wait_ge(h_first, n + 1)
                nc.vector.tensor_tensor(h_rest[:, n % 2], fused[:, n % 2], h_parts[:, n // FT % 2, 0, n % FT, :], ALU.subtract).then_inc(h_rest_ready, 1)

            def hidden_third(n):
                dve.wait_ge(h_second, n + 1)
                nc.vector.tensor_tensor(h_parts[:, n // FT % 2, 2, n % FT, :], h_rest[:, n % 2], h_parts[:, n // FT % 2, 1, n % FT, :],
                                        ALU.subtract).then_inc(h_split, 1)

            def scale_and_add(b):
                dve.wait_ge(down_ready, b + 1)
                nc.vector.tensor_tensor(y[:], down_ps[:, b % 2, 0:D], s_down[:], ALU.mult).then_inc(y_ready, 1)
                dve.wait_ge(y_ready, b + 1)
                norm.vector_begin(dve, order, b, y[:])

            split_rest(0)
            split_third(0)
            for n in range(END):
                b = sequence_at(n - 1)
                if n < TILES:
                    fuse(n)
                if 1 <= n <= TILES:
                    hidden_third(n - 1)
                if b is not None:
                    scale_and_add(b)
                if n < TILES:
                    hidden_rest(n)
                if group_to_split(n):
                    split_rest(group_to_split(n))
                if group_to_split(n - 1):
                    split_third(group_to_split(n - 1))
                if b is not None:
                    norm.vector_end(dve, b)

        @block.tensor
        def _(pe):
            def up(n):
                g, f = n // FT, n % FT
                if f == 0:
                    pe.wait_ge(x_first, g + 1)
                    pe.wait_ge(x_split, g + 1)
                for k, tile in enumerate((gate_ps, up_ps)):
                    need(pe, silu_ready if k == 0 else fused_ready, n - 1)
                    for c in range(DH):
                        for part in range(PARTS):
                            ins = nc.tensor.matmul(tile[:, n % 2], w_up[:, c, k, f * P:(f + 1) * P], x_parts[:, g % 2, part, c, :],
                                                   start=(c == 0 and part == 0), stop=(c == DH - 1 and part == PARTS - 1))
                    ins.then_inc(up_ready if k else gate_ready, 1)

            def down(b):
                g, j = b // GB, b % GB
                pe.wait_ge(h_split, FT * (g + 1))
                need(pe, y_ready, b - 1)
                for f in range(FT):
                    for part in range(PARTS):
                        ins = nc.tensor.matmul(down_ps[:, b % 2, 0:D], h_parts[:, g % 2, part, f, j * T:(j + 1) * T], w_down[:, f, :],
                                               start=(f == 0 and part == 0), stop=(f == FT - 1 and part == PARTS - 1))
                ins.then_inc(down_ready, 1)

            pe.wait_ge(cast_done, 3)
            for n in range(END):
                if n < TILES:
                    up(n)
                if sequence_at(n) is not None:
                    down(sequence_at(n))
                if sequence_at(n - 3) is not None:
                    norm.tensor(pe, sequence_at(n - 3))


class LatentWeights:

    H, K, DC, DQ, R = 16, 128, 64, 192, 64

    def __init__(self, nc, ctx):
        sb = lambda name, shape: ctx.enter_context(nc.sbuf_tensor(f"mla_{name}", shape, F32))
        H, DC = self.H, self.DC
        self.nc = nc
        self.to_keys = sb("to_keys", [P, DH, H, DC])
        self.to_out = sb("to_out", [P, H // 2, D])
        self.keys = sb("keys", [P, B, 2, T])
        self.values = sb("values", [T, B, DC + 1])

    def open(self, ctx, keep, io, acc):
        nc, H, K, DC, DQ, R = self.nc, self.H, self.K, self.DC, self.DQ, self.R
        sb = lambda name, shape: ctx.enter_context(nc.sbuf_tensor(f"mla_{name}", shape, F32))
        sem = lambda name: new_semaphore(nc, keep, f"mla_{name}")
        self.io, self.acc, self.ident, self.QH = io, acc, keep["ident"], DQ // 2
        first, second = sb("first", [P, H * D]), sb("second", [P, H * D])
        self.qrT = first[0:R, 0:H * DQ].rearrange("p (h d) -> p h d", h=H)
        self.krT = first[0:R, H * DQ:H * D].rearrange("p (h d) -> p h d", h=H)
        self.wq = first[:].rearrange("p (h d) -> p h d", h=H)
        self.kc_qT = second[0:self.QH, :].rearrange("p (c h k) -> p c h k", c=2, h=H)
        self.woT = second[:].rearrange("p (h d) -> p h d", h=H)
        self.t2, self.kc_kv = sb("t2", [K, H, DC]), sb("kc_kv", [K, H, DC])
        self.cosines, self.sines = sb("cosines", [T, DC]), sb("sines", [T, DC])
        self.t1 = self.keys[0:self.QH].rearrange("p b k t -> p (b k t)")[:, 0:2 * H * DC].rearrange("p (c h d) -> p c h d", c=2, h=H)
        out_flat = self.to_out[:].rearrange("p q n -> p (q n)")
        self.kv = out_flat[:, 0:B * DC].rearrange("p (b d) -> p b d", b=B)
        self.turned_kv = out_flat[:, B * DC:2 * B * DC].rearrange("p (b d) -> p b d", b=B)
        self.both = self.to_keys[:].rearrange("p c h d -> p (c h d)").rearrange("p (b k d) -> p b k d", b=B, k=2)
        self.loaded, self.wq_loaded, self.woT_loaded = sem("loaded"), sem("wq_loaded"), sem("woT_loaded")
        self.done, self.copied, self.both_ready, self.chain = sem("job_done"), sem("job_copied"), sem("both_ready"), sem("turn_chain")
        self.zeroed = sem("zeroed")
        self.JOBS = ["t1_0", "t1_1", "t2_0", "keysT_0", "keysT_1", "keys_0", "keys_1", "out_0", "out_1"]

    def sync(self, sp):
        io, K = self.io, self.K
        inputs = ((self.qrT, io["mla_qrT"]), (self.krT, io["mla_krT"]), (self.kc_qT, io["mla_kc_qT"]),
                  (self.kv, io["ctx"].rearrange("b t d -> t b d")), (self.cosines[:], io["cosines"]), (self.sines[:], io["sines"]),
                  (self.kc_kv[:], io["mla_kc_kv"].rearrange("h k d -> k h d")))
        for dst, src in inputs:
            sp.dma_start(dst, src).then_inc(self.loaded, 16)
        self.LOADED = 16 * len(inputs)
        sp.wait_ge(self.done, 2)
        sp.dma_start(self.wq, io["mla_wq"].rearrange("(h k) i -> k h i", k=K)).then_inc(self.wq_loaded, 16)
        sp.wait_ge(self.done, 3)
        sp.dma_start(self.woT, io["mla_woT"].rearrange("(h k) n -> k h n", k=K)).then_inc(self.woT_loaded, 16)

    def tensor(self, pe):
        nc, H, DC = self.nc, self.H, self.DC
        for i, job in enumerate(self.JOBS):
            name, c = job.split("_")
            c = int(c)
            tile = self.acc[:, i % 2]
            per_head = tile.rearrange("p (h d) -> p h d", h=H)
            need(pe, self.copied, i - 1)
            if name == "t1":
                pe.wait_ge(self.loaded, self.LOADED)
                for h in range(H):
                    ins = nc.tensor.matmul(per_head[0:self.QH, h, :], self.qrT[:, h, c * self.QH:(c + 1) * self.QH], self.krT[:, h, :], start=True, stop=True)
            elif name == "t2":
                pe.wait_ge(self.copied, i)
                for h in range(H):
                    for k in range(2):
                        ins = nc.tensor.matmul(per_head[:, h, :], self.kc_qT[:, k, h, :], self.t1[:, k, h, :], start=(k == 0), stop=(k == 1))
            elif name == "keysT":
                pe.wait_ge(self.both_ready, 1)
                for b in range(B // 2):
                    ins = nc.tensor.transpose(tile[:, b * T:(b + 1) * T], self.both[:, c * B // 2 + b].rearrange("p k d -> p (k d)"), self.ident[:])
            elif name == "keys":
                pe.wait_ge(self.wq_loaded, 16)
                for h in range(H):
                    ins = nc.tensor.matmul(per_head[:, h, :], self.wq[:, h, c * P:(c + 1) * P], self.t2[:, h, :], start=True, stop=True)
            else:
                pe.wait_ge(self.woT_loaded, 16)
                per_pair = tile.rearrange("p (q n) -> p q n", q=H // 4)
                for h in range(c * H // 2, (c + 1) * H // 2):
                    r = (h % 2) * DC
                    ins = nc.tensor.matmul(per_pair[r:r + DC, (h - c * H // 2) // 2, :], self.kc_kv[:, h, :], self.woT[:, h, :], start=True, stop=True)
            ins.then_inc(self.done, 1)

    def scalar(self, act, start, stop):
        nc, H, DC = self.nc, self.H, self.DC
        for i in range(start, stop):
            name, c = self.JOBS[i].split("_")
            c = int(c)
            tile = self.acc[:, i % 2]
            act.wait_ge(self.done, i + 1)
            if name == "t1":
                ins = nc.scalar.copy(self.t1[:, c].rearrange("p h d -> p (h d)"), tile[0:self.QH])
            elif name == "t2":
                ins = nc.scalar.copy(self.t2[:].rearrange("p h d -> p (h d)"), tile)
            elif name == "keysT":
                act.wait_ge(self.zeroed, 2)
                turned = tile.rearrange("p (b t) -> p b t", b=B // 2)
                for k in range(2):
                    rows = slice(k * DC, (k + 1) * DC)
                    ins = nc.scalar.copy(self.keys[rows, c * B // 2:(c + 1) * B // 2, k, :], turned[rows])
            elif name == "keys":
                ins = nc.scalar.copy(self.to_keys[:, c].rearrange("p h d -> p (h d)"), tile)
            else:
                ins = nc.scalar.copy(self.to_out[:, c * H // 4:(c + 1) * H // 4].rearrange("p q n -> p (q n)"), tile)
            ins.then_inc(self.copied, 1)

    def gpsimd(self, pool):
        nc, DC = self.nc, self.DC
        HALF = DC // 2
        order = Order(pool, self.chain)
        order(nc.gpsimd.memset(self.values[:, :, DC:DC + 1], 1.0))
        pool.wait_ge(self.loaded, self.LOADED)
        per_b = lambda table, lo, hi: table[:, lo:hi].unsqueeze(1).to_broadcast([T, B, hi - lo])
        order(nc.gpsimd.tensor_tensor(self.values[:, :, 0:DC], self.kv, per_b(self.cosines, 0, DC), ALU.mult))
        order(nc.gpsimd.tensor_tensor(self.turned_kv[:, :, 0:HALF], self.kv[:, :, HALF:DC], per_b(self.sines, 0, HALF), ALU.mult))
        order(nc.gpsimd.tensor_tensor(self.turned_kv[:, :, HALF:DC], self.kv[:, :, 0:HALF], per_b(self.sines, HALF, DC), ALU.mult))
        order(nc.gpsimd.tensor_tensor(self.values[:, :, 0:DC], self.values[:, :, 0:DC], self.turned_kv, ALU.add))
        nc.gpsimd.tensor_copy(self.both, self.values[:, :, 0:DC].unsqueeze(2).to_broadcast([T, B, 2, DC])).then_inc(self.both_ready, 1)
        pool.wait_ge(self.both_ready, 1)
        pool.wait_ge(self.done, 3)
        nc.gpsimd.memset(self.keys[0:DC, :, 1, :], 0.0).then_inc(self.zeroed, 1)
        pool.wait_ge(self.zeroed, 1)
        nc.gpsimd.memset(self.keys[DC:P, :, 0, :], 0.0).then_inc(self.zeroed, 1)


def batch_axis_attention(nc, keep, io, inputs, latent):
    H = 16
    HD = D // H
    L = B
    MASKED = -10000.0
    with ExitStack() as ctx:
        sb = lambda name, shape: ctx.enter_context(nc.sbuf_tensor(f"bat_{name}", shape, F32))
        ps = lambda name, shape: ctx.enter_context(nc.psum_tensor(f"bat_{name}", shape, F32))
        sem = lambda name: new_semaphore(nc, keep, f"bat_{name}")
        w_qkv, w_out, row_stats, b_qkv, b_out = inputs.w_qkv, inputs.w_out, inputs.row_stats, inputs.b_qkv, inputs.b_out
        row_max, row_sum = row_stats[:, 0:L * H], row_stats[:, L * H:2 * L * H]
        ones = sb("ones", [1, T])
        x_feat = sb("x_feat", [P, 2, DH, T])
        q, k, v = sb("q", [T, L, D]), sb("k", [T, L, D]), sb("v", [T, L, D])
        prod = sb("prod", [T, L, D])
        s = sb("s", [T, L, H, L])
        later = k
        weighted = (q, prod)
        attT = sb("attT", [P, 2, D])
        qkv_ps = ps("qkv_ps", [T, 2, 1024])
        attT_ps, out_norm_ps = ps("attT_ps", [P, 2, 512]), ps("out_norm_ps", [T, 2, 512])
        out_ps, normT = out_norm_ps[:, 0, 0:D], out_norm_ps[:, 1, 0:D]
        ones_set, x_ready, qkv_ready, qkv_copied = sem("ones_set"), sem("x_ready"), sem("qkv_ready"), sem("qkv_copied")
        shifted, exp_ready, weighted_ready, attT_ready, attT_copied, out_ready = (
            sem("shifted"), sem("exp_ready"), sem("weighted_ready"), sem("attT_ready"), sem("attT_copied"), sem("out_ready"))
        chain = sem("chain")
        norm = Norm(nc, ctx, "ba_n", keep, normT)
        latent.open(ctx, keep, io, qkv_ps)

        block = ctx.enter_context(nc.Block())

        @block.sync
        def _(sp):
            latent.sync(sp)

        @block.gpsimd
        def _(pool):
            nc.gpsimd.memset(ones[:], 1.0).then_inc(ones_set, 1)

            def step(l, par, pair):
                need(pool, qkv_ready, l - 1)
                nc.gpsimd.tensor_copy(x_feat[:, par], keep["xT"][:, :, bass.ts(l, T)]).then_inc(x_ready, 1)
            each_sequence(pool, step)
            latent.gpsimd(pool)
            with pool.Fori(0, L) as l:
                norm.gpsimd(pool, l)

        @block.tensor
        def _(pe):
            pe.wait_ge(ones_set, 1)

            def project(l, par, pair):
                need(pe, x_ready, l + 1)
                need(pe, qkv_copied, l - 1)
                for lo, n in ((0, 512), (512, 256)):
                    for c in range(DH):
                        nc.tensor.matmul(qkv_ps[:, par, lo:lo + n], x_feat[:, par, c, :], w_qkv[:, c, lo:lo + n],
                                         start=(c == 0), stop=False)
                    ins = nc.tensor.matmul(qkv_ps[:, par, lo:lo + n], ones[:], b_qkv[:, lo:lo + n], start=False, stop=True)
                ins.then_inc(qkv_ready, 1)
            each_sequence(pe, project)
            pe.wait_ge(qkv_copied, L)
            latent.tensor(pe)

            def add_up(l):
                pe.wait_ge(weighted_ready, l + 1)
                need(pe, attT_copied, l - 1)
                slots = min(l + 2, L)
                for c in range(DH):
                    for j in range(slots):
                        ins = nc.tensor.matmul(attT_ps[:, l % 2, c * T:(c + 1) * T], weighted[l % 2][:, j, c * P:(c + 1) * P], keep["ident"][:],
                                               start=(j == 0), stop=(j == slots - 1))
                ins.then_inc(attT_ready, 1)

            def out(l):
                pe.wait_ge(attT_copied, l + 1)
                need(pe, norm.var_ready, l)
                for c in range(DH):
                    nc.tensor.matmul(out_ps, attT[:, l % 2, c * T:(c + 1) * T], w_out[:, c, :], start=(c == 0), stop=False)
                nc.tensor.matmul(out_ps, ones[:], b_out[:], start=False, stop=True).then_inc(out_ready, 1)

            for l in range(L):
                if l >= 3:
                    norm.tensor(pe, l - 3)
                add_up(l)
                if l >= 1:
                    out(l - 1)
            out(L - 1)
            for l in range(L - 3, L):
                norm.tensor(pe, l)

        @block.scalar
        def _(act):
            def copy_qkv(l, par, pair):
                need(act, qkv_ready, l + 1)
                nc.scalar.mul(q[:, l, :], qkv_ps[:, par, 0:D], HD ** -0.5)
                nc.scalar.copy(k[:, l, :], qkv_ps[:, par, D:2 * D])
                nc.scalar.copy(v[:, l, :], qkv_ps[:, par, 2 * D:3 * D]).then_inc(qkv_copied, 1)
            each_sequence(act, copy_qkv)
            latent.scalar(act, 0, 7)
            act.wait_ge(shifted, 1)
            nc.scalar.activation(s[:], s[:], ACT.Exp).then_inc(exp_ready, 1)
            latent.scalar(act, 7, len(latent.JOBS))
            for l in range(L):
                if l >= 3:
                    norm.scalar(act, l - 3)
                act.wait_ge(attT_ready, l + 1)
                need(act, out_ready, l - 1)
                nc.scalar.copy(attT[:, l % 2, :], attT_ps[:, l % 2, 0:D]).then_inc(attT_copied, 1)
            for l in range(L - 3, L):
                norm.scalar(act, l)
            norm.done(act)

        @block.vector
        def _(dve):
            order = Order(dve, chain)
            by_head = lambda t: t.rearrange("p (h d) -> p h d", h=H)
            order(nc.vector.memset(s[:], MASKED))
            for l in range(L):
                dve.wait_ge(qkv_copied, l + 1)
                order(nc.vector.tensor_tensor(prod[:, 0:l + 1, :], k[:, 0:l + 1, :],
                                              q[:, l, :].unsqueeze(1).to_broadcast([T, l + 1, D]), ALU.mult))
                order(nc.vector.tensor_reduce(s[:, l, :, 0:l + 1].rearrange("p h k -> p k h"),
                                              prod[:, 0:l + 1, :].rearrange("p k (h d) -> p k h d", h=H), AX_X, ALU.add))
            rows = s[:].rearrange("p l h k -> p (l h) k")
            order(nc.vector.tensor_reduce(row_max, rows, AX_X, ALU.max))
            nc.vector.tensor_tensor(rows, rows, row_max.unsqueeze(2).to_broadcast([T, L * H, L]), ALU.subtract).then_inc(shifted, 1)
            order(nc.vector.tensor_copy(later[:, L - 2, :], v[:, L - 1, :]))
            for l in range(L - 3, -1, -1):
                order(nc.vector.tensor_tensor(later[:, l, :], later[:, l + 1, :], v[:, l + 1, :], ALU.add))
            dve.wait_ge(exp_ready, 1)
            order(nc.vector.tensor_reduce(row_sum, rows, AX_X, ALU.add))
            order(nc.vector.reciprocal(row_sum, row_sum))
            order(nc.vector.tensor_tensor(rows, rows, row_sum.unsqueeze(2).to_broadcast([T, L * H, L]), ALU.mult))

            def weigh(l):
                need(dve, attT_ready, l - 1)
                buf = weighted[l % 2]
                if l < L - 1:
                    nc.vector.tensor_tensor(by_head(buf[:, l + 1, :]), by_head(later[:, l, :]),
                                            s[:, l, :, L - 1].unsqueeze(2).to_broadcast([T, H, HD]), ALU.mult)
                v_h = v[:, 0:l + 1, :].rearrange("p k (h d) -> p k h d", h=H)
                p_h = s[:, l, :, 0:l + 1].rearrange("p h k -> p k h").unsqueeze(3).to_broadcast([T, l + 1, H, HD])
                nc.vector.tensor_tensor(buf[:, 0:l + 1, :].rearrange("p k (h d) -> p k h d", h=H), v_h, p_h, ALU.mult).then_inc(weighted_ready, 1)

            def add_norm(l):
                dve.wait_ge(out_ready, l + 1)
                norm.vector(dve, order, l, out_ps)

            for l in range(L):
                weigh(l)
                if l >= 2:
                    add_norm(l - 2)
            for l in range(L - 2, L):
                add_norm(l)


def latent_cross_attention(nc, keep, io, latent):
    H, DC = latent.H, latent.DC
    UH = 4
    U = H // UH
    PAIRS = H // 2
    to_keys, to_out, keys, values = latent.to_keys, latent.to_out, latent.keys, latent.values
    with ExitStack() as ctx:
        sb = lambda name, shape: ctx.enter_context(nc.sbuf_tensor(f"mla_{name}", shape, F32))
        sem = lambda name: new_semaphore(nc, keep, f"mla_{name}")

        ps = lambda name, shape: ctx.enter_context(nc.psum_tensor(f"mla_{name}", shape, F32))
        q_feat = sb("q_feat", [P, 2, PAIRS, T])
        NB = 4
        QP = PAIRS // 2
        probs, probsT, row_max = sb("probs", [T, NB, UH, T]), sb("probsT", [T, NB, UH, T]), sb("row_max", [T, NB, UH])
        rsum = sb("rsum", [T, NB, UH])
        attended = sb("attended", [T, 2, H, DC])
        attT = sb("attT", [P, 2, PAIRS, T])
        scores, turned = ps("scores", [T, 2, UH, T]), ps("turned", [T, 2, UH, T])
        weighted = ps("weighted", [T, UH, DC + 1])
        shared = ps("shared", [P, 2, QP, T])
        out_norm_ps = ps("out_norm_ps", [P, 2, D])
        out_ps, normT = out_norm_ps[:, 0, :], out_norm_ps[:, 1, :]
        q_done, q_copied, scores_ready, shifted, exp_ready = sem("q_done"), sem("q_copied"), sem("scores_ready"), sem("shifted"), sem("exp_ready")
        turn_ready, turn_copied, weigh_ready, scaled = sem("turn_ready"), sem("turn_copied"), sem("weigh_ready"), sem("scaled")
        attT_ready, attT_copied, out_ready, chain = sem("attT_ready"), sem("attT_copied"), sem("out_ready"), sem("chain")
        norm = Norm(nc, ctx, "mla_n", keep, normT)
        SCORE_LAG, TURN_LAG, WEIGH_LAG = 2, 3, 4
        OUT_LAG, NORM_LAG = 2, 3
        PEELED = 4
        block = ctx.enter_context(nc.Block())

        @block.gpsimd
        def _(pool):
            with pool.Fori(0, B) as b:
                norm.gpsimd(pool, b)

        @block.tensor
        def _(pe):
            def project(b, r):
                need(pe, attT_copied, 2 * (b - 3) + r + 1)
                for k in range(QP):
                    pair = r * QP + k
                    for c in range(DH):
                        ins = nc.tensor.matmul(shared[:, r, k, :], to_keys[:, c, 2 * pair:2 * pair + 2, :], keep["xT"][:, c, bass.ts(b, T)],
                                               start=(c == 0), stop=(c == DH - 1))
                ins.then_inc(q_done, 1)

            def score(b, par, u):
                need(pe, q_copied, 2 * b + u // 2 + 1)
                need(pe, shifted, U * b + u - 1)
                for k in range(UH // 2):
                    ins = nc.tensor.matmul(scores[:, u % 2, 2 * k:2 * k + 2, :], q_feat[:, par, u * UH // 2 + k, :], keys[:, b, :, :],
                                           start=True, stop=True)
                ins.then_inc(scores_ready, 1)

            def turn(b, par, u):
                need(pe, exp_ready, U * b + u + 1)
                need(pe, turn_copied, U * b + u - 1)
                for h in range(UH):
                    ins = nc.tensor.transpose(turned[:, u % 2, h, :], probs[:, u % NB, h, :], keep["ident"][:])
                ins.then_inc(turn_ready, 1)

            def weigh(b, par, u):
                need(pe, turn_copied, U * b + u + 1)
                need(pe, scaled, U * b + u)
                for h in range(UH):
                    ins = nc.tensor.matmul(weighted[:, h, :], probsT[:, u % NB, h, :], values[:, b, :], start=True, stop=True)
                ins.then_inc(weigh_ready, 1)

            def turn_out(b, par, r):
                need(pe, scaled, U * (b + 1))
                if isinstance(b, int) and b >= B - 2:
                    pe.wait_ge(q_copied, 2 * B)
                else:
                    need(pe, q_copied, 2 * (b + 2) + r + 1)
                for k in range(QP):
                    pair = r * QP + k
                    ins = nc.tensor.transpose(shared[:, r, k, :], attended[:, par, 2 * pair:2 * pair + 2, :].rearrange("p h d -> p (h d)"),
                                              keep["ident"][:])
                ins.then_inc(attT_ready, 1)

            def project_out(b, par):
                need(pe, attT_copied, 2 * b + 2)
                need(pe, norm.var_ready, b)
                for k in range(PAIRS):
                    ins = nc.tensor.matmul(out_ps, attT[:, par, k, :], to_out[:, k, :], start=(k == 0), stop=(k == PAIRS - 1))
                ins.then_inc(out_ready, 1)

            def step(b, par, pair):
                for u in range(U):
                    lagged(score, b, par, u, SCORE_LAG, U)
                    if u == 2 and since(b, NORM_LAG):
                        norm.tensor(pe, b - NORM_LAG)
                    if u < 2 and not (isinstance(b, int) and b == B):
                        project(b, u)
                    lagged(weigh, b, par, u, WEIGH_LAG, U)
                    if u == 2 and since(b, OUT_LAG):
                        for r in range(2):
                            turn_out(b - OUT_LAG, par, r)
                    lagged(turn, b, par, u, TURN_LAG, U)
                    if u == 3 and since(b, OUT_LAG):
                        project_out(b - OUT_LAG, par)
            each_sequence(pe, step, peeled=PEELED)
            step(B, 0, B // 2)
            norm.tensor(pe, B - 2)
            for r in range(2):
                turn_out(B - 1, 1, r)
            project_out(B - 1, 1)
            norm.tensor(pe, B - 1)

        @block.scalar
        def _(act):
            def copy_q(b, par, r):
                need(act, q_done, 2 * b + r + 1)
                nc.scalar.copy(q_feat[:, par, r * QP:(r + 1) * QP, :], shared[:, r]).then_inc(q_copied, 1)

            def exponential(b, par, u):
                need(act, shifted, U * b + u + 1)
                nc.scalar.activation(probs[:, u % NB], probs[:, u % NB], ACT.Exp).then_inc(exp_ready, 1)

            def copy_turned(b, par, u):
                need(act, turn_ready, U * b + u + 1)
                need(act, weigh_ready, U * b + u + 1 - NB)
                nc.scalar.copy(probsT[:, u % NB], turned[:, u % 2]).then_inc(turn_copied, 1)

            def copy_out(b, par, r):
                need(act, attT_ready, 2 * b + r + 1)
                nc.scalar.copy(attT[:, par, r * QP:(r + 1) * QP, :], shared[:, r]).then_inc(attT_copied, 1)

            def step(b, par, pair):
                for u in range(U):
                    if u == 2 and since(b, NORM_LAG):
                        norm.scalar(act, b - NORM_LAG)
                    lagged(exponential, b, par, u, SCORE_LAG, U)
                    if u < 2 and not (isinstance(b, int) and b == B):
                        copy_q(b, par, u)
                    if u == 2 and since(b, OUT_LAG):
                        for r in range(2):
                            copy_out(b - OUT_LAG, par, r)
                    lagged(copy_turned, b, par, u, TURN_LAG, U)
            each_sequence(act, step, peeled=PEELED)
            step(B, 0, B // 2)
            norm.scalar(act, B - 2)
            for r in range(2):
                copy_out(B - 1, 1, r)
            norm.scalar(act, B - 1)
            norm.done(act)

        @block.vector
        def _(dve):
            order = Order(dve, chain)

            def shift(b, par, u):
                need(dve, scores_ready, U * b + u + 1)
                order(nc.vector.tensor_reduce(row_max[:, u % NB], scores[:, u % 2], AX_X, ALU.max))
                need(dve, turn_ready, U * b + u + 1 - NB)
                nc.vector.tensor_tensor(probs[:, u % NB], scores[:, u % 2], row_max[:, u % NB].unsqueeze(2).to_broadcast([T, UH, T]),
                                        ALU.subtract).then_inc(shifted, 1)

            def scale(b, par, u):
                need(dve, weigh_ready, U * b + u + 1)
                order(nc.vector.reciprocal(rsum[:, u % NB], weighted[:, :, DC]))
                nc.vector.tensor_tensor(attended[:, par, u * UH:(u + 1) * UH, :], weighted[:, :, 0:DC],
                                        rsum[:, u % NB].unsqueeze(2).to_broadcast([T, UH, DC]), ALU.mult).then_inc(scaled, 1)

            def add(b):
                need(dve, out_ready, b + 1)
                norm.vector_begin(dve, order, b, out_ps)

            def step(b, par, pair):
                for u in range(U):
                    if u == 0 and since(b, NORM_LAG):
                        add(b - NORM_LAG)
                    lagged(shift, b, par, u, SCORE_LAG, U)
                    if u == 0 and since(b, NORM_LAG):
                        norm.vector_end(dve, b - NORM_LAG)
                    lagged(scale, b, par, u, WEIGH_LAG, U)
            each_sequence(dve, step, order, per=2 * (2 * U + norm.CHAIN - 1), peeled=PEELED)
            step(B, 0, B // 2)
            for b in range(B - 2, B):
                add(b)
                norm.vector_end(dve, b)


def mixture_of_experts(nc, keep, io, out):
    E, G, TOPK, TOPG, CAP, F, SCALE = 64, 8, 6, 4, 48, 96, 2.5
    EG = E // G
    N = B * T
    BIG = 1e30
    W = D + E
    PAIRS = E // 2
    SLOTS = 64
    ROUNDS = CAP // 8
    with ExitStack() as ctx:
        sb = lambda name, shape, dt=F32: ctx.enter_context(nc.sbuf_tensor(f"moe_{name}", shape, dt))
        sem = lambda name: new_semaphore(nc, keep, f"moe_{name}")
        table = nc.dram_tensor("moe_table", [N + P, W], F32, kind="Internal").ap()
        sums = [nc.dram_tensor(f"moe_sums_{k}", [N + P, D], F32, kind="Internal").ap() for k in range(2)]
        rows = sb("rows", [P, PAIRS], U32)
        rows_of = sb("rows_of", [SLOTS, E], U32)
        NW = 18
        w_gu, w_dn = sb("w_gu", [P, NW, 2, DH, 2 * F]), sb("w_dn", [F, NW, 2, D])
        w_loaded = [sem(f"w_loaded{k}") for k in range(NW)]

        def load_experts(sp, q):
            sp.dma_start(w_gu[:, q % NW], io["moe_w_gu"][q]).then_inc(w_loaded[q % NW], 16)
            sp.dma_start(w_dn[:, q % NW], io["moe_w_down"][q]).then_inc(w_loaded[q % NW], 16)

        with ExitStack() as inner:
            sbi = lambda name, shape, dt=F32: inner.enter_context(nc.sbuf_tensor(f"moe_{name}", shape, dt))
            psi = lambda name, shape: inner.enter_context(nc.psum_tensor(f"moe_{name}", shape, F32))
            w_route, bias = sbi("w_route", [P, DH, E]), sbi("bias", [P, E])
            ws_gu, ws_down = sbi("ws_gu", [P, DH, 2 * F]), sbi("ws_down", [F, D])
            not_first, lower = sbi("not_first", [P, B * E]), sbi("lower", [P, G * G])
            countdown, slot_no = sbi("countdown", [P, B]), sbi("slot_no", [P, 1])
            zeros = sbi("zeros", [P, W])
            score, biased, work, chosen = sbi("score", [T, B, E]), sbi("biased", [T, B, E]), sbi("work", [T, B, E]), sbi("chosen", [T, B, E])
            equal, prefix, pick = sbi("equal", [T, B, E]), sbi("prefix", [T, B * E]), sbi("pick", [T, B, E])
            best, count, second = sbi("best", [T, B * G]), sbi("count", [T, B * G]), sbi("second", [T, B * G])
            group_score, group_in = sbi("group_score", [T, B * G]), sbi("group_in", [T, B * G])
            ahead, tied = sbi("ahead", [T, B, G, G]), sbi("tied", [T, B, G, G])
            top8, above, total = sbi("top8", [T, B, 8]), sbi("above", [T, B]), sbi("total", [T, B])
            weights = sbi("weights", [T, B, E])
            order_key = sbi("order_key", [T, B, E])
            left = sbi("left", [P, 2, N // 2])
            top, merged, merged_left = sbi("top", [P, CAP]), sbi("merged", [E, 2, CAP]), sbi("merged_left", [E, 2, 2 * CAP])
            twice = sbi("twice", [E, P])
            row_f, empty = sbi("row_f", [P, E]), sbi("empty", [P, E])
            gate, up, hT = sbi("gate", [F, 2, 512]), sbi("up", [F, 2, 512]), sbi("hT", [F, N])
            shared_y = sbi("shared_y", [T, 2, D])
            logits = psi("logits", [T, B, E])
            keysT = psi("keysT", [P, N // 2])
            shared_gate, shared_up = psi("shared_gate", [P, 512]), psi("shared_up", [P, 512])
            shared_out = psi("shared_out", [T, 2, 512])
            loaded, zero_set, logits_ready, score_ready = sem("loaded"), sem("zero_set"), sem("logits_ready"), sem("score_ready")
            key_ready, keyT_ready, twice_ready, twiceT_ready = sem("key_ready"), sem("keyT_ready"), sem("twice_ready"), sem("twiceT_ready")
            weights_ready, stored, tokens_stored, rows_ready = sem("weights_ready"), sem("stored"), sem("tokens_stored"), sem("rows_ready")
            gate_ps_ready, up_copied, h_done, down_done, added = sem("gate_ps_ready"), sem("up_copied"), sem("h_done"), sem("down_done"), sem("added")
            down_copied, route_loaded = sem("down_copied"), sem("route_loaded")
            chain = sem("route_chain")
            block = inner.enter_context(nc.Block())

            @block.sync
            def _(sp):
                sp.dma_start(w_route[:], io["moe_w_route"].rearrange("(c p) e -> p c e", p=P)).then_inc(route_loaded, 16)
                for dst, src in ((ws_gu, io["moe_ws_gu"].rearrange("(c p) f -> p c f", p=P)), (bias, io["moe_bias"].unsqueeze(0).to_broadcast([P, E])),
                                 (not_first, io["moe_not_first"].unsqueeze(0).to_broadcast([P, B * E])),
                                 (lower, io["moe_lower"].unsqueeze(0).to_broadcast([P, G * G])),
                                 (countdown, io["moe_countdown"]), (slot_no, io["moe_slot_no"]),
                                 (ws_down, io["moe_ws_down"])):
                    sp.dma_start(dst[:], src).then_inc(loaded, 16)
                sp.dma_start(table[0:N, 0:D].rearrange("(b t) d -> t b d", t=T), keep["x_tok"][:]).then_inc(tokens_stored, 16)
                sp.wait_ge(zero_set, 1)
                sp.dma_start(table[N:N + P, :], zeros[:]).then_inc(stored, 16)
                for k in range(2):
                    sp.dma_start(sums[k].rearrange("(b t) d -> t b d", t=T), zeros[:, 0:D].unsqueeze(1).to_broadcast([P, B + 1, D])).then_inc(stored, 16)
                for q in range(NW):
                    load_experts(sp, q)
                sp.wait_ge(weights_ready, 1)
                sp.dma_start(table[0:N, D:W].rearrange("(b t) e -> t b e", t=T), weights[:]).then_inc(stored, 16)
                sp.wait_ge(stored, 4 * 16)
                sp.wait_ge(tokens_stored, 16)

            LOADED = 7 * 16

            @block.tensor
            def _(pe):
                pe.wait_ge(route_loaded, 16)
                for b in range(B):
                    for c in range(DH):
                        ins = nc.tensor.matmul(logits[:, b, :], keep["xT"][:, c, b * T:(b + 1) * T], w_route[:, c, :], start=(c == 0), stop=(c == DH - 1))
                ins.then_inc(logits_ready, 1)
                pe.wait_ge(loaded, LOADED)
                for g in range(4):
                    if g:
                        pe.wait_ge(up_copied, g)
                    for k, tile in enumerate((shared_gate, shared_up)):
                        for c in range(DH):
                            ins = nc.tensor.matmul(tile[0:F, :], ws_gu[:, c, k * F:(k + 1) * F], keep["xT"][:, c, g * 512:(g + 1) * 512],
                                                   start=(c == 0), stop=(c == DH - 1))
                    ins.then_inc(gate_ps_ready, 1)
                for b in range(B):
                    pe.wait_ge(h_done, b // 4 + 1)
                    if b > 1:
                        pe.wait_ge(down_copied, b - 1)
                    nc.tensor.matmul(shared_out[:, b % 2, 0:D], hT[:, b * T:(b + 1) * T], ws_down[:], start=True, stop=True).then_inc(down_done, 1)
                pe.wait_ge(key_ready, 1)
                for k in range(B // 2):
                    ins = nc.tensor.transpose(keysT[:, k * T:(k + 1) * T], order_key[:, 2 * k:2 * k + 2, :].rearrange("p b e -> p (b e)"), keep["ident"][:])
                ins.then_inc(keyT_ready, 1)
                pe.wait_ge(twice_ready, 1)
                nc.tensor.transpose(logits[:, 0, :], twice[:], keep["ident"][0:E, 0:E]).then_inc(twiceT_ready, 1)
            @block.gpsimd
            def _(pool):
                for g in range(4):
                    pool.wait_ge(up_copied, g + 1)
                    nc.gpsimd.tensor_tensor(hT[:, g * 512:(g + 1) * 512], up[:, g % 2], gate[:, g % 2], ALU.mult).then_inc(h_done, 1)
                pool.wait_ge(tokens_stored, 16)
                for b in range(B):
                    pool.wait_ge(down_copied, b + 1)
                    nc.gpsimd.tensor_tensor(keep["x_tok"][:, b, :], shared_y[:, b % 2], keep["x_tok"][:, b, :], ALU.add).then_inc(added, 1)

            @block.scalar
            def _(act):
                act.wait_ge(logits_ready, 1)
                nc.scalar.activation(score[:], logits[:], ACT.Sigmoid).then_inc(score_ready, 1)
                for g in range(4):
                    act.wait_ge(gate_ps_ready, g + 1)
                    if g > 1:
                        act.wait_ge(h_done, g - 1)
                    nc.scalar.activation(gate[:, g % 2], shared_gate[0:F, :], ACT.Silu)
                    nc.scalar.copy(up[:, g % 2], shared_up[0:F, :]).then_inc(up_copied, 1)
                for b in range(B):
                    act.wait_ge(down_done, b + 1)
                    if b > 1:
                        act.wait_ge(added, b - 1)
                    nc.scalar.copy(shared_y[:, b % 2], shared_out[:, b % 2, 0:D]).then_inc(down_copied, 1)

            @block.vector
            def _(dve):
                order = Order(dve, chain)
                tt, ts, tr = nc.vector.tensor_tensor, nc.vector.tensor_scalar, nc.vector.tensor_reduce
                stt = nc.vector.scalar_tensor_tensor
                nc.vector.memset(zeros[:], 0.0).then_inc(zero_set, 1)
                dve.wait_ge(loaded, LOADED)
                dve.wait_ge(score_ready, 1)
                by_group = lambda t: t[:].rearrange("p b (g e) -> p (b g) e", g=G)
                wide = lambda t, n: t[:].unsqueeze(2).to_broadcast([T, t.shape[1], n])
                order(tt(biased[:], score[:], bias[:].unsqueeze(1).to_broadcast([T, B, E]), ALU.add))
                order(tr(best[:], by_group(biased), AX_X, ALU.max))
                order(tt(by_group(equal), by_group(biased), wide(best, EG), ALU.is_equal))
                order(tr(count[:], by_group(equal), AX_X, ALU.add))
                order(stt(work[:].rearrange("p b e -> p (b e)"), equal[:].rearrange("p b e -> p (b e)"), -BIG, biased[:].rearrange("p b e -> p (b e)"), ALU.mult, ALU.add))
                order(tr(second[:], by_group(work), AX_X, ALU.max))
                order(ts(count[:], count[:], 2.0, -BIG, ALU.is_lt, ALU.mult))
                order(tt(count[:], count[:], best[:], ALU.add))
                order(tt(second[:], second[:], count[:], ALU.max))
                order(tt(group_score[:], best[:], second[:], ALU.add))
                gs = group_score[:].rearrange("p (b g) -> p b g", g=G)
                mine, others = gs.unsqueeze(3).to_broadcast([T, B, G, G]), gs.unsqueeze(2).to_broadcast([T, B, G, G])
                order(tt(ahead[:], others, mine, ALU.is_gt))
                order(tt(tied[:], others, mine, ALU.is_equal))
                order(tt(tied[:].rearrange("p b g h -> p b (g h)"), tied[:].rearrange("p b g h -> p b (g h)"),
                         lower[:].unsqueeze(1).to_broadcast([T, B, G * G]), ALU.mult))
                order(tt(ahead[:], ahead[:], tied[:], ALU.add))
                order(tr(group_in[:], ahead[:].rearrange("p b g h -> p (b g) h"), AX_X, ALU.add))
                order(ts(group_in[:], group_in[:], float(TOPG), None, ALU.is_lt))
                order(tt(by_group(work), by_group(biased), wide(group_in, EG), ALU.mult))
                order(ts(group_in[:], group_in[:], 1.0, BIG, ALU.subtract, ALU.mult))
                order(tt(by_group(work), by_group(work), wide(group_in, EG), ALU.add))
                for b in range(B):
                    ins = nc.vector.max(top8[:, b, :], work[:, b, :])
                order(ins)
                sixth = top8[:, :, TOPK - 1].unsqueeze(2).to_broadcast([T, B, E])
                order(tt(pick[:], work[:], sixth, ALU.is_gt))
                order(tt(equal[:], work[:], sixth, ALU.is_equal))
                order(tr(above[:], pick[:], AX_X, ALU.add))
                order(nc.vector.tensor_tensor_scan(prefix[:], not_first[:], equal[:].rearrange("p b e -> p (b e)"), 0.0, ALU.mult, ALU.add))
                pre = prefix[:].rearrange("p (b e) -> p b e", b=B)
                order(tt(pre, pre, wide(above, E), ALU.add))
                order(stt(equal[:].rearrange("p b e -> p (b e)"), prefix[:], float(TOPK), equal[:].rearrange("p b e -> p (b e)"), ALU.is_le, ALU.mult))
                order(tt(chosen[:], pick[:], equal[:], ALU.add))
                tt(order_key[:], chosen[:], wide(countdown, E), ALU.mult).then_inc(key_ready, 1)
                order(tt(work[:], score[:], chosen[:], ALU.mult))
                order(tr(total[:], work[:], AX_X, ALU.add))
                order(nc.vector.reciprocal(total[:], total[:]))
                order(ts(total[:], total[:], SCALE, None, ALU.mult))
                tt(weights[:], work[:], wide(total, E), ALU.mult).then_inc(weights_ready, 1)
                dve.wait_ge(keyT_ready, 1)
                src = keysT[:]
                for r in range(ROUNDS):
                    order(nc.vector.max(top[:, 8 * r:8 * r + 8], src))
                    if r < ROUNDS - 1:
                        order(nc.vector.match_replace(left[:, r % 2, :], top[:, 8 * r:8 * r + 8], src, 0.0))
                        src = left[:, r % 2, :]
                order(nc.vector.tensor_copy(merged[:, 0, :], top[0:E, :]))
                order(nc.vector.tensor_copy(merged[:, 1, :], top[E:P, :]))
                order(nc.vector.memset(twice[:], 0.0))
                src = merged[:].rearrange("p k s -> p (k s)")
                for r in range(ROUNDS):
                    order(nc.vector.max(twice[:, 8 * r:8 * r + 8], src))
                    if r < ROUNDS - 1:
                        order(nc.vector.match_replace(merged_left[:, r % 2, :], twice[:, 8 * r:8 * r + 8], src, 0.0))
                        src = merged_left[:, r % 2, :]
                nc.vector.tensor_copy(twice[:, SLOTS:SLOTS + CAP], twice[:, 0:CAP]).then_inc(twice_ready, 1)
                dve.wait_ge(twiceT_ready, 1)
                order(ts(row_f[:], logits[:, 0, :], -1.0, float(N), ALU.mult, ALU.add))
                order(ts(empty[:], logits[:, 0, :], 0.0, slot_no[:], ALU.is_equal, ALU.mult))
                order(tt(row_f[:], row_f[:], empty[:], ALU.add))
                turned = row_f[:].rearrange("p (q k) -> p q k", k=2)
                nc.vector.tensor_copy(rows[0:SLOTS, :], turned[0:SLOTS, :, 0])
                nc.vector.tensor_copy(rows[SLOTS:P, :], turned[SLOTS:P, :, 1])
                nc.vector.tensor_copy(rows_of[:], row_f[0:SLOTS, :]).then_inc(rows_ready, 1)

        with ExitStack() as inner:
            sbi = lambda name, shape, dt=F32: inner.enter_context(nc.sbuf_tensor(f"moe_{name}", shape, dt))
            psi = lambda name, shape: inner.enter_context(nc.psum_tensor(f"moe_{name}", shape, F32))
            gathered = sbi("gathered", [P, PAIRS, W])
            xgT = sbi("xgT", [P, 2, DH, P])
            gate2, h2, hT2 = sbi("gate2", [P, 2, F]), sbi("h2", [P, 2, F]), sbi("hT2", [F, 2, P])
            y2 = sbi("y2", [SLOTS, 4, 2, D])
            xgT_ps, gu_ps, hT_ps = psi("xgT_ps", [P, 2, 512]), psi("gu_ps", [P, 2, 512]), psi("hT_ps", [P, 2, 512])
            y_ps = psi("y_ps", [P, 2, 2, D])
            x_gathered = [sem(f"x_gathered{k}") for k in range(8)]
            xT_ready, xT_copied, gu_ready, silu2_ready, h2_ready = sem("xT_ready"), sem("xT_copied"), sem("gu_ready"), sem("silu2_ready"), sem("h2_ready")
            hT_ready, hT_copied, y_ready, y_copied = sem("hT_ready"), sem("hT_copied"), sem("y_ready"), sem("y_copied")
            scattered = [sem("scattered0"), sem("scattered1")]
            block = inner.enter_context(nc.Block())

            @block.sync
            def _(sp):
                for q in range(NW, PAIRS):
                    sp.wait_ge(y_ready, q - NW + 1)
                    load_experts(sp, q)

            @block.gpsimd
            def _(pool):
                AHEAD = 6
                for q in range(PAIRS + AHEAD):
                    if q < PAIRS:
                        if q >= 8:
                            pool.wait_ge(x_gathered[q % 8], 16 * (q // 8))
                        nc.gpsimd.indirect_dma_start(gathered[:, q, :], None, table, bass.IndirectOffsetOnAxis(ap=rows[:, q:q + 1], axis=0)).then_inc(x_gathered[q % 8], 16)
                    if q >= AHEAD:
                        s = q - AHEAD
                        pool.wait_ge(y_copied, s + 1)
                        for k in range(2):
                            if s:
                                pool.wait_ge(scattered[k], 16 * s)
                            nc.gpsimd.indirect_dma_start(sums[k], bass.IndirectOffsetOnAxis(ap=rows_of[0:CAP, 2 * s + k:2 * s + k + 1], axis=0),
                                                         y2[0:CAP, s % 4, k, :], None, compute_op=ALU.add).then_inc(scattered[k], 16)
                for k in range(2):
                    pool.wait_ge(scattered[k], 16 * PAIRS)

            @block.tensor
            def _(pe):
                def first_stage(q):
                    pe.wait_ge(x_gathered[q % 8], 16 * (q // 8 + 1))
                    if q > 1:
                        pe.wait_ge(xT_copied, q - 1)
                    for c in range(DH):
                        ins = nc.tensor.transpose(xgT_ps[:, q % 2, c * P:(c + 1) * P], gathered[:, q, c * P:(c + 1) * P], keep["ident"][:])
                    ins.then_inc(xT_ready, 1)

                def gate_up(q):
                    pe.wait_ge(xT_copied, q + 1)
                    pe.wait_ge(w_loaded[q % NW], 32 * (q // NW + 1))
                    if q > 1:
                        pe.wait_ge(h2_ready, q - 1)
                    for k in range(2):
                        lo = k * SLOTS
                        for c in range(DH):
                            ins = nc.tensor.matmul(gu_ps[lo:lo + SLOTS, q % 2, 0:2 * F], xgT[:, q % 2, c, lo:lo + SLOTS], w_gu[:, q % NW, k, c, :],
                                                   start=(c == 0), stop=(c == DH - 1))
                    ins.then_inc(gu_ready, 1)

                def turn_h(q):
                    pe.wait_ge(h2_ready, q + 1)
                    if q > 1:
                        pe.wait_ge(hT_copied, q - 1)
                    nc.tensor.transpose(hT_ps[0:F, q % 2, 0:P], h2[:, q % 2, :], keep["ident"][:]).then_inc(hT_ready, 1)

                def down(q):
                    pe.wait_ge(hT_copied, q + 1)
                    if q > 1:
                        pe.wait_ge(y_copied, q - 1)
                    for k in range(2):
                        ins = nc.tensor.matmul(y_ps[0:CAP, q % 2, k, :], hT2[:, q % 2, k * SLOTS:k * SLOTS + CAP], w_dn[:, q % NW, k, :], start=True, stop=True)
                    ins.then_inc(y_ready, 1)

                for q in range(PAIRS + 3):
                    if q < PAIRS:
                        first_stage(q)
                    if 1 <= q <= PAIRS:
                        gate_up(q - 1)
                    if 2 <= q <= PAIRS + 1:
                        turn_h(q - 2)
                    if q >= 3:
                        down(q - 3)

            @block.scalar
            def _(act):
                for q in range(PAIRS + 2):
                    if q < PAIRS:
                        act.wait_ge(xT_ready, q + 1)
                        if q > 1:
                            act.wait_ge(gu_ready, q - 1)
                        nc.scalar.copy(xgT[:, q % 2], xgT_ps[:, q % 2, 0:D].rearrange("p (c s) -> p c s", c=DH)).then_inc(xT_copied, 1)
                    if 1 <= q <= PAIRS:
                        s = q - 1
                        act.wait_ge(gu_ready, s + 1)
                        if s > 1:
                            act.wait_ge(h2_ready, s - 1)
                        nc.scalar.activation(gate2[:, s % 2], gu_ps[:, s % 2, 0:F], ACT.Silu).then_inc(silu2_ready, 1)
                    if q >= 2:
                        s = q - 2
                        act.wait_ge(hT_ready, s + 1)
                        if s > 1:
                            act.wait_ge(y_ready, s - 1)
                        nc.scalar.copy(hT2[:, s % 2], hT_ps[0:F, s % 2, 0:P]).then_inc(hT_copied, 1)

            @block.vector
            def _(dve):
                for q in range(PAIRS + 1):
                    if q < PAIRS:
                        dve.wait_ge(silu2_ready, q + 1)
                        if q > 1:
                            dve.wait_ge(hT_ready, q - 1)
                        for k in range(2):
                            lo = k * SLOTS
                            e = D + 2 * q + k
                            ins = nc.vector.scalar_tensor_tensor(h2[lo:lo + SLOTS, q % 2, :], gu_ps[lo:lo + SLOTS, q % 2, F:2 * F],
                                                                 gathered[lo:lo + SLOTS, q, e:e + 1], gate2[lo:lo + SLOTS, q % 2, :], ALU.mult, ALU.mult)
                        ins.then_inc(h2_ready, 1)
                    if q >= 1:
                        s = q - 1
                        dve.wait_ge(y_ready, s + 1)
                        if s >= 4:
                            for k in range(2):
                                dve.wait_ge(scattered[k], 16 * (s - 3))
                        nc.vector.tensor_copy(y2[0:CAP, s % 4], y_ps[0:CAP, s % 2]).then_inc(y_copied, 1)

        with ExitStack() as inner:
            sbi = lambda name, shape, dt=F32: inner.enter_context(nc.sbuf_tensor(f"moe_{name}", shape, dt))
            part = sbi("part", [T, 2, B, D])
            stats, mean_var, var_eps, rstd = sbi("stats", [T, B, 6]), sbi("mean_var", [T, B, 2]), sbi("var_eps", [T, B]), sbi("rstd", [T, B])
            NG, QB = 4, B // 4
            half = sbi("half", [T, QB])
            parts_loaded = [sem(f"parts_loaded{g}") for g in range(NG)]
            var_ready, rstd_ready, normed, written, half_set, chain = sem("var_ready"), sem("rstd_ready"), sem("normed"), sem("written"), sem("half_set"), sem("last_chain")
            group = lambda g: slice(g * QB, (g + 1) * QB)
            block = inner.enter_context(nc.Block())

            @block.sync
            def _(sp):
                for g in range(NG):
                    for k in range(2):
                        sp.dma_start(part[:, k, group(g)], sums[k][g * QB * T:(g + 1) * QB * T].rearrange("(b t) d -> t b d", t=T)).then_inc(parts_loaded[g], 16)
                for g in range(NG):
                    sp.wait_ge(normed, g + 1)
                    sp.dma_start(out[group(g)].rearrange("b t d -> t b d"), keep["x_tok"][:, group(g), :]).then_inc(written, 16)
                sp.wait_ge(written, NG * 16)

            @block.gpsimd
            def _(pool):
                nc.gpsimd.memset(half[:], -0.5).then_inc(half_set, 1)
                pool.wait_ge(half_set, 1)
                for g in range(NG):
                    pool.wait_ge(var_ready, g + 1)
                    nc.gpsimd.tensor_tensor(rstd[:, group(g)], var_eps[:, group(g)], half[:], ALU.pow).then_inc(rstd_ready, 1)

            @block.vector
            def _(dve):
                order = Order(dve, chain)
                x = keep["x_tok"]

                def statistics(g):
                    dve.wait_ge(parts_loaded[g], 32)
                    for k in range(2):
                        order(nc.vector.tensor_tensor(x[:, group(g)], x[:, group(g)], part[:, k, group(g)], ALU.add))
                    for b in range(g * QB, (g + 1) * QB):
                        ins = nc.vector.bn_stats(stats[:, b, :], x[:, b, :])
                    order(ins)
                    for b in range(g * QB, (g + 1) * QB):
                        ins = nc.vector.bn_aggr(mean_var[:, b, :], stats[:, b, :])
                    order(ins)
                    nc.vector.tensor_scalar(var_eps[:, group(g)], mean_var[:, group(g), 1], LN_EPS, None, ALU.add).then_inc(var_ready, 1)

                def apply(g):
                    dve.wait_ge(rstd_ready, g + 1)
                    for b in range(g * QB, (g + 1) * QB):
                        ins = nc.vector.tensor_scalar(x[:, b, :], x[:, b, :], mean_var[:, b, 0:1], rstd[:, b:b + 1], ALU.subtract, ALU.mult)
                    ins.then_inc(normed, 1)

                for g in range(NG):
                    statistics(g)
                    if g:
                        apply(g - 1)
                apply(NG - 1)


def test_time_training(nc, keep, io):
    H, HD, C = 32, 8, 16
    K1 = HD + 1
    NC = T // C
    NH, HT = 2, T // 2
    NG = 4
    HH = H // DH
    EPS = 1e-6
    with ExitStack() as ctx:
        sb = lambda name, shape: ctx.enter_context(nc.sbuf_tensor(f"ttt_{name}", shape, F32))
        sem = lambda name: new_semaphore(nc, keep, f"ttt_{name}")
        k_dram = nc.dram_tensor("ttt_k_by_head", [B, H * HD, T], F32, kind="Internal").ap()
        c_dram = nc.dram_tensor("ttt_c_by_head", [B, H * HD, T], F32, kind="Internal").ap()
        q_feat, k_feat = sb("q_feat", [P, DH, B * T]), sb("k_feat", [P, DH, B * T])
        tok = sb("tok", [P, C])
        w0, w_out = sb("w0", [P, DH, P]), sb("w_out", [P, DH, D])
        post_w, post_b = sb("post_w", [P, DH]), sb("post_b", [P, DH])
        gamma_row, beta_rows = sb("gamma_row", [T, D]), sb("beta_rows", [NH, D])
        inside, before = sb("inside", [P, HT]), sb("before", [P, HT])
        w_in, gamma2 = sb("w_in", [P, HD * K1]), sb("gamma2", [P, HD])
        tok_in, inverse, eps = sb("tok_in", [P, C]), sb("inverse", [P, C]), sb("eps", [P, 1])
        HP = H // 2
        g_pairs = sb("g_pairs", [P, NH, B, HP, 2 * HD])
        w_feat, head16 = sb("w_feat", [P, B * DH, HD]), sb("head16", [P, H // DH])
        biases, half_of = sb("biases", [NH, B * D]), sb("half_of", [NH, T])
        w_dram = nc.dram_tensor("ttt_w_by_head", [B * H, HD * HD], F32, kind="Internal").ap()
        b_dram = nc.dram_tensor("ttt_b_by_head", [B * H, HD], F32, kind="Internal").ap()

        with ExitStack() as seq:
            sbq = lambda name, shape: seq.enter_context(nc.sbuf_tensor(f"ttt_{name}", shape, F32))
            k_seq, c_seq, lr_seq = sbq("k_seq", [P, NG, K1, T]), sbq("c_seq", [P, NG, HD, T]), sbq("lr_seq", [P, NG, T])

            with ExitStack() as inner:
                sbi = lambda name, shape: inner.enter_context(nc.sbuf_tensor(f"ttt_{name}", shape, F32))
                w_qkv, w_lr = sbi("w_qkv", [P, DH, 3 * D]), sbi("w_lr", [P, DH, H])
                lr_bias, gamma, beta = sbi("lr_bias", [H, 1]), sbi("gamma", [P, DH]), sbi("beta", [P, DH])
                gamma_beta = sbi("gamma_beta", [P, DH])
                c_feat, lr = sbi("c_feat", [P, DH, B * T]), sbi("lr", [H, B * T])
                BANKS = 8
                acc = inner.enter_context(nc.psum_tensor("ttt_acc", [P, BANKS, 512], F32))
                w_loaded, xT_loaded, later_loaded, set_ = sem("w_loaded"), [sem(f"xT_loaded{g}") for g in range(NG)], sem("later_loaded"), sem("set")
                w_ready, proj_ready, proj_copied, mean_done = sem("w_ready"), sem("proj_ready"), sem("proj_copied"), sem("mean_done")
                col_mean = sbi("col_mean", [P, B * H])
                k_stored, c_stored, seq_loaded = sem("k_stored"), sem("c_stored"), sem("seq_loaded")
                block = inner.enter_context(nc.Block())
                JOBS = ("lr", "k0", "k1", "c0", "c1", "q0", "q1")
                NJ = len(JOBS)
                KC_DONE = 5

                @block.sync
                def _(sp):
                    cols = lambda g: slice(g * 512, (g + 1) * 512)
                    xT_in = io["x_feat"].rearrange("(c p) n -> p c n", p=P)
                    sp.dma_start(keep["xT"][:, :, cols(0)], xT_in[:, :, cols(0)]).then_inc(xT_loaded[0], 16)
                    for dst, src in ((w_lr[:], io["ttt_w_lr"].rearrange("(c p) h -> p c h", p=P)), (w_qkv[:], io["ttt_w_qkv"].rearrange("(c p) o -> p c o", p=P)),
                                     (lr_bias[:], io["ttt_lr_bias"]), (gamma[:], io["ttt_gamma_feat"]), (beta[:], io["ttt_beta_feat"])):
                        sp.dma_start(dst, src).then_inc(w_loaded, 16)
                    for g in range(1, NG):
                        sp.dma_start(keep["xT"][:, :, cols(g)], xT_in[:, :, cols(g)]).then_inc(xT_loaded[g], 16)
                    for g in range(NG):
                        sp.wait_ge(proj_copied, NJ * g + KC_DONE)
                        for src, dram, stored in ((k_feat, k_dram, k_stored), (c_feat, c_dram, c_stored)):
                            for c in range(DH):
                                sp.dma_start(dram[g * NG:(g + 1) * NG, c * P:(c + 1) * P, :].rearrange("b p t -> p b t"),
                                             src[:, c, cols(g)].rearrange("p (b t) -> p b t", t=T)).then_inc(stored, 16)
                        sp.wait_ge(k_stored, 32 * (g + 1))
                        sp.wait_ge(c_stored, 32 * (g + 1))
                        sp.dma_start(k_seq[:, g, 0:HD, :].rearrange("p d t -> p (d t)"),
                                     k_dram[g * NG:(g + 1) * NG].rearrange("b (h d) t -> (b h) (d t)", d=HD)).then_inc(seq_loaded, 16)
                        sp.dma_start(c_seq[:, g].rearrange("p d t -> p (d t)"),
                                     c_dram[g * NG:(g + 1) * NG].rearrange("b (h d) t -> (b h) (d t)", d=HD)).then_inc(seq_loaded, 16)
                    for b in range(NG):
                        sp.dma_start(lr_seq[b * H:(b + 1) * H, :, :], lr[:].rearrange("h (g b t) -> h g b t", b=NG, t=T)[:, :, b, :]).then_inc(seq_loaded, 16)
                    sp.wait_ge(seq_loaded, 16 * 12)

                LATER = 16 * (17 + 2 * NG)

                @block.gpsimd
                def _(pool):
                    later = [(keep["x_tok"][:], io["x"].rearrange("b t d -> t b d")), (keep["ident"][:], io["identity"]),
                             (keep["head_mask"][:], io["head_mask"]), (keep["group_mask"][:], io["group_mask"]),
                             (tok_in[:], io["ttt_token_idx"].unsqueeze(0).to_broadcast([P, C])), (inverse[:], io["ttt_inverse"].unsqueeze(0).to_broadcast([P, C])),
                             (w0[:], io["ttt_w0_bd"]), (head16[:], io["ttt_head16"]), (half_of[:], io["ttt_half_of"]),
                             (biases[0:1, :].rearrange("p (b n) -> p b n", b=B), io["ttt_b0"].unsqueeze(0).unsqueeze(0).to_broadcast([1, B, D])), (w_out[:], io["ttt_w_out"].rearrange("(c p) o -> p c o", p=P)),
                             (post_w[:], io["ttt_post_w"]), (post_b[:], io["ttt_post_b"]),
                             (gamma_row[:], io["ttt_gamma"].rearrange("h d -> (h d)").unsqueeze(0).to_broadcast([T, D])),
                             (beta_rows[:], io["ttt_beta"].rearrange("h d -> (h d)").unsqueeze(0).to_broadcast([NH, D])),
                             (inside[:], io["ttt_inside"]), (before[:], io["ttt_before"])]
                    for b in range(NG):
                        later.append((w_in[b * H:(b + 1) * H, :], io["ttt_w0_seq"]))
                        later.append((gamma2[b * H:(b + 1) * H, :], io["ttt_gamma"]))
                    nc.gpsimd.memset(keep["neg_half"][:], -0.5)
                    nc.gpsimd.memset(eps[:], EPS).then_inc(set_, 1)
                    pool.wait_ge(xT_loaded[NG - 1], 16)
                    for dst, src in later:
                        pool.dma_start(dst, src).then_inc(later_loaded, 16)
                    nc.gpsimd.memset(g_pairs[:], 0.0)
                    pool.wait_ge(set_, 1)
                    assert LATER == 16 * len(later)
                    pool.wait_ge(later_loaded, LATER)

                @block.tensor
                def _(pe):
                    column = {"q": 0, "k": D, "c": 2 * D}
                    for g in range(NG):
                        pe.wait_ge(xT_loaded[g], 16)
                        for n, job in enumerate(JOBS):
                            j = NJ * g + n
                            if j == 0:
                                pe.wait_ge(w_loaded, 16 * 5)
                            if j == JOBS.index("c0"):
                                pe.wait_ge(w_ready, 1)
                            need(pe, proj_copied, j + 1 - BANKS)
                            for c in range(DH):
                                if job == "lr":
                                    weights, tile = w_lr[:, c, :], acc[0:H, j % BANKS, :]
                                else:
                                    lo = column[job[0]] + int(job[1]) * P
                                    weights, tile = w_qkv[:, c, lo:lo + P], acc[:, j % BANKS, :]
                                ins = nc.tensor.matmul(tile, weights, keep["xT"][:, c, g * 512:(g + 1) * 512], start=(c == 0), stop=(c == DH - 1))
                            ins.then_inc(proj_ready, 1)

                @block.scalar
                def _(act):
                    act.wait_ge(w_ready, 1)
                    for g in range(NG):
                        cols = slice(g * 512, (g + 1) * 512)
                        for n, job in enumerate(JOBS):
                            j = NJ * g + n
                            tile = acc[:, j % BANKS, :]
                            act.wait_ge(proj_ready, j + 1)
                            if job == "lr":
                                ins = nc.scalar.activation(lr[:, cols], acc[0:H, j % BANKS, :], ACT.Sigmoid, bias=lr_bias[:])
                            elif job[0] == "c":
                                c = int(job[1])
                                ins = nc.scalar.activation(c_feat[:, c, cols], tile, ACT.Identity, bias=gamma_beta[:, c:c + 1], scale=gamma[:, c:c + 1])
                            else:
                                kept = k_feat if job[0] == "k" else q_feat
                                ins = nc.scalar.copy(kept[:, int(job[1]), cols], tile)
                            ins.then_inc(proj_copied, 1)

                @block.vector
                def _(dve):
                    nc.vector.memset(k_seq[:, :, HD, :], 1.0)
                    dve.wait_ge(w_loaded, 16 * 5)
                    nc.vector.tensor_tensor(gamma_beta[:], gamma[:], beta[:], ALU.mult)
                    nc.vector.tensor_tensor(w_qkv[:, :, 2 * D:3 * D], w_qkv[:, :, D:2 * D], w_qkv[:, :, 2 * D:3 * D], ALU.subtract).then_inc(w_ready, 1)
                    dve.wait_ge(later_loaded, LATER)
                    for k, t in enumerate((w0[:].rearrange("p c (h o) -> p (c h) o", o=HD), biases[0:1, :].rearrange("p (h o) -> p h o", o=HD))):
                        mean = col_mean[0:t.shape[0], 0:t.shape[1]]
                        nc.vector.tensor_reduce(mean, t, AX_X, ALU.add).then_inc(mean_done, 1)
                        dve.wait_ge(mean_done, 2 * k + 1)
                        nc.vector.scalar_tensor_tensor(t, mean.unsqueeze(2).to_broadcast(list(t.shape)), -1.0 / HD, t, ALU.mult, ALU.add).then_inc(mean_done, 1)
                        dve.wait_ge(mean_done, 2 * k + 2)

            with ExitStack() as inner:
                sbi = lambda name, shape: inner.enter_context(nc.sbuf_tensor(f"ttt_{name}", shape, F32))
                w, w_middle, neg_last = sbi("w", [P, NG, HD, K1]), sbi("w_middle", [P, NG, K1, HD]), sbi("neg_last", [P, 1])
                prod = sbi("prod", [P, NG, C * HD * K1])
                z, sq, x_hat, gx, gxx = (sbi(n, [P, NG * C, HD]) for n in ("z", "sq", "x_hat", "gx", "gxx"))
                std, var, rstd, s1, s2, coef = (sbi(n, [P, NG * C]) for n in ("std", "var", "rstd", "s1", "s2", "coef"))
                middle_mean = sbi("middle_mean", [P, NG, K1])
                mu, var_eps = sbi("mu", [P, NG * C]), sbi("var_eps1", [P, NG * C])
                step_w = sbi("step_w", [P, NG, HD, K1])
                g_seq = sbi("g_seq", [P, NG, HD, T])
                turned = inner.enter_context(nc.psum_tensor("ttt_turned", [P, 2, HD, P // 2], F32))
                var_ready, std_ready = sem("var_ready"), sem("std_ready")
                grads_ready, turn_ready, turn_copied, chain = sem("grads_ready"), sem("turn_ready"), sem("turn_copied"), sem("scan_chain")
                model_ready, z_products, step_products = sem("model_ready"), sem("z_products"), sem("step_products")
                turn_copied_v, middle_ready, w_stored, w_fetched = sem("turn_copied_v"), sem("middle_ready"), sem("w_stored"), sem("w_fetched")
                block = inner.enter_context(nc.Block())

                def keep_turned(engine_copy, half, g, ab):
                    rows = slice(ab * HT, (ab + 1) * HT)
                    src = turned[rows, (half * NG + g) % 2].rearrange("p o (m j) -> p m j o", j=4)
                    dst = g_pairs[rows, half, g * NG:(g + 1) * NG].rearrange("p b (m j) (a o) -> p a (b m) j o", j=4, a=2)[:, ab]
                    return engine_copy(dst, src)

                NV = 3
                def output_products(tt, g, now):
                    return tt(prod[:, g].rearrange("p (t o k) -> p t o k", t=C, o=HD),
                              k_seq[:, g, :, now].rearrange("p k t -> p t k").unsqueeze(2).to_broadcast([P, C, HD, K1]),
                              w[:, g].unsqueeze(1).to_broadcast([P, C, HD, K1]), ALU.mult)

                def step_product(tt, g, now):
                    return tt(prod[:, g].rearrange("p (o k t) -> p o k t", o=HD, k=K1),
                              k_seq[:, g, :, now].unsqueeze(1).to_broadcast([P, HD, K1, C]),
                              g_seq[:, g, :, now].unsqueeze(2).to_broadcast([P, HD, K1, C]), ALU.mult)

                @block.gpsimd
                def _(pool):
                    with pool.Fori(0, NC) as n:
                        need(pool, model_ready, n + 1)
                        for g in range(NV, NG):
                            ins = output_products(nc.gpsimd.tensor_tensor, g, bass.ts(n, C))
                        ins.then_inc(z_products, 1)
                        need(pool, grads_ready, n + 1)
                        for g in range(NV, NG):
                            ins = step_product(nc.gpsimd.tensor_tensor, g, bass.ts(n, C))
                        ins.then_inc(step_products, 1)

                @block.sync
                def _(sp):
                    sp.wait_ge(middle_ready, 1)
                    sp.dma_start(w_dram.rearrange("(g p) f -> p g f", g=NG), w_middle[:, :, 0:HD, :].rearrange("p g k o -> p g (k o)")).then_inc(w_stored, 16)
                    sp.dma_start(b_dram.rearrange("(g p) f -> p g f", g=NG), w_middle[:, :, HD, :]).then_inc(w_stored, 16)
                    sp.wait_ge(w_stored, 32)
                    sp.dma_start(w_feat[:], w_dram.rearrange("(n h) (k o) -> (h k) n o", h=H // DH, o=HD)).then_inc(w_fetched, 16)
                    sp.dma_start(biases[1:2, :], b_dram.rearrange("n o -> (n o)").unsqueeze(0)).then_inc(w_fetched, 16)
                    sp.wait_ge(w_fetched, 32)

                @block.scalar
                def _(act):
                    def turned_gradients(half, g, ab):
                        act.wait_ge(turn_ready, half * NG + g + 1)
                        return keep_turned(nc.scalar.copy, half, g, ab)

                    for half in range(NH):
                        with act.Fori(half * NC // NH, (half + 1) * NC // NH) as n:
                            need(act, var_ready, n + 1)
                            nc.scalar.activation(std[:], var[:], ACT.Sqrt, bias=eps[:], scale=1.0 / HD).then_inc(std_ready, 1)
                    for half in range(NH):
                        for g in range(NG):
                            for ab in range(2 - half):
                                ins = turned_gradients(half, g, ab)
                            ins.then_inc(turn_copied, 1)

                @block.tensor
                def _(pe):
                    for half in range(NH):
                        pe.wait_ge(grads_ready, (half + 1) * NC // NH)
                        for g in range(NG):
                            n = half * NG + g
                            if n > 1:
                                pe.wait_ge(turn_copied, n - 1)
                            if n > 1 + NG:
                                pe.wait_ge(turn_copied_v, n - 1 - NG)
                            for o in range(HD):
                                for ab in range(2):
                                    ins = nc.tensor.matmul(turned[ab * HT:(ab + 1) * HT, n % 2, o, :], g_seq[:, g, o, half * HT:(half + 1) * HT],
                                                           keep["ident"][:].rearrange("p (m a j) -> p a m j", a=2, j=4)[:, ab], start=True, stop=True)
                            ins.then_inc(turn_ready, 1)

                @block.vector
                def _(dve):
                    order = Order(dve, chain)
                    tt, ts, tr, stt = nc.vector.tensor_tensor, nc.vector.tensor_scalar, nc.vector.tensor_reduce, nc.vector.scalar_tensor_tensor
                    nc.vector.tensor_copy(w[:].rearrange("p g o k -> p g (o k)"), w_in[:].unsqueeze(1).to_broadcast([P, NG, HD * K1])).then_inc(model_ready, 1)
                    dve.wait_ge(model_ready, 1)
                    order(tt(gamma2[:], gamma2[:], gamma2[:], ALU.mult))
                    order(tt(tok[:], tok_in[:], inverse[:], ALU.add))
                    order(ts(tok[:], tok[:], 0.0, None, ALU.max))
                    order(ts(neg_last[:], tok[:, C - 1:C], -1.0, None, ALU.mult))
                    wide = lambda t: t[:].unsqueeze(2).to_broadcast([P, NG * C, HD])
                    CHAIN = 24
                    start = order.k
                    for half in range(NH):
                        with dve.Fori(0, NC // NH) as m:
                            order.enter(m, CHAIN)
                            n = m + half * NC // NH
                            now = bass.ts(n, C)
                            for g in range(NV):
                                ins = output_products(tt, g, now)
                            order(ins)
                            z_of = lambda lo, hi: (z[:, lo * C:hi * C], prod[:, lo:hi].rearrange("p g (t o k) -> p (g t o) k", t=C, o=HD))
                            order(tr(*z_of(0, NV), AX_X, ALU.add))
                            need(dve, z_products, n + 1)
                            order(tr(*z_of(NV, NG), AX_X, ALU.add))
                            order(tr(mu[:], z[:], AX_X, ALU.add))
                            order(stt(z[:], wide(mu), -1.0 / HD, z[:], ALU.mult, ALU.add))
                            order(tt(sq[:], z[:], z[:], ALU.mult))
                            tr(var[:], sq[:], AX_X, ALU.add).then_inc(var_ready, 1)
                            need(dve, var_ready, n + 1)
                            ts(var_eps[:], var[:], 1.0 / HD, EPS, ALU.mult, ALU.add)
                            order(tt(gx[:], z[:], gamma2[:].unsqueeze(1).to_broadcast([P, NG * C, HD]), ALU.mult))
                            need(dve, std_ready, n + 1)
                            order(refined_rstd(nc, order, rstd[:], std[:], var_eps[:], s1[:]))
                            order(tt(x_hat[:], z[:], wide(rstd), ALU.mult))
                            order(tt(gx[:], gx[:], wide(rstd), ALU.mult))
                            order(tt(gx[:].rearrange("p (g t) o -> p g t o", g=NG), gx[:].rearrange("p (g t) o -> p g t o", g=NG),
                                     c_seq[:, :, :, now].rearrange("p g o t -> p g t o"), ALU.add))
                            order(tr(s1[:], gx[:], AX_X, ALU.add))
                            order(tt(gxx[:], gx[:], x_hat[:], ALU.mult))
                            order(tr(s2[:], gxx[:], AX_X, ALU.add))
                            order(tt(gxx[:], x_hat[:], wide(s2), ALU.mult))
                            order(stt(gx[:], gxx[:], -1.0 / HD, gx[:], ALU.mult, ALU.add))
                            order(stt(gx[:], wide(s1), -1.0 / HD, gx[:], ALU.mult, ALU.add))
                            order(stt(coef[:].rearrange("p (g t) -> p g t", g=NG), lr_seq[:, :, now], 1.0 / HD, rstd[:].rearrange("p (g t) -> p g t", g=NG), ALU.mult, ALU.mult))
                            tt(g_seq[:, :, :, now].rearrange("p g o t -> p g t o"), gx[:].rearrange("p (g t) o -> p g t o", g=NG),
                               coef[:].rearrange("p (g t) -> p g t", g=NG).unsqueeze(3).to_broadcast([P, NG, C, HD]), ALU.mult).then_inc(grads_ready, 1)
                            need(dve, grads_ready, n + 1)
                            for g in range(NV):
                                ins = step_product(tt, g, now)
                            order(ins)
                            step_of = lambda lo, hi: (step_w[:, lo:hi].rearrange("p g o k -> p (g o k)"), prod[:, lo:hi].rearrange("p g (m t) -> p (g m) t", t=C))
                            order(tr(*step_of(0, NV), AX_X, ALU.add))
                            need(dve, step_products, n + 1)
                            order(tr(*step_of(NV, NG), AX_X, ALU.add))
                            stt(w[:].rearrange("p g o k -> p (g o k)"), step_w[:].rearrange("p g o k -> p (g o k)"), neg_last[:], w[:].rearrange("p g o k -> p (g o k)"),
                                ALU.mult, ALU.add).then_inc(model_ready, 1)
                            need(dve, model_ready, n + 2)
                            order.leave(NC // NH)
                        if half == 0:
                            w_cols = w[:].rearrange("p g o k -> p g k o")
                            order(tr(middle_mean[:], w_cols, AX_X, ALU.add))
                            order(ts(middle_mean[:], middle_mean[:], 1.0 / HD, None, ALU.mult))
                            tt(w_middle[:], w_cols, middle_mean[:].unsqueeze(3).to_broadcast([P, NG, K1, HD]), ALU.subtract).then_inc(middle_ready, 1)
                    for g in range(NG):
                        dve.wait_ge(turn_ready, NG + g + 1)
                        keep_turned(nc.vector.tensor_copy, 1, g, 1).then_inc(turn_copied_v, 1)

        with ExitStack() as inner:
            sbi = lambda name, shape: inner.enter_context(nc.sbuf_tensor(f"ttt_{name}", shape, F32))
            psi = lambda name, shape: inner.enter_context(nc.psum_tensor(f"ttt_{name}", shape, F32))
            mask = sbi("mask", [P, HT])
            neg_last = sbi("neg_last2", [P, 1])
            U, UH, NB = 4, 4, 4
            APPLY_LAG = 2
            PEELED = 4
            q_bd, q_now = sbi("q_bd", [P, 2, DH, UH, T]), sbi("q_now", [P, 2, DH, T])
            k_now = sbi("k_now", [P, 2, U, NH, 2, HT])
            g_now = sbi("g_now", [P, 2, NH, HP, 2 * HD])
            w_now = sbi("w_now", [P, 2, DH, H // DH, HD])
            masked = sbi("masked", [P, NB, NH, UH, HT])
            z, sq, res = sbi("z2", [T, H, HD]), sbi("sq2", [T, H, HD]), sbi("res", [T, D])
            spare_h, var, std, rstd = sbi("spare_h", [T, H]), sbi("var2", [T, H]), sbi("std2", [T, H]), sbi("rstd2", [T, H])
            head_var_eps = sbi("head_var_eps", [T, H])
            stats, mean_var, var_eps, rstd_post = sbi("stats", [T, 6]), sbi("mean_var", [T, 2]), sbi("var_eps", [T, 1]), sbi("rstd_post", [T, 1])
            spare = sbi("spare", [T, 1])
            resT = sbi("resT", [P, DH, T])
            scores, z_ps = psi("scores", [P, NB, NH, UH, HT]), psi("z_ps", [T, 2, 512])
            turned_ps, out_norm_ps = psi("turned_ps", [P, 2, D]), psi("out_norm_ps", [P, 2, D])
            q_tok_ps, resT_ps = turned_ps[:, 0, :], turned_ps[:, 1, :].rearrange("p (c t) -> p c t", c=DH)
            out_ps, normT = out_norm_ps[:, 0, :], out_norm_ps[:, 1, :]
            now_ready, bd_ready, scores_ready, masked_ready, applied = sem("now_ready"), sem("bd_ready"), sem("scores_ready"), sem("masked_ready"), sem("applied")
            z_kept, squared, var_ready, std_ready, q_read = sem("z_kept"), sem("squared2"), sem("var_ready2"), sem("std_ready2"), sem("q_read")
            post_var_ready, post_rstd_ready, post_ready = sem("post_var_ready"), sem("post_rstd_ready"), sem("post_ready")
            resT_ready, resT_copied, out_ready, chain = sem("resT_ready"), sem("resT_copied"), sem("out_ready"), sem("out_chain")
            q_ready = sem("q_tok_ready")
            norm = Norm(nc, inner, "ttt_n", keep, normT)
            block = inner.enter_context(nc.Block())
            def unit(step, b, par, u, lag):
                of = b if u >= lag else b - 1
                if live(of):
                    step(of, par if u >= lag else 1 - par, (u - lag) % U)

            def with_rest(eng, step, after=4, **loop):
                each_sequence(eng, step, peeled=PEELED, **loop)
                for b in range(B, B + after):
                    step(b, b % 2, b // 2)

            @block.gpsimd
            def _(pool):
                def square(b):
                    need(pool, z_kept, b + 1)
                    nc.gpsimd.tensor_tensor(sq[:], z[:], z[:], ALU.mult).then_inc(squared, 1)

                def rstd_after(b):
                    need(pool, post_var_ready, b + 1)
                    nc.gpsimd.tensor_tensor(rstd_post[:], var_eps[:], keep["neg_half"][:], ALU.pow).then_inc(post_rstd_ready, 1)

                def prepare(b, par):
                    need(pool, scores_ready, U * (b - 1))
                    nc.gpsimd.tensor_tensor(w_now[:, par], w_feat[:, bass.ts(b, DH), :].unsqueeze(2).to_broadcast([P, DH, H // DH, HD]),
                                            head16[:].unsqueeze(1).unsqueeze(3).to_broadcast([P, DH, H // DH, HD]), ALU.mult)
                    k_halves = k_feat[:].rearrange("p c (n t) -> p c n t", t=HT)
                    for c in range(DH):
                        for half in range(NH):
                            ins = nc.gpsimd.tensor_tensor(k_now[:, par, 2 * c:2 * c + 2, half], k_halves[:, c, 2 * b + half, :].unsqueeze(1).unsqueeze(1).to_broadcast([P, 2, 2, HT]),
                                                          keep["group_mask"][:].rearrange("p (m a) -> p m a", a=2).unsqueeze(3).to_broadcast([P, 2, 2, HT]), ALU.mult)
                    ins.then_inc(now_ready, 1)

                def step(b, par, pair):
                    if live(b):
                        prepare(b, par)
                    if live(b - 3):
                        rstd_after(b - 3)
                    if live(b - 4):
                        norm.gpsimd(pool, b - 4)
                    if live(b - 2):
                        square(b - 2)
                with_rest(pool, step, after=5)

            @block.scalar
            def _(act):

                def spread_queries(b, par):
                    need(act, scores_ready, U * (b - 1))
                    need(act, q_ready, b - 1)
                    for j in range(UH):
                        nc.scalar.mul(q_bd[:, par, :, j, :], q_feat[:, :, bass.ts(b, T)], keep["head_mask"][:, j:j + 1])
                    nc.scalar.copy(q_now[:, par], q_feat[:, :, bass.ts(b, T)])

                def take_gradients(b, par):
                    need(act, applied, U * (b - 1))
                    nc.scalar.copy(g_now[:, par], g_pairs[:, :, b]).then_inc(bd_ready, 1)

                def keep_z(b, par):
                    need(act, applied, U * (b + 1))
                    need(act, q_read, b)
                    nc.scalar.copy(z[:].rearrange("p h d -> p (h d)"), z_ps[:, par, 0:D]).then_inc(z_kept, 1)

                def deviation(b):
                    need(act, var_ready, b + 1)
                    nc.scalar.activation(std[:], var[:], ACT.Sqrt, bias=eps[:], scale=1.0 / HD).then_inc(std_ready, 1)

                def copy_res(b):
                    need(act, resT_ready, b + 1)
                    need(act, out_ready, b)
                    for c in range(DH):
                        ins = nc.scalar.activation(resT[:, c, :], resT_ps[:, c, :], ACT.Identity, bias=post_b[:, c:c + 1], scale=post_w[:, c:c + 1])
                    ins.then_inc(resT_copied, 1)

                def step(b, par, pair):
                    if live(b):
                        spread_queries(b, par)
                    if live(b - 2):
                        keep_z(b - 2, par)
                    if live(b):
                        take_gradients(b, par)
                    if live(b - 4):
                        norm.scalar(act, b - 4)
                    if live(b - 3):
                        copy_res(b - 3)
                    if live(b - 2):
                        deviation(b - 2)
                with_rest(act, step, after=5)
                norm.done(act)

            @block.tensor
            def _(pe):
                def score(b, par, u):
                    if u == 0:
                        need(pe, now_ready, b + 1)
                        need(pe, bd_ready, b + 1)
                    need(pe, masked_ready, U * b + u + 1 - NB)
                    for half in range(NH):
                        ins = nc.tensor.matmul(scores[:, u % NB, half], k_now[:, par, u, half], q_bd[:, par, u // 2, :, half * HT:(half + 1) * HT], start=True, stop=True)
                    ins.then_inc(scores_ready, 1)

                def begin(b, par):
                    need(pe, z_kept, b - 1)
                    nc.tensor.matmul(z_ps[:, par, 0:D], half_of[:], biases[:, bass.ts(b, D)], start=True, stop=False, skip_group_check=True)
                    for half in range(NH):
                        rows = slice(half * HT, (half + 1) * HT)
                        for c in range(DH):
                            model = w_now[:, par, c] if half else w0[:, c, :].rearrange("p (h d) -> p h d", d=HD)
                            nc.tensor.matmul(z_ps[rows, par, c * P:(c + 1) * P], q_now[:, par, c, rows], model, start=False, stop=False, skip_group_check=True)

                def turn_queries(b, par):
                    need(pe, q_read, b)
                    nc.tensor.matmul(q_tok_ps, half_of[:], beta_rows[:], start=True, stop=False, skip_group_check=True)
                    for c in range(DH):
                        ins = nc.tensor.matmul(q_tok_ps[:, c * P:(c + 1) * P], q_now[:, par, c, :], keep["ident"][:], start=False, stop=(c == DH - 1), skip_group_check=True)
                    ins.then_inc(q_ready, 1)

                def apply(b, par, u):
                    need(pe, masked_ready, U * b + u + 1)
                    for half in range(NH):
                        rows = slice(half * HT, (half + 1) * HT)
                        by_pair = z_ps[rows, par, u * 2 * UH * HD:(u + 1) * 2 * UH * HD].rearrange("p (a j d) -> p a j d", a=2, j=UH)
                        for j in range(UH):
                            ins = nc.tensor.matmul(by_pair[:, :, j, :], masked[:, u % NB, half, j, :], g_now[:, par, half, u * UH + j, :], start=False,
                                                   stop=(u == U - 1 and j == UH - 1), skip_group_check=True)
                    ins.then_inc(applied, 1)

                def turn_res(b):
                    need(pe, post_ready, b + 1)
                    need(pe, resT_copied, b)
                    for c in range(DH):
                        ins = nc.tensor.transpose(resT_ps[:, c, :], res[:, c * P:(c + 1) * P], keep["ident"][:])
                    ins.then_inc(resT_ready, 1)

                def out(b):
                    need(pe, resT_copied, b + 1)
                    need(pe, norm.var_ready, b)
                    for c in range(DH):
                        ins = nc.tensor.matmul(out_ps[:], resT[:, c, :], w_out[:, c, :], start=(c == 0), stop=(c == DH - 1))
                    ins.then_inc(out_ready, 1)

                def step(b, par, pair):
                    for u in range(U):
                        if live(b):
                            score(b, par, u)
                        if u == 0 and live(b):
                            begin(b, par)
                        if u == 1 and live(b - 1):
                            turn_queries(b - 1, 1 - par)
                        unit(apply, b, par, u, APPLY_LAG)
                        if u == 2 and live(b - 3):
                            norm.tensor(pe, b - 3)
                        if u == 2 and live(b - 2):
                            turn_res(b - 2)
                        if u == 3 and live(b - 2):
                            out(b - 2)
                with_rest(pe, step)

            @block.vector
            def _(dve):
                order = Order(dve, chain)
                tt, ts, tr, stt = nc.vector.tensor_tensor, nc.vector.tensor_scalar, nc.vector.tensor_reduce, nc.vector.scalar_tensor_tensor
                order(ts(neg_last[:], tok[:, C - 1:C], -1.0, None, ALU.mult))
                order(tt(mask[:].rearrange("p (n i) -> p n i", i=C), inside[:].rearrange("p (n i) -> p n i", i=C), tok[:].unsqueeze(1).to_broadcast([P, HT // C, C]), ALU.mult))
                order(stt(mask[:], before[:], neg_last[:], mask[:], ALU.mult, ALU.subtract))

                def masks(b, u):
                    need(dve, scores_ready, U * b + u + 1)
                    need(dve, applied, U * b + u + 1 - NB)
                    stt(masked[:, u % NB].rearrange("p n j i -> p (n j) i"), scores[:, u % NB].rearrange("p n j i -> p (n j) i"), 1.0,
                        mask[:].unsqueeze(1).to_broadcast([P, NH * UH, HT]), ALU.add, ALU.mult).then_inc(masked_ready, 1)

                wide = lambda t: t[:].unsqueeze(2).to_broadcast([T, H, HD])

                def variance(b):
                    need(dve, squared, b + 1)
                    tr(var[:], sq[:], AX_X, ALU.add).then_inc(var_ready, 1)
                    need(dve, var_ready, b + 1)
                    order(ts(head_var_eps[:], var[:], 1.0 / HD, EPS, ALU.mult, ALU.add))

                def head_norm(b):
                    need(dve, std_ready, b + 1)
                    order(refined_rstd(nc, order, rstd[:], std[:], head_var_eps[:], spare_h[:]))
                    order(tt(z[:], z[:], wide(rstd), ALU.mult))

                def residual(b):
                    z2 = z[:].rearrange("p h d -> p (h d)")
                    order(tt(z2, z2, gamma_row[:], ALU.mult))
                    need(dve, resT_ready, b)
                    need(dve, q_ready, b + 1)
                    tt(res[:], z2, q_tok_ps, ALU.add).then_inc(q_read, 1)

                def post_stats(b):
                    need(dve, q_read, b + 1)
                    order(nc.vector.bn_stats(stats[:], res[:]))
                    nc.vector.memset(spare[:], 0.0)
                    order(nc.vector.bn_aggr(mean_var[:], stats[:]))
                    ts(var_eps[:], mean_var[:, 1:2], EPS, None, ALU.add).then_inc(post_var_ready, 1)

                def post_norm(b):
                    need(dve, post_rstd_ready, b + 1)
                    ts(res[:], res[:], mean_var[:, 0:1], rstd_post[:], ALU.subtract, ALU.mult).then_inc(post_ready, 1)

                def block_norm(b):
                    need(dve, out_ready, b + 1)
                    norm.vector_begin(dve, order, b, out_ps)

                def step(b, par, pair):
                    for u in range(U):
                        if live(b):
                            masks(b, u)
                        if u == 0 and live(b - 2):
                            post_stats(b - 2)
                        if u == 0 and live(b - 3):
                            block_norm(b - 3)
                        if u == 1 and live(b - 3):
                            norm.vector_end(dve, b - 3)
                        if u == 1 and live(b - 2):
                            post_norm(b - 2)
                        if live(b - 1):
                            if u == 2:
                                variance(b - 1)
                            if u == 3:
                                head_norm(b - 1)
                                residual(b - 1)
                with_rest(dve, step, order=order, per=2 * (9 + norm.CHAIN - 1))


def open_persistent(nc, ctx):
    keep = {"semaphores": []}
    sb = lambda name, shape: ctx.enter_context(nc.sbuf_tensor(name, shape, F32))
    keep["x_tok"] = sb("x_tok", [T, B, D])
    keep["xT"] = sb("xT", [P, DH, B * T])
    keep["ident"] = sb("ident", [P, P])
    keep["neg_half"] = sb("neg_half", [P, 1])
    keep["head_mask"] = sb("head_mask", [P, 4])
    keep["group_mask"] = sb("group_mask", [P, 4])
    return keep


def decoder(nc, io, out):
    with ExitStack() as ctx:
        keep = open_persistent(nc, ctx)
        test_time_training(nc, keep, io)
        give_back_semaphores(nc, keep)
        with ExitStack() as later:
            batch_axis = BatchAxisInputs(nc, later, io)
            with ExitStack() as both:
                ffn = FfnInputs(nc, both, io)
                cross_attention_gqa(nc, keep, io, ffn.loads)
                give_back_semaphores(nc, keep)
                gated_ffn_int8(nc, keep, io, ffn, batch_axis.loads)
                give_back_semaphores(nc, keep)
            with ExitStack() as both:
                latent = LatentWeights(nc, both)
                batch_axis_attention(nc, keep, io, batch_axis, latent)
                give_back_semaphores(nc, keep)
                latent_cross_attention(nc, keep, io, latent)
                give_back_semaphores(nc, keep)
        mixture_of_experts(nc, keep, io, out)


def lay_out(x, ctx, inputs):
    a0 = lambda name: np.asarray(inputs[f"L0_attn_{name}"])
    f0 = lambda name: np.asarray(inputs[f"L0_ffn_{name}"])
    a1 = lambda name: np.asarray(inputs[f"L1_attn_{name}"])
    m1 = lambda name: np.asarray(inputs[f"L1_xattn_{name}"])
    e1 = lambda name: np.asarray(inputs[f"L1_ffn_{name}"])
    feat = lambda v: v.reshape(-1, P).T
    io = {"x": x, "x_feat": x.reshape(B * T, D).T, "ctx": ctx}

    part = np.arange(P)
    io["identity"] = np.eye(P, dtype=np.float32)
    io["group_mask"] = (part[:, None] // 32 == np.arange(4)[None, :]).astype(np.float32)
    io["head_mask"] = (part[:, None] // 8 % 4 == np.arange(4)[None, :]).astype(np.float32)

    heads, hd, chunk = 32, 8, 16
    io["ttt_w_qkv"] = np.concatenate([a0("q_w").T, a0("k_w").T, a0("v_w").T], axis=1)
    io["ttt_w_lr"] = a0("ttt_lr_weight").reshape(heads, D).T
    io["ttt_lr_bias"] = a0("ttt_lr_bias")
    io["ttt_gamma_feat"], io["ttt_beta_feat"] = feat(a0("ttt_norm_weight")), feat(a0("ttt_norm_bias"))
    io["ttt_gamma"], io["ttt_beta"] = a0("ttt_norm_weight"), a0("ttt_norm_bias")
    w_first = a0("W1")
    io["ttt_w0_seq"] = np.concatenate([w_first.transpose(0, 2, 1), a0("b1").transpose(0, 2, 1)], axis=2).reshape(heads, hd * (hd + 1))
    w_bd = np.zeros((P, DH, P), w_first.dtype)
    for h in range(heads):
        r = h % (heads // DH) * hd
        w_bd[r:r + hd, h // (heads // DH), r:r + hd] = w_first[h]
    io["ttt_w0_bd"], io["ttt_b0"] = w_bd, a0("b1").reshape(D)
    io["ttt_token_idx"] = a0("learnable_token_idx")
    io["ttt_inverse"] = np.float32(1) / np.arange(1, chunk + 1, dtype=np.float32)
    io["ttt_w_out"] = a0("o_w").T
    io["ttt_post_w"], io["ttt_post_b"] = feat(a0("post_norm_weight")), feat(a0("post_norm_bias"))
    same, earlier = part[:, None] // chunk == part[None, :] // chunk, part[:, None] // chunk < part[None, :] // chunk
    tiled = lambda a: np.tile(a[:T // 2, :T // 2], (2, 1)).astype(np.float32)
    io["ttt_inside"] = tiled(same & (part[:, None] <= part[None, :]))
    io["ttt_before"] = tiled(earlier)
    io["ttt_head16"] = (part[:, None] // hd == np.arange(heads // DH)[None, :]).astype(np.float32)
    io["ttt_half_of"] = (np.arange(2)[:, None] == part[None, :] // (T // 2)).astype(np.float32)

    by_head = ctx.transpose(0, 2, 1).reshape(B, DH, 4, 1, 8, T)
    io["ctx_rep"] = np.broadcast_to(by_head, (B, DH, 4, 4, 8, T)).reshape(B, DH, P, T)

    words = lambda a: np.ascontiguousarray(a).view(np.int32)
    io["ffn_w_gate"], io["ffn_w_up"], io["ffn_w_down"] = words(f0("w_gate")), words(f0("w_up")), words(f0("w_down"))
    io["ffn_s_gate"], io["ffn_s_up"], io["ffn_s_down"] = feat(f0("s_gate")), feat(f0("s_up")), f0("s_down")

    io["ba_w_qkv"] = np.concatenate([a1("q_proj").T, a1("k_proj").T, a1("v_proj").T], axis=1)
    io["ba_b_qkv"] = np.concatenate([a1("q_bias"), a1("k_bias"), a1("v_bias")])
    io["ba_w_out"], io["ba_b_out"] = a1("out_proj").T, a1("out_bias")

    dc = ctx.shape[2]
    frequency = (np.float32(1) / np.float32(10000) ** (np.arange(0, dc, 2, dtype=np.float32) / np.float32(dc))).astype(np.float32)
    angle = np.arange(T, dtype=np.float32)[:, None] * frequency[None, :]
    sign = np.where(np.arange(dc) < dc // 2, np.float32(-1), np.float32(1))
    io["cosines"] = np.repeat(np.cos(angle), 2, axis=-1)
    io["sines"] = np.repeat(np.sin(angle), 2, axis=-1) * sign
    io["mla_wq"], io["mla_kc_kv"], io["mla_woT"] = m1("Wq"), m1("w_kc_kv"), m1("Wo").T
    io["mla_kc_qT"] = m1("w_kc_q").reshape(16, 128, 2, 96).transpose(3, 2, 0, 1)
    io["mla_qrT"], io["mla_krT"] = m1("W_qr").transpose(2, 0, 1), m1("W_kr").transpose(2, 0, 1)

    experts, groups, f = 64, 8, 96
    io["moe_w_route"], io["moe_bias"] = e1("gate_w"), e1("bias")
    io["moe_not_first"] = (np.arange(B * experts) % experts != 0).astype(np.float32)
    io["moe_lower"] = (np.arange(groups)[None, :] < np.arange(groups)[:, None]).astype(np.float32).reshape(-1)
    io["moe_countdown"] = (B * T - (np.arange(B)[None, :] * T + part[:, None])).astype(np.float32)
    io["moe_slot_no"] = part[:, None].astype(np.float32)
    io["moe_ws_gu"], io["moe_ws_down"] = np.concatenate([e1("ws_gate"), e1("ws_up")], axis=1), e1("ws_down")
    gate_up = np.concatenate([e1("w_gate").reshape(experts // 2, 2, DH, P, f), e1("w_up").reshape(experts // 2, 2, DH, P, f)], axis=-1)
    io["moe_w_gu"] = gate_up.transpose(0, 3, 1, 2, 4)
    io["moe_w_down"] = e1("w_down").reshape(experts // 2, 2, f, D).transpose(0, 2, 1, 3)
    return {name: np.ascontiguousarray(a) for name, a in io.items()}


def kernel(**inputs):
    import concourse.bacc as bacc
    from concourse.bass_utils import run_bass_kernel_spmd

    nc = bacc.Bacc("TRN2", target_bir_lowering=False, num_devices=1)
    arrays = lay_out(np.asarray(inputs["x"]), np.asarray(inputs["ctx_512"]), inputs)
    io = {name: nc.dram_tensor(f"in_{name}", a.shape, mybir.dt.from_np(a.dtype), kind="ExternalInput").ap() for name, a in arrays.items()}
    out = nc.dram_tensor("out", (B, T, D), F32, kind="ExternalOutput").ap()
    decoder(nc, io, out)
    result = run_bass_kernel_spmd(nc, [{f"in_{name}": a for name, a in arrays.items()}], core_ids=[0])
    return result.results[0]["out"]
```
